# Optimizing a Trainium2 kernel written in Bass

```python
import numpy as np
import jax
import jax.numpy as jnp

def _softmax(x, axis=-1):
    return jax.nn.softmax(x, axis=axis)

def _gelu(x):
    return jax.nn.gelu(x, approximate=True)

def _silu(x):
    return jax.nn.silu(x)

def _sigmoid(x):
    return jax.nn.sigmoid(x)

def _layernorm(x, axis=-1, eps=1e-05):
    m = jnp.mean(x, axis=axis, keepdims=True)
    v = jnp.var(x, axis=axis, keepdims=True)
    return (x - m) / jnp.sqrt(v + eps)

def _scatter_add(tgt, idx, src, axis=0):
    return tgt.at[idx].add(src)

def _segment_sum(src, seg, n):
    return jax.ops.segment_sum(src, seg, n)
kernel_name = 'mk_xattn_ffn_d2_seqx_r4_0efcf5'

def setup_inputs(seed: int=0):
    np.random.seed(seed)
    _w = jnp.asarray

    def _rec_inputs():
        import jax
        import jax.numpy as jnp
        _rk = jax.random.key(seed)
        x = -0.0003929 + 0.9999 * jax.random.normal(jax.random.fold_in(_rk, 1), (4, 1024, 256), jnp.float32)
        _lenS = 1024 - jax.random.randint(jax.random.fold_in(_rk, 7), (4,), 0, max(1, 1024 // 4) + 1, jnp.int32)
        _lenS2 = 77 - jax.random.randint(jax.random.fold_in(_rk, 8), (4,), 0, max(1, 77 // 4) + 1, jnp.int32)
        _ctx_512P = jax.random.normal(jax.random.fold_in(_rk, 11), (4, 16, 128), jnp.float32)
        _ctx_512c = jax.random.dirichlet(jax.random.fold_in(_rk, 511), 0.3 * jnp.ones((16,), jnp.float32), (4, 77))
        _ctx_512t = jnp.einsum('bsk,bkd->bsd', _ctx_512c, _ctx_512P)
        _ctx_512t = _ctx_512t * jax.lax.rsqrt(jnp.mean(jnp.square(_ctx_512t)) + 1e-12) * 0.953939
        ctx_512 = -1.39393e-06 + 0.999914 * (_ctx_512t + 0.3 * jax.random.normal(jax.random.fold_in(_rk, 611), (4, 77, 128), jnp.float32))
        return (x, ctx_512)
    x, ctx_512 = _rec_inputs()

    def _L0_xattn_setup():
        import jax, jax.numpy as jnp
        import numpy as np
        HEADS = 16
        D_MODEL = 256
        IMG_MODEL = 128
        D_K = D_MODEL // HEADS
        key = jax.random.key(seed)
        ks = jax.random.split(key, 12)
        B, LQ, LKV = (8, 512, 256)
        s_dm = 1.0 / np.sqrt(D_MODEL)
        s_im = 1.0 / np.sqrt(IMG_MODEL)
        return {'q': jax.random.normal(ks[0], (B, LQ, D_MODEL), jnp.float32), 'k': jax.random.normal(ks[1], (B, LKV, IMG_MODEL), jnp.float32), 'v': jax.random.normal(ks[2], (B, LKV, IMG_MODEL), jnp.float32), 'Wq': jax.random.normal(ks[3], (D_MODEL, D_MODEL), jnp.float32) * s_dm, 'bq': jnp.zeros((D_MODEL,), jnp.float32), 'Wk': jax.random.normal(ks[4], (IMG_MODEL, D_MODEL), jnp.float32) * s_im, 'bk': jnp.zeros((D_MODEL,), jnp.float32), 'Wv': jax.random.normal(ks[5], (IMG_MODEL, D_MODEL), jnp.float32) * s_im, 'bv': jnp.zeros((D_MODEL,), jnp.float32), 'Wo': jax.random.normal(ks[6], (D_MODEL, D_MODEL), jnp.float32) * s_dm, 'bo': jnp.zeros((D_MODEL,), jnp.float32)}
    _L0_xattn_all = _L0_xattn_setup()
    _L0_xattn_in = {k: v for k, v in _L0_xattn_all.items() if k in ('Wq', 'bq', 'Wk', 'bk', 'Wv', 'bv', 'Wo', 'bo')}
    del _L0_xattn_all

    def _L0_ffn_setup():
        import jax, jax.numpy as jnp
        import numpy as np
        NUM_EXPERTS = 8
        CAPACITY = 1024
        key = jax.random.key(seed)
        ks = jax.random.split(key, 5)
        dim, hidden = (256, 512)
        x = jax.random.normal(ks[0], (4, 1024, dim), dtype=jnp.float32)
        wg = jax.random.normal(ks[1], (dim, NUM_EXPERTS), dtype=jnp.float32) * 0.02
        w1 = jax.random.normal(ks[2], (NUM_EXPERTS, dim, hidden), dtype=jnp.float32) * 0.02
        w3 = jax.random.normal(ks[3], (NUM_EXPERTS, dim, hidden), dtype=jnp.float32) * 0.02
        w2 = jax.random.normal(ks[4], (NUM_EXPERTS, hidden, dim), dtype=jnp.float32) * 0.02
        return {'x': x, 'wg': wg, 'w1': w1, 'w3': w3, 'w2': w2}
    _L0_ffn_all = _L0_ffn_setup()
    _L0_ffn_in = {k: v for k, v in _L0_ffn_all.items() if k in ('wg', 'w1', 'w3', 'w2')}
    del _L0_ffn_all

    def _L1_xattn_setup():
        import jax, jax.numpy as jnp
        import numpy as np
        DIM = 256
        LATENT_DIM = 128
        NUM_HEADS = 16
        HEAD_DIM = DIM // NUM_HEADS
        SCALE = HEAD_DIM ** (-0.5)
        key = jax.random.key(seed)
        k1, k2, k3, k4, k5 = jax.random.split(key, 5)
        B, xN, zN = (2, 512, 512)
        x = jax.random.normal(k1, (B, xN, DIM), dtype=jnp.float32)
        z = jax.random.normal(k2, (B, zN, LATENT_DIM), dtype=jnp.float32)
        Wq = jax.random.normal(k3, (DIM, DIM), dtype=jnp.float32) * DIM ** (-0.5)
        Wkv = jax.random.normal(k4, (2 * DIM, LATENT_DIM), dtype=jnp.float32) * LATENT_DIM ** (-0.5)
        Wo = jax.random.normal(k5, (DIM, DIM), dtype=jnp.float32) * DIM ** (-0.5)
        return {'x': x, 'z': z, 'Wq': Wq, 'Wkv': Wkv, 'Wo': Wo}
    _L1_xattn_all = _L1_xattn_setup()
    _L1_xattn_in = {k: v for k, v in _L1_xattn_all.items() if k in ('Wq', 'Wkv', 'Wo')}
    del _L1_xattn_all

    def _L1_ffn_setup():
        import jax, jax.numpy as jnp
        import numpy as np
        B, L, D = (2, 512, 256)
        E = 15
        H = D * 1
        K = 3
        T = 1.0
        key = jax.random.key(seed)
        ks = jax.random.split(key, 12)
        s = 0.02
        return {'x': jax.random.normal(ks[0], (B, L, D), dtype=jnp.float32), 'router_W': jax.random.normal(ks[1], (D, E), dtype=jnp.float32) * s, 'router_b': jnp.zeros((E,), dtype=jnp.float32), 'sW1': jax.random.normal(ks[2], (D, H), dtype=jnp.float32) * s, 'sb1': jnp.zeros((H,), dtype=jnp.float32), 'sW2': jax.random.normal(ks[3], (H, D), dtype=jnp.float32) * s, 'sb2': jnp.zeros((D,), dtype=jnp.float32), 'eW1': jax.random.normal(ks[4], (E, D, H), dtype=jnp.float32) * s, 'eb1': jnp.zeros((E, H), dtype=jnp.float32), 'eW2': jax.random.normal(ks[5], (E, H, D), dtype=jnp.float32) * s, 'eb2': jnp.zeros((E, D), dtype=jnp.float32)}
    _L1_ffn_all = _L1_ffn_setup()
    _L1_ffn_in = {k: v for k, v in _L1_ffn_all.items() if k in ('router_W', 'router_b', 'sW1', 'sb1', 'sW2', 'sb2', 'eW1', 'eb1', 'eW2', 'eb2')}
    del _L1_ffn_all
    return {'x': x, 'ctx_512': ctx_512, 'L0_xattn_Wq': _L0_xattn_in['Wq'], 'L0_xattn_bq': _L0_xattn_in['bq'], 'L0_xattn_Wk': _L0_xattn_in['Wk'], 'L0_xattn_bk': _L0_xattn_in['bk'], 'L0_xattn_Wv': _L0_xattn_in['Wv'], 'L0_xattn_bv': _L0_xattn_in['bv'], 'L0_xattn_Wo': _L0_xattn_in['Wo'], 'L0_xattn_bo': _L0_xattn_in['bo'], 'L0_ffn_wg': _L0_ffn_in['wg'], 'L0_ffn_w1': _L0_ffn_in['w1'], 'L0_ffn_w3': _L0_ffn_in['w3'], 'L0_ffn_w2': _L0_ffn_in['w2'], 'L1_xattn_Wq': _L1_xattn_in['Wq'], 'L1_xattn_Wkv': _L1_xattn_in['Wkv'], 'L1_xattn_Wo': _L1_xattn_in['Wo'], 'L1_ffn_router_W': _L1_ffn_in['router_W'], 'L1_ffn_router_b': _L1_ffn_in['router_b'], 'L1_ffn_sW1': _L1_ffn_in['sW1'], 'L1_ffn_sb1': _L1_ffn_in['sb1'], 'L1_ffn_sW2': _L1_ffn_in['sW2'], 'L1_ffn_sb2': _L1_ffn_in['sb2'], 'L1_ffn_eW1': _L1_ffn_in['eW1'], 'L1_ffn_eb1': _L1_ffn_in['eb1'], 'L1_ffn_eW2': _L1_ffn_in['eW2'], 'L1_ffn_eb2': _L1_ffn_in['eb2']}

def reference(x, ctx_512, L0_xattn_Wq, L0_xattn_bq, L0_xattn_Wk, L0_xattn_bk, L0_xattn_Wv, L0_xattn_bv, L0_xattn_Wo, L0_xattn_bo, L0_ffn_wg, L0_ffn_w1, L0_ffn_w3, L0_ffn_w2, L1_xattn_Wq, L1_xattn_Wkv, L1_xattn_Wo, L1_ffn_router_W, L1_ffn_router_b, L1_ffn_sW1, L1_ffn_sb1, L1_ffn_sW2, L1_ffn_sb2, L1_ffn_eW1, L1_ffn_eb1, L1_ffn_eW2, L1_ffn_eb2):
    import jax
    import jax.numpy as jnp

    def _L0_xattn_ref(q, k, v, Wq, bq, Wk, bk, Wv, bv, Wo, bo):
        import jax, jax.numpy as jnp
        import numpy as np
        HEADS = 16
        D_MODEL = 256
        IMG_MODEL = 128
        D_K = D_MODEL // HEADS
        B, LQ, _ = q.shape
        LKV = k.shape[1]
        qh = (q @ Wq + bq).reshape(B, LQ, HEADS, D_K).transpose(0, 2, 1, 3)
        kh = (k @ Wk + bk).reshape(B, LKV, HEADS, D_K).transpose(0, 2, 1, 3)
        vh = (v @ Wv + bv).reshape(B, LKV, HEADS, D_K).transpose(0, 2, 1, 3)
        scale = 1.0 / np.sqrt(D_K)
        scores = jnp.einsum('bhqd,bhkd->bhqk', qh, kh) * scale
        attn = jax.nn.softmax(scores, axis=-1)
        out = jnp.einsum('bhqk,bhkd->bhqd', attn, vh)
        concat = out.transpose(0, 2, 1, 3).reshape(B, LQ, D_MODEL)
        return concat @ Wo + bo

    def _L0_ffn_ref(x, wg, w1, w3, w2):
        import jax, jax.numpy as jnp
        import numpy as np
        NUM_EXPERTS = 8
        CAPACITY = 1024
        bz, slen, dim = x.shape
        xt = x.reshape(bz * slen, dim)
        scores = jax.nn.softmax(xt @ wg, axis=-1)
        top_scores, sel = jax.lax.top_k(scores.T, CAPACITY)
        token_idx = sel.reshape(-1)
        routed = xt[token_idx] * top_scores.reshape(-1, 1)
        routed = routed.reshape(NUM_EXPERTS, CAPACITY, dim)
        h = jax.nn.silu(jnp.einsum('ecd,edh->ech', routed, w1)) * jnp.einsum('ecd,edh->ech', routed, w3)
        routed_out = jnp.einsum('ech,ehd->ecd', h, w2).reshape(-1, dim)
        out = jnp.zeros_like(xt).at[token_idx].add(routed_out)
        return out.reshape(bz, slen, dim)

    def _L1_xattn_ref(x, z, Wq, Wkv, Wo):
        import jax, jax.numpy as jnp
        import numpy as np
        DIM = 256
        LATENT_DIM = 128
        NUM_HEADS = 16
        HEAD_DIM = DIM // NUM_HEADS
        SCALE = HEAD_DIM ** (-0.5)
        B, xN, _ = x.shape
        _, zN, _ = z.shape
        Q = (x @ Wq.T).reshape(B, xN, NUM_HEADS, HEAD_DIM)
        KV = (z @ Wkv.T).reshape(B, zN, 2, NUM_HEADS, HEAD_DIM)
        K = KV[:, :, 0]
        V = KV[:, :, 1]
        attn = jnp.einsum('bqhd,bkhd->bhqk', Q, K) * SCALE
        attn = jax.nn.softmax(attn, axis=-1)
        O = jnp.einsum('bhqk,bkhd->bqhd', attn, V).reshape(B, xN, DIM)
        return O @ Wo.T

    def _L1_ffn_ref(x, router_W, router_b, sW1, sb1, sW2, sb2, eW1, eb1, eW2, eb2):
        import jax, jax.numpy as jnp
        import numpy as np
        B, L, D = (2, 512, 256)
        E = 15
        H = D * 1
        K = 3
        T = 1.0
        b, l, d = x.shape
        n = b * l
        xt = x.reshape(n, d)
        shared = jax.nn.relu(xt @ sW1 + sb1) @ sW2 + sb2
        logits = xt @ router_W + router_b
        probs = jax.nn.softmax(logits / T, axis=-1)
        top_p, top_i = jax.lax.top_k(probs, K)
        cw = jnp.zeros((n, E), dtype=probs.dtype)
        cw = cw.at[jnp.arange(n)[:, None], top_i].set(top_p)
        h = jax.nn.relu(jnp.einsum('nd,edh->neh', xt, eW1) + eb1)
        ye = jnp.einsum('neh,ehd->ned', h, eW2) + eb2
        routed = jnp.einsum('ned,ne->nd', ye, cw)
        return (shared + routed).reshape(b, l, d)
    x = x + _L0_xattn_ref(_layernorm(x, axis=-1), ctx_512, ctx_512, L0_xattn_Wq, L0_xattn_bq, L0_xattn_Wk, L0_xattn_bk, L0_xattn_Wv, L0_xattn_bv, L0_xattn_Wo, L0_xattn_bo)
    x = x + _L0_ffn_ref(_layernorm(x, axis=-1), L0_ffn_wg, L0_ffn_w1, L0_ffn_w3, L0_ffn_w2)
    x = x + _L1_xattn_ref(_layernorm(x, axis=-1), ctx_512, L1_xattn_Wq, L1_xattn_Wkv, L1_xattn_Wo)
    x = x + _L1_ffn_ref(_layernorm(x, axis=-1), L1_ffn_router_W, L1_ffn_router_b, L1_ffn_sW1, L1_ffn_sb1, L1_ffn_sW2, L1_ffn_sb2, L1_ffn_eW1, L1_ffn_eb1, L1_ffn_eW2, L1_ffn_eb2)
    return x

_drawn_inputs = setup_inputs


def setup_inputs(seed=0):
    import zlib

    import numpy as np

    out = dict(_drawn_inputs(seed))
    spreads = {'L0_xattn_bq': (0.0, 0.396),
     'L0_xattn_bk': (0.0, 2.0),
     'L0_xattn_bv': (0.0, 0.1),
     'L0_xattn_bo': (0.0, 0.1),
     'L1_ffn_router_b': (0.0, 0.8),
     'L1_ffn_sb1': (0.0, 2.0),
     'L1_ffn_sb2': (0.0, 0.693),
     'L1_ffn_eb1': (0.0, 0.8),
     'L1_ffn_eb2': (0.0, 1.662)}
    factors = {'L0_ffn_wg': 8.0,
     'L0_ffn_w1': 8.0,
     'L0_ffn_w3': 8.0,
     'L0_ffn_w2': 8.0,
     'L1_ffn_router_W': 3.673,
     'L1_ffn_eW1': 6.917,
     'L1_ffn_eW2': 5.518,
     'L1_ffn_sW1': 7.575,
     'L1_ffn_sW2': 3.764}
    for name, (base, spread) in spreads.items():
        noise = np.random.default_rng([zlib.crc32(name.encode()), seed]).standard_normal(out[name].shape)
        drawn = base * np.exp(spread * noise) if base else spread * noise
        out[name] = jnp.asarray(drawn.astype(out[name].dtype))
    for name, factor in factors.items():
        out[name] = (out[name] * factor).astype(out[name].dtype)
    return out
```

```python
from contextlib import ExitStack

import concourse.bass as bass
from concourse import mybir

ALU = mybir.AluOpType
ACT = mybir.ActivationFunctionType
F32 = mybir.dt.float32
F32R = mybir.dt.float32r
I32 = mybir.dt.int32
BF16 = mybir.dt.bfloat16
AX_X = mybir.AxisListType.X

P = 128
BATCH, SEQ, D = 4, 1024, 256
TOK = BATCH * SEQ
NT = TOK // P
GT = 4
GN = GT * P
NG = TOK // GN
DC = D // P
KV, CTX = 77, 128
H, DH = 16, 16
HC = H // DC
EPS = 1e-5
E0, CAP, HID0 = 8, 1024, 512
E1, TOP, HID1 = 15, 3, 256
BANK = 512


class Sem:

    def __init__(self, handle):
        self.handle, self.value = handle, 0

    def mark(self, by):
        self.value += by
        return (self, self.value)


class Lane:

    def __init__(self):
        self.steps, self.seen = [], {}

    def wait(self, *marks):
        for m in marks:
            if m is not None and self.seen.get(m[0], 0) < m[1]:
                self.seen[m[0]] = m[1]
                self.steps.append(lambda eng, m=m: eng.wait_ge(m[0].handle, m[1]))

    def do(self, call, sem=None, by=1):
        if sem is None:
            self.steps.append(call)
            return None
        self.steps.append(lambda eng: call(eng).then_inc(sem.handle, by))
        return sem.mark(by)

    def play(self, eng):
        for s in self.steps:
            s(eng)


class Banks:

    def __init__(self, tensors):
        self.tensors, self.free, self.n = tensors, [None] * len(tensors), 0

    def take(self):
        i = self.n % len(self.tensors)
        self.n += 1
        return i, self.tensors[i], self.free[i]

    def release(self, i, mark):
        self.free[i] = mark


def interleave(*streams):
    live = [[g, n] for g, n in streams]
    while live:
        for item in list(live):
            for _ in range(item[1]):
                try:
                    next(item[0])
                except StopIteration:
                    live.remove(item)
                    break


def f(ap):
    return ap.bitcast(F32)


def build(nc, A, out):
    pe, act, dve, pool, sp = (Lane() for _ in range(5))
    ctx = ExitStack()
    names = {}

    def sem(name):
        if name not in names:
            names[name] = Sem(ctx.enter_context(nc.semaphore("s_" + name)))
        return names[name]

    def sb(stack, name, shape, dt=F32):
        return stack.enter_context(nc.sbuf_tensor(name, shape, dt))

    with ctx:
        bank = [ctx.enter_context(nc.psum_tensor(f"bank{i}", [P, BANK], F32)) for i in range(8)]
        x_sb = sb(ctx, "x_sb", [P, NT, D])
        ident = sb(ctx, "ident", [P, P])
        neg_half = sb(ctx, "neg_half", [P, GT])
        phase_end = sem("phase_end")

        s_const = sem("const")
        zero = pool.do(lambda e: e.memset(ident[:, :], 0.0), s_const)
        pool.wait(zero)
        pool.do(lambda e: e.affine_select(out=ident[:, :], in_=ident[:, :], compare_op=ALU.not_equal, fill=1.0,
                                          base=0, pattern=[[-1, P]], channel_multiplier=1), s_const)
        const_done = pool.do(lambda e: e.memset(neg_half[:, :], -0.5), s_const)

        x_in = A["x"].rearrange("b (t p) d -> p (b t) d", p=P)
        x_ready = []
        for g in range(NG):
            x_ready.append([sp.do(lambda e, g=g: e.dma_start(x_sb[:, g * GT:(g + 1) * GT, :],
                                                             x_in[:, g * GT:(g + 1) * GT, :]), sem(f"x_io{g}"), 16)])

        def end_phase():
            for lane in (pe, act, dve, pool, sp):
                lane.do(lambda e: e.drain(), phase_end)
            for lane in (pe, act, dve, pool, sp):
                lane.wait((phase_end, phase_end.value))

        def split_weights(stack, name, source, shape, stage, arrived):
            hi, lo = sb(stack, name + "_hi", shape, F32R), sb(stack, name + "_lo", shape, F32R)
            pool.wait(arrived)
            m = pool.do(lambda e: e.tensor_copy(hi[:], stage), sem("weights"))
            pool.wait(m)
            m = pool.do(lambda e: e.tensor_tensor(lo[:], stage, f(hi[:]), ALU.subtract), sem("weights"))
            return hi, lo, m

        def matmul3(o, w_hi, w_lo, x_hi, x_lo, first, last, done=None):
            pe.do(lambda e: e.matmul(o, w_hi, x_hi, start=first, stop=False))
            pe.do(lambda e: e.matmul(o, w_lo, x_hi, start=False, stop=False))
            return pe.do(lambda e: e.matmul(o, w_hi, x_lo, start=False, stop=last), done)

        def layernorm(g, tmp, xn, ready, free):
            b = g % 2
            stats, mv, rstd = tmp
            dve.wait(*ready)
            for j in range(GT):
                m = dve.do(lambda e, j=j: e.bn_stats(stats[:, b, j, :], x_sb[:, g * GT + j, :]), sem("ln_stats"))
            dve.wait(m)
            for j in range(GT):
                m = dve.do(lambda e, j=j: e.bn_aggr(mv[:, b, j, :], stats[:, b, j, :]), sem("ln_stats"))
            dve.wait(m)
            m = dve.do(lambda e: e.tensor_scalar(rstd[:, b, 0, :], mv[:, b, :, 1], EPS, None, ALU.add), sem("ln_var"))
            pool.wait(m, const_done)
            m = pool.do(lambda e: e.tensor_tensor(rstd[:, b, 1, :], rstd[:, b, 0, :], neg_half[:, :], ALU.pow),
                        sem("ln_rstd"))
            dve.wait(m, *free)
            for j in range(GT):
                m = dve.do(lambda e, j=j: e.tensor_scalar(xn[:, j, :], x_sb[:, g * GT + j, :], mv[:, b, j, 0:1],
                                                          rstd[:, b, 1, j:j + 1], ALU.subtract, ALU.mult),
                           sem("ln_out"))
            return m

        def transpose_split(banks, src, src_ready, hi, lo, free, what):
            marks = []
            for c in range(DC):
                i, w, bank_free = banks.take()
                pe.wait(bank_free, src_ready, const_done)
                for j in range(GT):
                    m = pe.do(lambda e, w=w, c=c, j=j: e.transpose(w[:, j * P:(j + 1) * P],
                                                                   src[:, j, c * P:(c + 1) * P], ident[:, :]),
                              sem(what + "_T") if j == GT - 1 else None)
                act.wait(m, *free)
                m = act.do(lambda e, w=w, c=c: e.activation(hi[:, c, :], w[:, :], ACT.Copy), sem(what + "_hi"))
                dve.wait(m, *free)
                m = dve.do(lambda e, w=w, c=c: e.tensor_tensor(lo[:, c, :], w[:, :], f(hi[:, c, :]), ALU.subtract),
                           sem(what + "_lo"))
                banks.release(i, m)
                marks.append(m)
                yield
            return marks[-1]

        def attention(L, wq_d, wk_d, wv_d, wo_d, bq_d, bk_d, bv_d, bo_d, xr):
            st = ExitStack()
            with st:
                work = Banks([bank[i] for i in range(4)])
                smax = Banks([bank[i] for i in range(4, 6)])
                sexp = Banks([bank[i] for i in range(6, 8)])
                n = f"a{L}_"
                ln_tmp = (sb(st, n + "stats", [P, 2, GT, 6]), sb(st, n + "mv", [P, 2, GT, 2]),
                          sb(st, n + "rstd", [P, 2, 2, GT]))
                kaug = sb(st, n + "kaug", [P, H, BATCH, KV], F32R)
                kblk = sb(st, n + "kblk", [P, DC, BATCH, HC, KV], F32R)
                vaug = sb(st, n + "vaug", [KV, BATCH, H, DH + 1])
                qb = sb(st, n + "qb", [P, 4 * DC])
                wq_hi, wq_lo = sb(st, n + "wq_hi", [P, DC, D], F32R), sb(st, n + "wq_lo", [P, DC, D], F32R)
                wo_hi, wo_lo = sb(st, n + "wo_hi", [P, DC, D], F32R), sb(st, n + "wo_lo", [P, DC, D], F32R)

                with ExitStack() as s2:
                    stage = sb(s2, n + "stage", [P, 2 * DC, D])
                    wk = sb(s2, n + "wk", [P, D])
                    wv = sb(s2, n + "wv", [P, D])
                    ctx_sb = sb(s2, n + "ctx", [KV, BATCH, CTX])
                    ctxT = sb(s2, n + "ctxT", [P, BATCH, KV])
                    k_hi = sb(s2, n + "k_hi", [P, DC, BATCH * KV], F32R)
                    k_lo = sb(s2, n + "k_lo", [P, DC, BATCH * KV], F32R)
                    pair = sb(s2, n + "pair", [P, 2])
                    head = sb(s2, n + "head", [P, HC])
                    bvb = sb(s2, n + "bvb", [KV, D])

                    def load(dst, src, name):
                        return sp.do(lambda e: e.dma_start(dst, src), sem("attn_in_" + name), 16)

                    ctx_in = load(ctx_sb[:], A["ctx_512"].rearrange("b s c -> s b c"), "ctx")
                    wk_in = load(wk[:], wk_d, "wk")
                    wv_in = load(wv[:], wv_d, "wv")
                    wq_in = load(stage[:, 0:DC, :], wq_d.rearrange("(c p) n -> p c n", p=P), "wq")
                    wo_in = load(stage[:, DC:2 * DC, :], wo_d.rearrange("(c p) n -> p c n", p=P), "wo")
                    if bq_d is not None:
                        bq_in = load(qb[:, 0:DC], bq_d, "bq")
                        bk_in = load(qb[:, DC:2 * DC], bk_d, "bk")
                        bv_in = load(bvb[:], bv_d.rearrange("(a n) -> a n", a=1).broadcast_to([KV, D]), "bv")
                    else:
                        bq_in = bk_in = dve.do(lambda e: e.memset(qb[:], 0.0), sem("attn_bias"))
                        bv_in = dve.do(lambda e: e.memset(bvb[:], 0.0), sem("attn_bias"))

                    pool.do(lambda e: e.memset(pair[:], 1.0), sem("attn_mask"))
                    m = pool.do(lambda e: e.memset(head[:], 1.0), sem("attn_mask"))
                    pool.wait(m)
                    m = pool.do(lambda e: e.affine_select(out=head[:], in_=head[:], compare_op=ALU.is_ge, fill=0.0,
                                                          base=0, pattern=[[-DH, HC]], channel_multiplier=1),
                                sem("attn_mask"))
                    pool.wait(m)
                    m = pool.do(lambda e: e.affine_select(out=head[:], in_=head[:], compare_op=ALU.is_ge, fill=0.0,
                                                          base=DH - 1, pattern=[[DH, HC]], channel_multiplier=-1),
                                sem("attn_mask"))
                    dve.wait(m)
                    m = dve.do(lambda e: e.tensor_reduce(pair[:], head[:].rearrange("p (a i) -> p i a", i=2),
                                                         AX_X, ALU.add), sem("attn_mask2"))
                    mask_done = m

                    for part, (hi, lo), arrived in ((0, (wq_hi, wq_lo), wq_in), (1, (wo_hi, wo_lo), wo_in)):
                        src = stage[:, part * DC:(part + 1) * DC, :]
                        pool.wait(arrived)
                        m = pool.do(lambda e, hi=hi, src=src: e.tensor_copy(hi[:], src), sem("attn_w"))
                        pool.wait(m)
                        w_done = pool.do(lambda e, hi=hi, lo=lo, src=src: e.tensor_tensor(lo[:], src, f(hi[:]),
                                                                                         ALU.subtract), sem("attn_w"))

                    i, w, bf = work.take()
                    pe.wait(bf, ctx_in, const_done)
                    for b in range(BATCH):
                        m = pe.do(lambda e, b=b, w=w: e.transpose(w[:, b * KV:(b + 1) * KV], ctx_sb[:, b, :],
                                                                  ident[0:KV, 0:KV]), sem("attn_ctxT_p"))
                    act.wait(m)
                    ctxT_done = act.do(lambda e, w=w: e.activation(ctxT[:].rearrange("p b s -> p (b s)"),
                                                                   w[:, 0:BATCH * KV], ACT.Copy), sem("attn_ctxT"))
                    work.release(i, ctxT_done)

                    k_done = []
                    for m_ in range(DC):
                        i, w, bf = work.take()
                        pe.wait(bf, wk_in, ctxT_done)
                        m = pe.do(lambda e, w=w, m_=m_: e.matmul(w[:, 0:BATCH * KV], wk[:, m_ * P:(m_ + 1) * P],
                                                                ctxT[:].rearrange("p b s -> p (b s)"),
                                                                start=True, stop=True), sem("attn_k_p"))
                        act.wait(m, bk_in)
                        m = act.do(lambda e, w=w, m_=m_: e.activation(k_hi[:, m_, :], w[:, 0:BATCH * KV], ACT.Identity,
                                                                     bias=qb[:, DC + m_:DC + m_ + 1]), sem("attn_k_hi"))
                        dve.wait(m, bk_in)
                        m = dve.do(lambda e, w=w, m_=m_: e.scalar_tensor_tensor(
                            out=k_lo[:, m_, :], in0=w[:, 0:BATCH * KV], scalar=qb[:, DC + m_:DC + m_ + 1],
                            in1=f(k_hi[:, m_, :]), op0=ALU.add, op1=ALU.subtract), sem("attn_k_lo"))
                        work.release(i, m)
                        k_done.append(m)

                    dve.wait(k_done[-1], mask_done)
                    for m_ in range(DC):
                        for r in range(4):
                            q = slice(32 * r, 32 * r + 32)
                            h0 = m_ * HC + 2 * r
                            for rows, src in ((0, k_hi), (32, k_lo), (64, k_hi)):
                                kaug_done = dve.do(lambda e, q=q, h0=h0, rows=rows, src=src, m_=m_: e.tensor_tensor(
                                    kaug[rows:rows + 32, h0:h0 + 2, :, :].rearrange("p h b s -> p h (b s)"),
                                    f(src[q, m_, :]).rearrange("p (o s) -> p o s", o=1).broadcast_to([32, 2, BATCH * KV]),
                                    pair[q, :].rearrange("p (h o) -> p h o", o=1).broadcast_to([32, 2, BATCH * KV]),
                                    ALU.mult), sem("attn_kaug"))
                    kaug_done = dve.do(lambda e: e.tensor_copy(
                        kaug[96:96 + H, :, :, :].rearrange("p h b s -> p h (b s)"),
                        ident[96:96 + H, 96:96 + H].rearrange("p (h o) -> p h o", o=1).broadcast_to([H, H, BATCH * KV])),
                        sem("attn_kaug"))
                    for m_ in range(DC):
                        for b in range(BATCH):
                            kblk_done = dve.do(lambda e, m_=m_, b=b: e.tensor_tensor(
                                kblk[:, m_, b, :, :],
                                f(k_hi[:, m_, b * KV:(b + 1) * KV]).rearrange("p (o s) -> p o s", o=1)
                                .broadcast_to([P, HC, KV]),
                                head[:].rearrange("p (h o) -> p h o", o=1).broadcast_to([P, HC, KV]),
                                ALU.mult), sem("attn_kblk"))

                    ones = pool.do(lambda e: e.memset(vaug[:, :, :, DH:DH + 1], 1.0), sem("attn_ones"))
                    for b in range(BATCH):
                        i, w, bf = work.take()
                        pe.wait(bf, wv_in, ctxT_done)
                        m = pe.do(lambda e, w=w, b=b: e.matmul(w[0:KV, 0:D], ctxT[:, b, :], wv[:, :],
                                                              start=True, stop=True), sem("attn_v_p"))
                        dve.wait(m, bv_in)
                        v_done = dve.do(lambda e, w=w, b=b: e.tensor_tensor(
                            vaug[:, b, :, 0:DH], w[0:KV, 0:D].rearrange("s (h d) -> s h d", h=H),
                            bvb[:].rearrange("s (h d) -> s h d", h=H), ALU.add), sem("attn_v"))
                        work.release(i, v_done)
                    end_phase()

                xn = sb(st, n + "xn", [P, GT, D])
                xT = sb(st, n + "xT_hi", [P, DC, GN], F32R), sb(st, n + "xT_lo", [P, DC, GN], F32R)
                q_hi, q_lo = sb(st, n + "q_hi", [P, DC, GN], F32R), sb(st, n + "q_lo", [P, DC, GN], F32R)
                qaug = [sb(st, n + f"qaug{i}", [P, DC, 4, GN], F32R) for i in range(2)]
                nmax = sb(st, n + "nmax", [P, GT, H])
                nmaxT = sb(st, n + "nmaxT", [H, GN], F32R)
                prob = sb(st, n + "prob", [KV, H, GN])
                rden = sb(st, n + "rden", [P, 2, H])
                o_sb = sb(st, n + "o", [P, GT, D])
                oT = sb(st, n + "oT_hi", [P, DC, GN], F32R), sb(st, n + "oT_lo", [P, DC, GN], F32R)
                bob = None
                if bo_d is not None:
                    bob = sb(st, n + "bob", [P, D])
                    bo_in = sp.do(lambda e: e.dma_start(bob[:], bo_d.rearrange("(a n) -> a n", a=1)
                                                        .broadcast_to([P, D])), sem("attn_bo"), 16)

                M = {}

                def mark(what, g):
                    return M.get((what, g))

                def front(g):
                    ln = layernorm(g, ln_tmp, xn, xr[g], [mark("xT", g - 1)])
                    yield
                    m = yield from transpose_split(work, xn, ln, xT[0], xT[1], [mark("q_p", g - 1)], "attn_x")
                    M["xT", g] = m
                    b = g * GN // SEQ
                    for m_ in range(DC):
                        i, w, bf = work.take()
                        pe.wait(bf, M["xT", g], w_done)
                        for c in range(DC):
                            ws = slice(m_ * P, (m_ + 1) * P)
                            m = matmul3(w[:, :], wq_hi[:, c, ws], wq_lo[:, c, ws], xT[0][:, c, :], xT[1][:, c, :],
                                        c == 0, c == DC - 1, sem("attn_q_p"))
                        M["q_p", g] = m
                        act.wait(m, bq_in, mark("qaug", g - 1), mark("max_p", g - 1))
                        m = act.do(lambda e, w=w, m_=m_: e.activation(q_hi[:, m_, :], w[:, :], ACT.Identity,
                                                                     bias=qb[:, m_:m_ + 1]), sem("attn_q_hi"))
                        dve.wait(m, bq_in, mark("qaug", g - 1))
                        m = dve.do(lambda e, w=w, m_=m_: e.scalar_tensor_tensor(
                            out=q_lo[:, m_, :], in0=w[:, :], scalar=qb[:, m_:m_ + 1], in1=f(q_hi[:, m_, :]),
                            op0=ALU.add, op1=ALU.subtract), sem("attn_q_lo"))
                        work.release(i, m)
                        M["q", g] = m
                        yield
                    dst = qaug[g % 2]
                    sp.wait(M["q", g], mark("s_p", g - 2))
                    s_q = sem(f"attn_qaug{g % 2}")
                    for r in range(4):
                        for rows, src in ((0, q_hi), (32, q_hi), (64, q_lo)):
                            sp.do(lambda e, dst=dst, r=r, rows=rows, src=src: e.dma_start(
                                f(dst[rows:rows + 32, :, r, :]), f(src[32 * r:32 * r + 32, :, :])), s_q, 16)
                    for j in range(GT):
                        for m_ in range(DC):
                            for half in range(2):
                                i, w, bf = smax.take()
                                pe.wait(bf, M["q", g], kblk_done)
                                hs = slice(half * HC // 2, (half + 1) * HC // 2)
                                m = pe.do(lambda e, w=w, j=j, m_=m_, hs=hs: e.matmul(
                                    w[:, 0:HC // 2 * KV], q_hi[:, m_, j * P:(j + 1) * P],
                                    kblk[:, m_, b, hs, :].rearrange("p h s -> p (h s)"), start=True, stop=True),
                                    sem("attn_max_p"))
                                M["max_p", g] = m
                                h0 = m_ * HC + half * HC // 2
                                dve.wait(m, mark("nmaxT_p", g - 1))
                                m = dve.do(lambda e, w=w, j=j, h0=h0: e.tensor_reduce(
                                    nmax[:, j, h0:h0 + HC // 2],
                                    w[:, 0:HC // 2 * KV].rearrange("p (h s) -> p h s", s=KV), AX_X, ALU.max,
                                    negate=True), sem("attn_nmax"))
                                smax.release(i, m)
                            yield
                    i, w, bf = work.take()
                    pe.wait(bf, m)
                    for j in range(GT):
                        m = pe.do(lambda e, w=w, j=j: e.transpose(w[0:H, j * P:(j + 1) * P], nmax[:, j, :],
                                                                 ident[:, :]), sem("attn_nmaxT_p"))
                    M["nmaxT_p", g] = m
                    dve.wait(m, mark("qaug", g - 1))
                    m = dve.do(lambda e, w=w: e.tensor_copy(nmaxT[:, :], w[0:H, :]), sem("attn_nmaxT"))
                    work.release(i, m)
                    sp.wait(m)
                    M["qaug", g] = sp.do(lambda e, dst=dst: e.dma_start(
                        f(dst[96:96 + H, :, :, :]).rearrange("p m r t -> p (m r) t"),
                        f(nmaxT[:, :]).rearrange("p (o t) -> p o t", o=1).broadcast_to([H, 4 * DC, GN])), s_q, 16)
                    yield

                def scores(g):
                    b = g * GN // SEQ
                    for h in range(H):
                        i, w, bf = sexp.take()
                        pe.wait(bf, M["qaug", g], kaug_done)
                        m = pe.do(lambda e, w=w, h=h: e.matmul(w[0:KV, :], kaug[0:96 + H, h, b, :],
                                                              qaug[g % 2][0:96 + H, h // HC, h % HC // 2, :],
                                                              start=True, stop=True), sem("attn_s_p"))
                        M["s_p", g] = m
                        act.wait(m, mark("pv_p", g - 1))
                        m = act.do(lambda e, w=w, h=h: e.activation(prob[:, h, :], w[0:KV, :], ACT.Exp,
                                                                   scale=float(DH) ** -0.5), sem("attn_prob"))
                        sexp.release(i, m)
                        M["prob", g] = m
                        yield

                def back(g):
                    b = g * GN // SEQ
                    for j in range(GT):
                        i, w, bf = work.take()
                        pe.wait(bf, M["prob", g], v_done, ones)
                        for h in range(H):
                            m = pe.do(lambda e, w=w, j=j, h=h: e.matmul(
                                w[:, h * (DH + 1):(h + 1) * (DH + 1)], prob[:, h, j * P:(j + 1) * P],
                                vaug[:, b, h, :], start=True, stop=True), sem("attn_pv_p") if h == H - 1 else None)
                        M["pv_p", g] = m
                        o = w[:, 0:H * (DH + 1)].rearrange("p (h d) -> p h d", d=DH + 1)
                        dve.wait(m)
                        m = dve.do(lambda e, o=o, j=j: e.reciprocal(
                            rden[:, j % 2, :].rearrange("p (h o) -> p h o", o=1), o[:, :, DH:DH + 1]),
                            sem("attn_rden"))
                        dve.wait(m, mark("oT_p", g - 1))
                        m = dve.do(lambda e, o=o, j=j: e.tensor_tensor(
                            o_sb[:, j, :].rearrange("p (h d) -> p h d", d=DH), o[:, :, 0:DH],
                            rden[:, j % 2, :].rearrange("p (h o) -> p h o", o=1).broadcast_to([P, H, DH]),
                            ALU.mult), sem("attn_o"))
                        work.release(i, m)
                        M["o", g] = m
                        yield
                    m = yield from transpose_split(work, o_sb, M["o", g], oT[0], oT[1], [mark("y_p", g - 1)], "attn_o")
                    M["oT_p", g] = m
                    for j in range(GT):
                        i, w, bf = work.take()
                        pe.wait(bf, M["oT_p", g], w_done)
                        ts = slice(j * P, (j + 1) * P)
                        for c in range(DC):
                            m = matmul3(w[:, 0:D], oT[0][:, c, ts], oT[1][:, c, ts], wo_hi[:, c, :], wo_lo[:, c, :],
                                        c == 0, c == DC - 1, sem("attn_y_p"))
                        M["y_p", g] = m
                        xt = x_sb[:, g * GT + j, :]
                        dve.wait(m)
                        m = dve.do(lambda e, w=w, xt=xt: e.tensor_tensor(xt, w[:, 0:D], xt, ALU.add), sem("attn_x"))
                        work.release(i, m)
                        if bob is not None:
                            pool.wait(m, bo_in)
                            m = pool.do(lambda e, xt=xt: e.tensor_tensor(xt, xt, bob[:], ALU.add), sem("attn_xb"))
                        M["x", g] = m
                        yield

                interleave((front(0), 1))
                for g in range(NG + 1):
                    streams = []
                    if g < NG:
                        streams.append((scores(g), 1))
                    if g > 0:
                        streams.insert(0, (back(g - 1), 1))
                    if g + 1 < NG:
                        streams.append((front(g + 1), 1))
                    if g > 0 and g < NG:
                        bk = back(g - 1)
                        for _ in range(GT):
                            next(bk)
                        streams[0] = (bk, 1)
                    interleave(*streams)
                end_phase()
            return [[M["x", g]] for g in range(NG)]

        def experts_swiglu(xr):
            st = ExitStack()
            with st:
                n = "e0_"
                xn = sb(st, n + "xn", [P, NT, D])
                gate = sb(st, n + "gate", [P, NT, E0])
                s_gate = sem(n + "gate")
                with ExitStack() as s2:
                    work = Banks([bank[i] for i in range(3)])
                    ln_tmp = (sb(s2, n + "stats", [P, 2, GT, 6]), sb(s2, n + "mv", [P, 2, GT, 2]),
                              sb(s2, n + "rstd", [P, 2, 2, GT]))
                    xT = [sb(s2, n + f"xT{i}", [P, DC, GN]) for i in range(2)]
                    wg = sb(s2, n + "wg", [P, DC, E0])
                    lg = sb(s2, n + "lg", [P, NT, E0])
                    pr = sb(s2, n + "pr", [P, NT, E0])
                    red = sb(s2, n + "red", [P, 3, NT])
                    wg_in = sp.do(lambda e: e.dma_start(wg[:], A["L0_ffn_wg"].rearrange("(c p) n -> p c n", p=P)),
                                  sem(n + "wg"), 16)
                    logits = bank[7]
                    xT_used = [None, None]
                    for g in range(NG):
                        ln = layernorm(g, ln_tmp, xn[:, g * GT:(g + 1) * GT, :], xr[g], [])
                        for c in range(DC):
                            i, w, bf = work.take()
                            pe.wait(bf, ln)
                            for j in range(GT):
                                m = pe.do(lambda e, w=w, g=g, c=c, j=j: e.transpose(
                                    w[:, j * P:(j + 1) * P], xn[:, g * GT + j, c * P:(c + 1) * P], ident[:, :]),
                                    sem(n + "xT_p") if j == GT - 1 else None)
                            act.wait(m, xT_used[g % 2])
                            m = act.do(lambda e, w=w, g=g, c=c: e.activation(xT[g % 2][:, c, :], w[:, :], ACT.Copy),
                                       sem(n + "xT"))
                            work.release(i, m)
                        pe.wait(m, wg_in)
                        for j in range(GT):
                            t = g * GT + j
                            for c in range(DC):
                                m = pe.do(lambda e, g=g, c=c, j=j, t=t: e.matmul(
                                    logits[:, t * E0:(t + 1) * E0], xT[g % 2][:, c, j * P:(j + 1) * P], wg[:, c, :],
                                    start=(c == 0), stop=(c == DC - 1)), sem(n + "logits"))
                        xT_used[g % 2] = m
                    def bc(k):
                        return red[:, k, :].rearrange("p (t o) -> p t o", o=1).broadcast_to([P, NT, E0])

                    lgv = logits[:, 0:NT * E0].rearrange("p (t e) -> p t e", e=E0)
                    dve.wait(m)
                    m = dve.do(lambda e: e.tensor_reduce(red[:, 0, :], lgv, AX_X, ALU.max), s_gate)
                    dve.wait(m)
                    m = dve.do(lambda e: e.tensor_tensor(lg[:], lgv, bc(0), ALU.subtract), s_gate)
                    act.wait(m)
                    m = act.do(lambda e: e.activation(lg[:], lg[:], ACT.Exp), sem(n + "exp"))
                    dve.wait(m)
                    m = dve.do(lambda e: e.tensor_reduce(red[:, 1, :], lg[:], AX_X, ALU.add), s_gate)
                    dve.wait(m)
                    m = dve.do(lambda e: e.reciprocal(red[:, 2, :], red[:, 1, :]), s_gate)
                    dve.wait(m)
                    m = dve.do(lambda e: e.tensor_tensor(
                        pr[:].rearrange("p t e -> p e t"), lg[:].rearrange("p t e -> p e t"),
                        red[:, 2, :].rearrange("p (o t) -> p o t", o=1).broadcast_to([P, E0, NT]), ALU.mult), s_gate)
                    select_tokens(s2, n, pr, gate, m)
                    end_phase()

                ffn_blocks(st, n, xn, gate)
                end_phase()

        NCH = P // E0
        CHT = NT // NCH
        CHN = CHT * P

        def select_tokens(s2, n, pr, gate, ready):
            s = sem(n + "sel")
            cb = Banks([bank[3], bank[4]])
            prc = sb(s2, n + "prc", [P, CHT, E0, NCH])
            prT = sb(s2, n + "prT", [P, CHN])
            junk = sb(s2, n + "junk", [P, CHN])
            cnt = sb(s2, n + "cnt", [P, 2])
            cand = sb(s2, n + "cand", [P, 2], I32)
            flip = sb(s2, n + "flip", [P, 1], I32)
            bits = sb(s2, n + "bits", [P, 31], I32)
            same = sb(s2, n + "same", [P, E0, NCH])
            before = sb(s2, n + "before", [P, E0, NCH])
            eq = sb(s2, n + "eq", [P, CHN])
            gt = sb(s2, n + "gt", [P, CHN])
            rank = sb(s2, n + "rank", [P, CHN])
            zeros = sb(s2, n + "zeros", [P, CHN])
            tot = sb(s2, n + "tot", [P, 4])

            k = sem(n + "selc")
            m = pool.do(lambda e: e.memset(same[:], 1.0), k)
            m = pool.do(lambda e: e.memset(zeros[:], 0.0), k)
            pool.wait(m)
            for sgn, base in ((1, 0), (-1, NCH - 1)):
                m = pool.do(lambda e, sgn=sgn, base=base: e.affine_select(
                    out=same[:], in_=same[:], compare_op=ALU.is_ge, fill=0.0, base=base,
                    pattern=[[-sgn * NCH, E0], [0, NCH]], channel_multiplier=sgn), k)
                pool.wait(m)
            m = pool.do(lambda e: e.affine_select(out=before[:], in_=same[:], compare_op=ALU.is_gt, fill=0.0, base=0,
                                                  pattern=[[NCH, E0], [1, NCH]], channel_multiplier=-1), k)
            for b in range(30):
                m = pool.do(lambda e, b=b: e.memset(bits[:, b:b + 1], 1 << b), k)
            consts = m
            same2, before2 = same[:].rearrange("p e c -> p (e c)"), before[:].rearrange("p e c -> p (e c)")

            dve.wait(ready)
            m = dve.do(lambda e: e.tensor_copy(prc[:].rearrange("p j e c -> p e c j"),
                                               pr[:].rearrange("p (c j) e -> p e c j", j=CHT)), s)
            pe.wait(m)
            i, w, bf = cb.take()
            for j in range(CHT):
                m = pe.do(lambda e, w=w, j=j: e.transpose(w[:, j * P:(j + 1) * P],
                                                          prc[:, j, :, :].rearrange("p e c -> p (e c)"), ident[:, :]),
                          sem(n + "selp"))
            dve.wait(m, consts)
            m = dve.do(lambda e, w=w: e.tensor_copy(prT[:], w[:, 0:CHN]), s)
            cb.release(i, m)
            dve.wait(m)
            m = dve.do(lambda e: e.tensor_copy(cand[:, 0:1], bits[:, 29:30]), s)
            for b in range(29, -1, -1):
                dve.wait(m)
                m = dve.do(lambda e: e.tensor_scalar(junk[:], prT[:], cand[:, 0:1].bitcast(F32), None, ALU.is_ge,
                                                     ALU.add, accum_out=cnt[:, 0:1]), s)
                i, w, bf = cb.take()
                pe.wait(m, bf)
                m = pe.do(lambda e, w=w: e.matmul(w[:, 0:1], same2, cnt[:, 0:1], start=True, stop=True),
                          sem(n + "selp"))
                dve.wait(m)
                m = dve.do(lambda e, w=w, b=b: e.tensor_scalar(flip[:], w[:, 0:1], float(CAP), float(1 << b),
                                                               ALU.is_lt, ALU.mult), s)
                cb.release(i, m)
                dve.wait(m)
                if b:
                    m = dve.do(lambda e, b=b: e.scalar_tensor_tensor(
                        out=cand[:, 0:1], in0=flip[:], scalar=bits[:, b - 1:b], in1=cand[:, 0:1],
                        op0=ALU.bitwise_or, op1=ALU.bitwise_xor), s)
                else:
                    m = dve.do(lambda e: e.tensor_tensor(cand[:, 0:1], flip[:], cand[:, 0:1], ALU.bitwise_xor), s)
            thr = cand[:, 0:1].bitcast(F32)
            dve.wait(m)
            dve.do(lambda e: e.tensor_scalar(gt[:], prT[:], thr, None, ALU.is_gt, ALU.add, accum_out=tot[:, 0:1]), s)
            m = dve.do(lambda e: e.tensor_scalar(eq[:], prT[:], thr, None, ALU.is_equal, ALU.add,
                                                 accum_out=tot[:, 1:2]), s)
            i, w, bf = cb.take()
            pe.wait(m, bf)
            pe.do(lambda e, w=w: e.matmul(w[:, 0:1], same2, tot[:, 0:1], start=True, stop=True))
            m1 = pe.do(lambda e, w=w: e.matmul(w[:, 1:2], before2, tot[:, 1:2], start=True, stop=True),
                       sem(n + "selp"))
            dve.wait(m)
            m = dve.do(lambda e: e.tensor_tensor_scan(rank[:], eq[:], zeros[:], 0.0, ALU.add, ALU.add), s)
            dve.wait(m1)
            m2 = dve.do(lambda e, w=w: e.tensor_copy(tot[:, 2:4], w[:, 0:2]), s)
            cb.release(i, m2)
            dve.wait(m2)
            m = dve.do(lambda e: e.tensor_tensor(tot[:, 0:1], tot[:, 2:3], tot[:, 3:4], ALU.add), s)
            dve.wait(m)
            m = dve.do(lambda e: e.tensor_scalar(rank[:], rank[:], tot[:, 0:1], float(CAP), ALU.add, ALU.is_le), s)
            dve.wait(m)
            m = dve.do(lambda e: e.tensor_tensor(eq[:], eq[:], rank[:], ALU.mult), s)
            dve.wait(m)
            m = dve.do(lambda e: e.tensor_tensor(gt[:], gt[:], eq[:], ALU.add), s)
            dve.wait(m)
            m = dve.do(lambda e: e.tensor_tensor(prT[:], prT[:], gt[:], ALU.mult), s)
            pe.wait(m)
            i, w, bf = cb.take()
            pe.wait(bf)
            for j in range(CHT):
                m = pe.do(lambda e, w=w, j=j: e.transpose(w[:, j * P:(j + 1) * P], prT[:, j * P:(j + 1) * P],
                                                          ident[:, :]), sem(n + "selp"))
            dve.wait(m)
            m = dve.do(lambda e, w=w: e.tensor_copy(gate[:].rearrange("p (c j) e -> p j e c", j=CHT),
                                                    w[:, 0:CHN].rearrange("p (j e c) -> p j e c", j=CHT, e=E0)), s)
            cb.release(i, m)

        def ffn_blocks(st, n, xn, gate):
            tb, ab, yb = Banks(bank[0:2]), Banks(bank[2:6]), Banks(bank[6:8])
            HCH = HID0 // P
            xs = sb(st, n + "xs", [P, GT, D])
            xT = [(sb(st, n + f"xs_hi{i}", [P, DC, GN], F32R), sb(st, n + f"xs_lo{i}", [P, DC, GN], F32R))
                  for i in range(2)]
            hT = (sb(st, n + "h_hi", [P, HCH, GN], F32R), sb(st, n + "h_lo", [P, HCH, GN], F32R))
            silu = [sb(st, n + f"silu{i}", [P, GN]) for i in range(2)]
            h32 = [sb(st, n + f"h32_{i}", [P, GN]) for i in range(2)]
            cols = (DC * HID0, DC * HID0, HCH * D)
            stage = sb(st, n + "stage", [P, sum(cols)])
            wts = [(sb(st, n + f"w_hi{i}", [P, sum(cols)], F32R), sb(st, n + f"w_lo{i}", [P, sum(cols)], F32R))
                   for i in range(2)]
            M = {}

            def mark(*k):
                return M.get(k)

            def weights(e):
                at = 0
                for k, name in enumerate(("w1", "w3", "w2")):
                    src = A["L0_ffn_" + name][e].rearrange("(c p) n -> p c n", p=P)
                    dst = stage[:, at:at + cols[k]].rearrange("p (c n) -> p c n", c=src.shape[1])
                    sp.wait(mark("w", e - 1, k))
                    arrived = sp.do(lambda q, dst=dst, src=src: q.dma_start(dst, src), sem(n + "stage" + name), 16)
                    hi, lo = (t[:, at:at + cols[k]] for t in wts[e % 2])
                    raw = stage[:, at:at + cols[k]]
                    pool.wait(arrived, mark("y_p", (e - 1) * NG - 1))
                    m = pool.do(lambda q, hi=hi, raw=raw: q.tensor_copy(hi, raw), sem(n + "w"))
                    pool.wait(m)
                    M["w", e, k] = pool.do(lambda q, hi=hi, lo=lo, raw=raw: q.tensor_tensor(lo, raw, f(hi),
                                                                                           ALU.subtract), sem(n + "w"))
                    at += cols[k]

            def wview(e, k, part):
                at = sum(cols[:k])
                return wts[e % 2][part][:, at:at + cols[k]].rearrange("p (c n) -> p c n", n=HID0 if k < 2 else D)

            def load(i):
                e, g = divmod(i, NG)
                for j in range(GT):
                    t = g * GT + j
                    dve.wait(mark("xT", i - 1))
                    m = dve.do(lambda q, t=t, j=j: q.tensor_scalar(xs[:, j, :], xn[:, t, :], gate[:, t, e:e + 1], None,
                                                                   ALU.mult), sem(n + "xs"))
                m = yield from transpose_split(tb, xs, m, xT[i % 2][0], xT[i % 2][1], [mark("h_p", i - 2)], n + "x")
                M["xT", i] = m

            def hidden(i):
                e = i // NG
                x_hi, x_lo = xT[i % 2]
                for m_ in range(HCH):
                    ia, wa, fa = ab.take()
                    ib, wb, fb = ab.take()
                    ws = slice(m_ * P, (m_ + 1) * P)
                    pe.wait(M["xT", i], M["w", e, 1])
                    for k, w, bf in ((0, wa, fa), (1, wb, fb)):
                        pe.wait(bf)
                        for c in range(DC):
                            m = matmul3(w[:, :], wview(e, k, 0)[:, c, ws], wview(e, k, 1)[:, c, ws], x_hi[:, c, :],
                                        x_lo[:, c, :], c == 0, c == DC - 1, sem(n + "h_p"))
                        if k == 0:
                            act.wait(m, mark("h32", i, m_ - 2) if m_ > 1 else mark("h32", i - 1, m_ + HCH - 2))
                            ms = act.do(lambda q, w=w, m_=m_: q.activation(silu[m_ % 2][:], w[:, :], ACT.Silu),
                                        sem(n + "silu"))
                            ab.release(ia, ms)
                    M["h_p", i] = m
                    dve.wait(m, ms, mark("h_hi", i, m_ - 2) if m_ > 1 else mark("h_hi", i - 1, m_ + HCH - 2))
                    m = dve.do(lambda q, w=wb, m_=m_: q.tensor_tensor(h32[m_ % 2][:], silu[m_ % 2][:], w[:, :],
                                                                     ALU.mult), sem(n + "h32"))
                    ab.release(ib, m)
                    M["h32", i, m_] = m
                    act.wait(m, mark("y_p", i - 1))
                    m = act.do(lambda q, m_=m_: q.activation(hT[0][:, m_, :], h32[m_ % 2][:], ACT.Copy),
                               sem(n + "h_hi"))
                    M["h_hi", i, m_] = m
                    dve.wait(m, mark("y_p", i - 1))
                    m = dve.do(lambda q, m_=m_: q.tensor_tensor(hT[1][:, m_, :], h32[m_ % 2][:],
                                                               f(hT[0][:, m_, :]), ALU.subtract), sem(n + "h_lo"))
                    M["h", i] = m
                    yield

            def output(i):
                e, g = divmod(i, NG)
                for j in range(GT):
                    iy, w, bf = yb.take()
                    ts = slice(j * P, (j + 1) * P)
                    pe.wait(bf, M["h", i], M["w", e, 2])
                    for c in range(HCH):
                        m = matmul3(w[:, 0:D], hT[0][:, c, ts], hT[1][:, c, ts], wview(e, 2, 0)[:, c, :],
                                    wview(e, 2, 1)[:, c, :], c == 0, c == HCH - 1, sem(n + "y_p"))
                    M["y_p", i] = m
                    xt = x_sb[:, g * GT + j, :]
                    dve.wait(m, mark("x", i - 1))
                    m = dve.do(lambda q, w=w, xt=xt: q.tensor_tensor(xt, w[:, 0:D], xt, ALU.add), sem(n + "x"))
                    yb.release(iy, m)
                    M["x", i] = m
                    yield

            NB = E0 * NG
            weights(0)
            interleave((load(0), 1))
            for i in range(NB):
                if i % NG == 1 and i // NG + 1 < E0:
                    weights(i // NG + 1)
                interleave((hidden(i), 1), *([(load(i + 1), 1)] if i + 1 < NB else []))
                interleave((output(i), 1))

        def experts_relu(xr):
            st = ExitStack()
            with st:
                n = "e1_"
                NE = E1 + 1
                cw = sb(st, n + "cw", [P, NT, NE])
                cwT = sb(st, n + "cwT", [NE, NT, P])
                b2 = sb(st, n + "b2", [NE, D])
                b1 = sb(st, n + "b1", [P, NE, HID1 // P])
                b2_in = [sp.do(lambda e: e.dma_start(b2[0:E1, :], A["L1_ffn_eb2"]), sem(n + "b2"), 16),
                         sp.do(lambda e: e.dma_start(b2[E1:NE, :], A["L1_ffn_sb2"].rearrange("(a n) -> a n", a=1)),
                               sem(n + "b2s"), 16)]
                b1_in = [sp.do(lambda e: e.dma_start(b1[:, 0:E1, :], A["L1_ffn_eb1"]), sem(n + "b1"), 16),
                         sp.do(lambda e: e.dma_start(b1[:, E1, :], A["L1_ffn_sb1"]),
                               sem(n + "b1s"), 16)]
                xT = [(sb(st, n + f"xT_hi{g}", [P, DC, GN], F32R), sb(st, n + f"xT_lo{g}", [P, DC, GN], F32R))
                      for g in range(NG)]
                xT_done = []
                with ExitStack() as s2:
                    work = Banks([bank[i] for i in range(3)])
                    ln_tmp = (sb(s2, n + "stats", [P, 2, GT, 6]), sb(s2, n + "mv", [P, 2, GT, 2]),
                              sb(s2, n + "rstd", [P, 2, 2, GT]))
                    xn = sb(s2, n + "xn", [P, GT, D])
                    x32 = [sb(s2, n + f"x32_{i}", [P, DC, GN]) for i in range(2)]
                    rw = sb(s2, n + "rw", [P, DC, E1])
                    rb = sb(s2, n + "rb", [P, E1])
                    lg = sb(s2, n + "lg", [P, NT, E1])
                    pr = sb(s2, n + "pr", [P, NT, E1])
                    red = sb(s2, n + "red", [P, 3, NT])
                    top8 = sb(s2, n + "top8", [P, NT, 8])
                    eq = sb(s2, n + "eq", [P, NT, E1])
                    gt = sb(s2, n + "gt", [P, NT, E1])
                    rank = sb(s2, n + "rank", [P, NT * E1])
                    ngt = sb(s2, n + "ngt", [P, NT])
                    seg = sb(s2, n + "seg", [P, NT, E1])
                    rw_in = sp.do(lambda e: e.dma_start(rw[:], A["L1_ffn_router_W"].rearrange("(c p) n -> p c n", p=P)),
                                  sem(n + "rw"), 16)
                    rb_in = sp.do(lambda e: e.dma_start(rb[:], A["L1_ffn_router_b"].rearrange("(a n) -> a n", a=1)
                                                        .broadcast_to([P, E1])), sem(n + "rb"), 16)
                    logits = bank[7]
                    x32_used = [None, None]
                    xT_p = None
                    for g in range(NG):
                        ln = layernorm(g, ln_tmp, xn, xr[g], [xT_p])
                        for c in range(DC):
                            i, w, bf = work.take()
                            pe.wait(bf, ln)
                            for j in range(GT):
                                m = pe.do(lambda e, w=w, c=c, j=j: e.transpose(
                                    w[:, j * P:(j + 1) * P], xn[:, j, c * P:(c + 1) * P], ident[:, :]),
                                    sem(n + "xT_p") if j == GT - 1 else None)
                            xT_p = m
                            act.wait(m, x32_used[g % 2])
                            m = act.do(lambda e, w=w, g=g, c=c: e.activation(x32[g % 2][:, c, :], w[:, :], ACT.Copy),
                                       sem(n + "x32"))
                            work.release(i, m)
                            pool.wait(m)
                            mh = pool.do(lambda e, g=g, c=c: e.tensor_copy(xT[g][0][:, c, :], x32[g % 2][:, c, :]),
                                         sem(n + "xT_hi"))
                            dve.wait(mh)
                            ml = dve.do(lambda e, g=g, c=c: e.tensor_tensor(xT[g][1][:, c, :], x32[g % 2][:, c, :],
                                                                           f(xT[g][0][:, c, :]), ALU.subtract),
                                        sem(n + "xT_lo"))
                        xT_done.append(ml)
                        pe.wait(m, rw_in)
                        for j in range(GT):
                            t = g * GT + j
                            for c in range(DC):
                                m = pe.do(lambda e, g=g, c=c, j=j, t=t: e.matmul(
                                    logits[:, t * NE:t * NE + E1], x32[g % 2][:, c, j * P:(j + 1) * P], rw[:, c, :],
                                    start=(c == 0), stop=(c == DC - 1)), sem(n + "logits"))
                        pe.wait(ml)
                        x32_used[g % 2] = pe.do(lambda e: e.nop(), sem(n + "x32_used"))

                    s = sem(n + "route")

                    def bc(a, e=E1):
                        return a.rearrange("p (t o) -> p t o", o=1).broadcast_to([P, NT, e])

                    def step(fn, *marks):
                        dve.wait(*(marks or (last[0],)))
                        last[0] = dve.do(fn, s)

                    last = [m]
                    lgv = logits[:, :].rearrange("p (t e) -> p t e", e=NE)[:, :, 0:E1]
                    step(lambda e: e.tensor_tensor(lg[:], lgv, rb[:].rearrange("p (o e) -> p o e", o=1)
                                                   .broadcast_to([P, NT, E1]), ALU.add), m, rb_in)
                    step(lambda e: e.tensor_reduce(red[:, 0, :], lg[:], AX_X, ALU.max))
                    step(lambda e: e.tensor_tensor(lg[:], lg[:], bc(red[:, 0, :]), ALU.subtract))
                    act.wait(last[0])
                    m = act.do(lambda e: e.activation(pr[:], lg[:], ACT.Exp), sem(n + "exp"))
                    step(lambda e: e.tensor_reduce(red[:, 1, :], pr[:], AX_X, ALU.add), m)
                    step(lambda e: e.reciprocal(red[:, 2, :], red[:, 1, :]))
                    step(lambda e: e.tensor_tensor(pr[:], pr[:], bc(red[:, 2, :]), ALU.mult))
                    dve.wait(last[0])
                    for t in range(NT):
                        last[0] = dve.do(lambda e, t=t: e.max(top8[:, t, :], pr[:, t, :]), s)
                    thr = top8[:, :, TOP - 1]
                    step(lambda e: e.tensor_tensor(gt[:], pr[:], bc(thr), ALU.is_gt))
                    step(lambda e: e.tensor_tensor(eq[:], pr[:], bc(thr), ALU.is_equal))
                    step(lambda e: e.tensor_reduce(ngt[:], gt[:], AX_X, ALU.add))
                    step(lambda e: e.memset(seg[:], 1.0))
                    step(lambda e: e.memset(seg[:, :, 0:1], 0.0))
                    step(lambda e: e.tensor_tensor_scan(rank[:], seg[:].rearrange("p t e -> p (t e)"),
                                                        eq[:].rearrange("p t e -> p (t e)"), 0.0, ALU.mult, ALU.add))
                    rk = rank[:].rearrange("p (t e) -> p t e", e=E1)
                    step(lambda e: e.tensor_tensor(rk, rk, bc(ngt[:]), ALU.add))
                    step(lambda e: e.tensor_scalar(rk, rk, float(TOP), None, ALU.is_le))
                    step(lambda e: e.tensor_tensor(eq[:], eq[:], rk, ALU.mult))
                    step(lambda e: e.tensor_tensor(gt[:], gt[:], eq[:], ALU.add))
                    step(lambda e: e.tensor_tensor(cw[:, :, 0:E1], gt[:], pr[:], ALU.mult))
                    step(lambda e: e.memset(cw[:, :, E1:NE], 1.0))
                    for g in range(NG):
                        i, w, bf = work.take()
                        pe.wait(bf, last[0])
                        for j in range(GT):
                            m = pe.do(lambda e, w=w, g=g, j=j: e.transpose(w[0:NE, j * P:(j + 1) * P],
                                                                          cw[:, g * GT + j, :], ident[:, :]),
                                      sem(n + "cwT_p"))
                        act.wait(m)
                        cwT_done = act.do(lambda e, w=w, g=g: e.activation(
                            cwT[:, g * GT:(g + 1) * GT, :].rearrange("p t n -> p (t n)"), w[0:NE, :], ACT.Copy),
                            sem(n + "cwT"))
                        work.release(i, cwT_done)
                    pe.wait(cwT_done, *b2_in)
                    for t in range(NT):
                        i, w, bf = work.take()
                        pe.wait(bf)
                        m = pe.do(lambda e, w=w, t=t: e.matmul(w[:, 0:D], cwT[:, t, :], b2[:, :], start=True, stop=True),
                                  sem(n + "b2_p"))
                        dve.wait(m)
                        m = dve.do(lambda e, w=w, t=t: e.tensor_tensor(x_sb[:, t, :], w[:, 0:D], x_sb[:, t, :], ALU.add),
                                   sem(n + "xb"))
                        work.release(i, m)
                    end_phase()

                ab, yb = Banks(bank[0:4]), Banks(bank[4:8])
                HCH = HID1 // P
                h32 = [sb(st, n + f"h32_{i}", [P, GN]) for i in range(2)]
                hT = [(sb(st, n + f"h_hi{i}", [P, HCH, GN], F32R), sb(st, n + f"h_lo{i}", [P, HCH, GN], F32R))
                      for i in range(2)]
                cols = (DC * HID1, HCH * D)
                stage = sb(st, n + "stage", [P, sum(cols)])
                wts = [(sb(st, n + f"w_hi{i}", [P, sum(cols)], F32R), sb(st, n + f"w_lo{i}", [P, sum(cols)], F32R))
                       for i in range(2)]
                M = {}

                def mark(*k):
                    return M.get(k)

                def weights(e):
                    at = 0
                    for k, (name, sname) in enumerate((("eW1", "sW1"), ("eW2", "sW2"))):
                        src = (A["L1_ffn_" + name][e] if e < E1 else A["L1_ffn_" + sname]).rearrange(
                            "(c p) n -> p c n", p=P)
                        raw = stage[:, at:at + cols[k]]
                        sp.wait(mark("w", e - 1, k))
                        arrived = sp.do(lambda q, raw=raw, src=src: q.dma_start(
                            raw.rearrange("p (c n) -> p c n", c=src.shape[1]), src), sem(n + "stage" + name), 16)
                        hi, lo = (t[:, at:at + cols[k]] for t in wts[e % 2])
                        pool.wait(arrived, mark("y_p", (e - 1) * NG - 1))
                        m = pool.do(lambda q, hi=hi, raw=raw: q.tensor_copy(hi, raw), sem(n + "w"))
                        pool.wait(m)
                        M["w", e, k] = pool.do(lambda q, hi=hi, lo=lo, raw=raw: q.tensor_tensor(
                            lo, raw, f(hi), ALU.subtract), sem(n + "w"))
                        at += cols[k]

                def wview(e, k, part):
                    at = sum(cols[:k])
                    return wts[e % 2][part][:, at:at + cols[k]].rearrange("p (c n) -> p c n", c=2)

                def hidden(i):
                    e, g = divmod(i, NG)
                    x_hi, x_lo = xT[g]
                    for m_ in range(HCH):
                        ia, w, bf = ab.take()
                        ws = slice(m_ * P, (m_ + 1) * P)
                        pe.wait(bf, xT_done[g], M["w", e, 0])
                        for c in range(DC):
                            m = matmul3(w[:, :], wview(e, 0, 0)[:, c, ws], wview(e, 0, 1)[:, c, ws], x_hi[:, c, :],
                                        x_lo[:, c, :], c == 0, c == DC - 1, sem(n + "h_p"))
                        act.wait(m, mark("h_lo", i - 1, m_), *b1_in)
                        m = act.do(lambda q, w=w, m_=m_, e=e: q.activation(h32[m_][:], w[:, :], ACT.Relu,
                                                                         bias=b1[:, e, m_:m_ + 1]), sem(n + "h32"))
                        ab.release(ia, m)
                        act.wait(m, mark("y_p", i - 2))
                        m = act.do(lambda q, m_=m_: q.activation(hT[i % 2][0][:, m_, :], h32[m_][:], ACT.Copy),
                                   sem(n + "h_hi"))
                        dve.wait(m)
                        m = dve.do(lambda q, m_=m_: q.tensor_tensor(hT[i % 2][1][:, m_, :], h32[m_][:],
                                                                   f(hT[i % 2][0][:, m_, :]), ALU.subtract),
                                   sem(n + "h_lo"))
                        M["h_lo", i, m_] = m
                        M["h", i] = m
                        yield

                def output(i):
                    e, g = divmod(i, NG)
                    h_hi, h_lo = hT[i % 2]
                    for j in range(GT):
                        iy, w, bf = yb.take()
                        ts = slice(j * P, (j + 1) * P)
                        pe.wait(bf, M["h", i], M["w", e, 1])
                        for c in range(HCH):
                            m = matmul3(w[:, 0:D], h_hi[:, c, ts], h_lo[:, c, ts], wview(e, 1, 0)[:, c, :],
                                        wview(e, 1, 1)[:, c, :], c == 0, c == HCH - 1, sem(n + "y_p"))
                        M["y_p", i] = m
                        t = g * GT + j
                        dve.wait(m, mark("x", i - 1))
                        m = dve.do(lambda q, w=w, t=t: q.scalar_tensor_tensor(
                            out=x_sb[:, t, :], in0=w[:, 0:D], scalar=cw[:, t, e:e + 1], in1=x_sb[:, t, :],
                            op0=ALU.mult, op1=ALU.add), sem(n + "x"))
                        yb.release(iy, m)
                        M["x", i] = m
                        if j % 2:
                            yield
                    if e == NE - 1:
                        store_group(g, m)

                NB = NE * NG
                weights(0)
                for i in range(NB + 1):
                    if i % NG == 2 and i // NG + 1 < NE:
                        weights(i // NG + 1)
                    interleave(*([(hidden(i), 1)] if i < NB else []), *([(output(i - 1), 1)] if i else []))

        stored = []
        out_v = out.rearrange("b (t p) d -> p (b t) d", p=P)

        def store_group(g, ready):
            sp.wait(ready)
            stored.append(sp.do(lambda e: e.dma_start(out_v[:, g * GT:(g + 1) * GT, :],
                                                      x_sb[:, g * GT:(g + 1) * GT, :]), sem(f"x_io{g}"), 16))

        xr = attention(0, A["L0_xattn_Wq"], A["L0_xattn_Wk"], A["L0_xattn_Wv"], A["L0_xattn_Wo"], A["L0_xattn_bq"],
                       A["L0_xattn_bk"], A["L0_xattn_bv"], A["L0_xattn_bo"], x_ready)
        experts_swiglu(xr)
        xr = attention(1, A["L1_WqT"], A["L1_WkT"], A["L1_WvT"], A["L1_WoT"], None, None, None, None,
                       [[] for _ in range(NG)])
        experts_relu(xr)
        sp.wait(*stored)

        block = ctx.enter_context(nc.Block())

        @block.sync
        def _(eng):
            sp.play(eng)

        @block.gpsimd
        def _(eng):
            pool.play(eng)

        @block.scalar
        def _(eng):
            act.play(eng)

        @block.vector
        def _(eng):
            dve.play(eng)

        @block.tensor
        def _(eng):
            pe.play(eng)


_DIRECT = ["x", "ctx_512", "L0_xattn_Wq", "L0_xattn_bq", "L0_xattn_Wk", "L0_xattn_bk", "L0_xattn_Wv", "L0_xattn_bv",
           "L0_xattn_Wo", "L0_xattn_bo", "L0_ffn_wg", "L0_ffn_w1", "L0_ffn_w3", "L0_ffn_w2", "L1_ffn_router_W",
           "L1_ffn_router_b", "L1_ffn_sW1", "L1_ffn_sb1", "L1_ffn_sW2", "L1_ffn_sb2", "L1_ffn_eW1", "L1_ffn_eW2",
           "L1_ffn_eb2"]


def kernel(**inputs):
    import numpy as np
    import concourse.bacc as bacc
    from concourse.bass_utils import run_bass_kernel_spmd

    laid = {name: np.asarray(inputs[name]) for name in _DIRECT}
    laid["L1_WqT"] = np.asarray(inputs["L1_xattn_Wq"]).T
    laid["L1_WkT"] = np.asarray(inputs["L1_xattn_Wkv"])[:D].T
    laid["L1_WvT"] = np.asarray(inputs["L1_xattn_Wkv"])[D:].T
    laid["L1_WoT"] = np.asarray(inputs["L1_xattn_Wo"]).T
    laid["L1_ffn_eb1"] = np.asarray(inputs["L1_ffn_eb1"]).reshape(E1, HID1 // P, P).transpose(2, 0, 1)

    for name in ("L0_xattn_bq", "L0_xattn_bk", "L1_ffn_sb1"):
        laid[name] = np.asarray(inputs[name]).reshape(-1, P).T

    nc = bacc.Bacc("TRN2", target_bir_lowering=False, num_devices=1)
    arrays, aps = {}, {}
    for name, a in laid.items():
        arrays[f"in_{name}"] = np.ascontiguousarray(a)
        aps[name] = nc.dram_tensor(f"in_{name}", a.shape, mybir.dt.from_np(a.dtype), kind="ExternalInput").ap()
    out = nc.dram_tensor("out_x", (BATCH, SEQ, D), F32, kind="ExternalOutput").ap()
    build(nc, aps, out)
    r = run_bass_kernel_spmd(nc, [arrays], core_ids=[0])
    return r.results[0]["out_x"]
```

```python
from contextlib import ExitStack

import concourse.bass as bass
from concourse import mybir

ALU = mybir.AluOpType
ACT = mybir.ActivationFunctionType
F32 = mybir.dt.float32
F32R = mybir.dt.float32r
I32 = mybir.dt.int32
BF16 = mybir.dt.bfloat16
AX_X = mybir.AxisListType.X

P = 128
BATCH, SEQ, D = 4, 1024, 256
TOK = BATCH * SEQ
NT = TOK // P
GT = 4
GN = GT * P
NG = TOK // GN
DC = D // P
KV, CTX = 77, 128
H, DH = 16, 16
HC = H // DC
EPS = 1e-5
E0, CAP, HID0 = 8, 1024, 512
E1, TOP, HID1 = 15, 3, 256
BANK = 512


class Sem:

    def __init__(self, handle):
        self.handle, self.value = handle, 0

    def mark(self, by):
        self.value += by
        return (self, self.value)


class Lane:

    def __init__(self):
        self.steps, self.seen = [], {}

    def wait(self, *marks):
        for m in marks:
            if m is not None and self.seen.get(m[0], 0) < m[1]:
                self.seen[m[0]] = m[1]
                self.steps.append(lambda eng, m=m: eng.wait_ge(m[0].handle, m[1]))

    def do(self, call, sem=None, by=1):
        if sem is None:
            self.steps.append(call)
            return None
        self.steps.append(lambda eng: call(eng).then_inc(sem.handle, by))
        return sem.mark(by)

    def play(self, eng):
        for s in self.steps:
            s(eng)


class Banks:

    def __init__(self, tensors):
        self.tensors, self.free, self.n = tensors, [None] * len(tensors), 0

    def take(self):
        i = self.n % len(self.tensors)
        self.n += 1
        return i, self.tensors[i], self.free[i]

    def release(self, i, mark):
        self.free[i] = mark


def interleave(*streams):
    live = [[g, n] for g, n in streams]
    while live:
        for item in list(live):
            for _ in range(item[1]):
                try:
                    next(item[0])
                except StopIteration:
                    live.remove(item)
                    break


def f(ap):
    return ap.bitcast(F32)


def build(nc, A, out):
    pe, act, dve, pool, sp = (Lane() for _ in range(5))
    ctx = ExitStack()
    names = {}

    def sem(name):
        if name not in names:
            names[name] = Sem(ctx.enter_context(nc.semaphore("s_" + name)))
        return names[name]

    def sb(stack, name, shape, dt=F32):
        return stack.enter_context(nc.sbuf_tensor(name, shape, dt))

    with ctx:
        bank = [ctx.enter_context(nc.psum_tensor(f"bank{i}", [P, BANK], F32)) for i in range(8)]
        x_sb = sb(ctx, "x_sb", [P, NT, D])
        ident = sb(ctx, "ident", [P, P])
        neg_half = sb(ctx, "neg_half", [P, GT])
        phase_end = sem("phase_end")
        xn_d = nc.dram_tensor("xn_scratch", (TOK, D), F32, kind="Internal").ap()
        acc_d = nc.dram_tensor("acc_scratch", (TOK, D), F32, kind="Internal").ap()

        s_const = sem("const")
        zero = pool.do(lambda e: e.memset(ident[:, :], 0.0), s_const)
        pool.wait(zero)
        pool.do(lambda e: e.affine_select(out=ident[:, :], in_=ident[:, :], compare_op=ALU.not_equal, fill=1.0,
                                          base=0, pattern=[[-1, P]], channel_multiplier=1), s_const)
        const_done = pool.do(lambda e: e.memset(neg_half[:, :], -0.5), s_const)

        x_in = A["x"].rearrange("b (t p) d -> p (b t) d", p=P)
        x_ready = []
        for g in range(NG):
            x_ready.append([sp.do(lambda e, g=g: e.dma_start(x_sb[:, g * GT:(g + 1) * GT, :],
                                                             x_in[:, g * GT:(g + 1) * GT, :]), sem(f"x_io{g}"), 16)])

        def rows(d):
            return d.rearrange("(t p) d -> p t d", p=P)

        def end_phase():
            for lane in (pe, act, dve, pool, sp):
                lane.do(lambda e: e.drain(), phase_end)
            for lane in (pe, act, dve, pool, sp):
                lane.wait((phase_end, phase_end.value))

        def split_weights(stack, name, source, shape, stage, arrived):
            hi, lo = sb(stack, name + "_hi", shape, F32R), sb(stack, name + "_lo", shape, F32R)
            pool.wait(arrived)
            m = pool.do(lambda e: e.tensor_copy(hi[:], stage), sem("weights"))
            pool.wait(m)
            m = pool.do(lambda e: e.tensor_tensor(lo[:], stage, f(hi[:]), ALU.subtract), sem("weights"))
            return hi, lo, m

        def matmul3(o, w_hi, w_lo, x_hi, x_lo, first, last, done=None):
            pe.do(lambda e: e.matmul(o, w_hi, x_hi, start=first, stop=False))
            pe.do(lambda e: e.matmul(o, w_lo, x_hi, start=False, stop=False))
            return pe.do(lambda e: e.matmul(o, w_hi, x_lo, start=False, stop=last), done)

        def layernorm(g, tmp, xn, ready, free):
            b = g % 2
            stats, mv, rstd = tmp
            dve.wait(*ready)
            for j in range(GT):
                m = dve.do(lambda e, j=j: e.bn_stats(stats[:, b, j, :], x_sb[:, g * GT + j, :]), sem("ln_stats"))
            dve.wait(m)
            for j in range(GT):
                m = dve.do(lambda e, j=j: e.bn_aggr(mv[:, b, j, :], stats[:, b, j, :]), sem("ln_stats"))
            dve.wait(m)
            m = dve.do(lambda e: e.tensor_scalar(rstd[:, b, 0, :], mv[:, b, :, 1], EPS, None, ALU.add), sem("ln_var"))
            pool.wait(m, const_done)
            m = pool.do(lambda e: e.tensor_tensor(rstd[:, b, 1, :], rstd[:, b, 0, :], neg_half[:, :], ALU.pow),
                        sem("ln_rstd"))
            dve.wait(m, *free)
            for j in range(GT):
                m = dve.do(lambda e, j=j: e.tensor_scalar(xn[:, j, :], x_sb[:, g * GT + j, :], mv[:, b, j, 0:1],
                                                          rstd[:, b, 1, j:j + 1], ALU.subtract, ALU.mult),
                           sem("ln_out"))
            return m

        def transpose_split(banks, src, src_ready, hi, lo, free, what):
            marks = []
            for c in range(DC):
                i, w, bank_free = banks.take()
                pe.wait(bank_free, src_ready, const_done)
                for j in range(GT):
                    m = pe.do(lambda e, w=w, c=c, j=j: e.transpose(w[:, j * P:(j + 1) * P],
                                                                   src[:, j, c * P:(c + 1) * P], ident[:, :]),
                              sem(what + "_T") if j == GT - 1 else None)
                act.wait(m, *free)
                m = act.do(lambda e, w=w, c=c: e.activation(hi[:, c, :], w[:, :], ACT.Copy), sem(what + "_hi"))
                dve.wait(m, *free)
                m = dve.do(lambda e, w=w, c=c: e.tensor_tensor(lo[:, c, :], w[:, :], f(hi[:, c, :]), ALU.subtract),
                           sem(what + "_lo"))
                banks.release(i, m)
                marks.append(m)
                yield
            return marks[-1]

        def attention(L, wq_d, wk_d, wv_d, wo_d, bq_d, bk_d, bv_d, bo_d, xr):
            st = ExitStack()
            with st:
                work = Banks([bank[i] for i in range(4)])
                smax = Banks([bank[i] for i in range(4, 6)])
                sexp = Banks([bank[i] for i in range(6, 8)])
                n = f"a{L}_"
                ln_tmp = (sb(st, n + "stats", [P, 2, GT, 6]), sb(st, n + "mv", [P, 2, GT, 2]),
                          sb(st, n + "rstd", [P, 2, 2, GT]))
                kaug = sb(st, n + "kaug", [P, H, BATCH, KV], F32R)
                kblk = sb(st, n + "kblk", [P, DC, BATCH, HC, KV], F32R)
                vaug = sb(st, n + "vaug", [KV, BATCH, H, DH + 1])
                qb = sb(st, n + "qb", [P, 4 * DC])
                wq_hi, wq_lo = sb(st, n + "wq_hi", [P, DC, D], F32R), sb(st, n + "wq_lo", [P, DC, D], F32R)
                wo_hi, wo_lo = sb(st, n + "wo_hi", [P, DC, D], F32R), sb(st, n + "wo_lo", [P, DC, D], F32R)

                with ExitStack() as s2:
                    stage = sb(s2, n + "stage", [P, 2 * DC, D])
                    wk = sb(s2, n + "wk", [P, D])
                    wv = sb(s2, n + "wv", [P, D])
                    ctx_sb = sb(s2, n + "ctx", [KV, BATCH, CTX])
                    ctxT = sb(s2, n + "ctxT", [P, BATCH, KV])
                    k_hi = sb(s2, n + "k_hi", [P, DC, BATCH * KV], F32R)
                    k_lo = sb(s2, n + "k_lo", [P, DC, BATCH * KV], F32R)
                    pair = sb(s2, n + "pair", [P, 2])
                    head = sb(s2, n + "head", [P, HC])
                    bvb = sb(s2, n + "bvb", [KV, D])

                    def load(dst, src, name):
                        return sp.do(lambda e: e.dma_start(dst, src), sem("attn_in_" + name), 16)

                    ctx_in = load(ctx_sb[:], A["ctx_512"].rearrange("b s c -> s b c"), "ctx")
                    wk_in = load(wk[:], wk_d, "wk")
                    wv_in = load(wv[:], wv_d, "wv")
                    wq_in = load(stage[:, 0:DC, :], wq_d.rearrange("(c p) n -> p c n", p=P), "wq")
                    wo_in = load(stage[:, DC:2 * DC, :], wo_d.rearrange("(c p) n -> p c n", p=P), "wo")
                    if bq_d is not None:
                        bq_in = load(qb[:, 0:DC], bq_d, "bq")
                        bk_in = load(qb[:, DC:2 * DC], bk_d, "bk")
                        bv_in = load(bvb[:], bv_d.rearrange("(a n) -> a n", a=1).broadcast_to([KV, D]), "bv")
                    else:
                        bq_in = bk_in = dve.do(lambda e: e.memset(qb[:], 0.0), sem("attn_bias"))
                        bv_in = dve.do(lambda e: e.memset(bvb[:], 0.0), sem("attn_bias"))

                    pool.do(lambda e: e.memset(pair[:], 1.0), sem("attn_mask"))
                    m = pool.do(lambda e: e.memset(head[:], 1.0), sem("attn_mask"))
                    pool.wait(m)
                    m = pool.do(lambda e: e.affine_select(out=head[:], in_=head[:], compare_op=ALU.is_ge, fill=0.0,
                                                          base=0, pattern=[[-DH, HC]], channel_multiplier=1),
                                sem("attn_mask"))
                    pool.wait(m)
                    m = pool.do(lambda e: e.affine_select(out=head[:], in_=head[:], compare_op=ALU.is_ge, fill=0.0,
                                                          base=DH - 1, pattern=[[DH, HC]], channel_multiplier=-1),
                                sem("attn_mask"))
                    dve.wait(m)
                    m = dve.do(lambda e: e.tensor_reduce(pair[:], head[:].rearrange("p (a i) -> p i a", i=2),
                                                         AX_X, ALU.add), sem("attn_mask2"))
                    mask_done = m

                    for part, (hi, lo), arrived in ((0, (wq_hi, wq_lo), wq_in), (1, (wo_hi, wo_lo), wo_in)):
                        src = stage[:, part * DC:(part + 1) * DC, :]
                        pool.wait(arrived)
                        m = pool.do(lambda e, hi=hi, src=src: e.tensor_copy(hi[:], src), sem("attn_w"))
                        pool.wait(m)
                        w_done = pool.do(lambda e, hi=hi, lo=lo, src=src: e.tensor_tensor(lo[:], src, f(hi[:]),
                                                                                         ALU.subtract), sem("attn_w"))

                    i, w, bf = work.take()
                    pe.wait(bf, ctx_in, const_done)
                    for b in range(BATCH):
                        m = pe.do(lambda e, b=b, w=w: e.transpose(w[:, b * KV:(b + 1) * KV], ctx_sb[:, b, :],
                                                                  ident[0:KV, 0:KV]), sem("attn_ctxT_p"))
                    act.wait(m)
                    ctxT_done = act.do(lambda e, w=w: e.activation(ctxT[:].rearrange("p b s -> p (b s)"),
                                                                   w[:, 0:BATCH * KV], ACT.Copy), sem("attn_ctxT"))
                    work.release(i, ctxT_done)

                    k_done = []
                    for m_ in range(DC):
                        i, w, bf = work.take()
                        pe.wait(bf, wk_in, ctxT_done)
                        m = pe.do(lambda e, w=w, m_=m_: e.matmul(w[:, 0:BATCH * KV], wk[:, m_ * P:(m_ + 1) * P],
                                                                ctxT[:].rearrange("p b s -> p (b s)"),
                                                                start=True, stop=True), sem("attn_k_p"))
                        act.wait(m, bk_in)
                        m = act.do(lambda e, w=w, m_=m_: e.activation(k_hi[:, m_, :], w[:, 0:BATCH * KV], ACT.Identity,
                                                                     bias=qb[:, DC + m_:DC + m_ + 1]), sem("attn_k_hi"))
                        dve.wait(m, bk_in)
                        m = dve.do(lambda e, w=w, m_=m_: e.scalar_tensor_tensor(
                            out=k_lo[:, m_, :], in0=w[:, 0:BATCH * KV], scalar=qb[:, DC + m_:DC + m_ + 1],
                            in1=f(k_hi[:, m_, :]), op0=ALU.add, op1=ALU.subtract), sem("attn_k_lo"))
                        work.release(i, m)
                        k_done.append(m)

                    dve.wait(k_done[-1], mask_done)
                    for m_ in range(DC):
                        for r in range(4):
                            q = slice(32 * r, 32 * r + 32)
                            h0 = m_ * HC + 2 * r
                            for rows, src in ((0, k_hi), (32, k_lo), (64, k_hi)):
                                kaug_done = dve.do(lambda e, q=q, h0=h0, rows=rows, src=src, m_=m_: e.tensor_tensor(
                                    kaug[rows:rows + 32, h0:h0 + 2, :, :].rearrange("p h b s -> p h (b s)"),
                                    f(src[q, m_, :]).rearrange("p (o s) -> p o s", o=1).broadcast_to([32, 2, BATCH * KV]),
                                    pair[q, :].rearrange("p (h o) -> p h o", o=1).broadcast_to([32, 2, BATCH * KV]),
                                    ALU.mult), sem("attn_kaug"))
                    kaug_done = dve.do(lambda e: e.tensor_copy(
                        kaug[96:96 + H, :, :, :].rearrange("p h b s -> p h (b s)"),
                        ident[96:96 + H, 96:96 + H].rearrange("p (h o) -> p h o", o=1).broadcast_to([H, H, BATCH * KV])),
                        sem("attn_kaug"))
                    for m_ in range(DC):
                        for b in range(BATCH):
                            kblk_done = dve.do(lambda e, m_=m_, b=b: e.tensor_tensor(
                                kblk[:, m_, b, :, :],
                                f(k_hi[:, m_, b * KV:(b + 1) * KV]).rearrange("p (o s) -> p o s", o=1)
                                .broadcast_to([P, HC, KV]),
                                head[:].rearrange("p (h o) -> p h o", o=1).broadcast_to([P, HC, KV]),
                                ALU.mult), sem("attn_kblk"))

                    ones = pool.do(lambda e: e.memset(vaug[:, :, :, DH:DH + 1], 1.0), sem("attn_ones"))
                    for b in range(BATCH):
                        i, w, bf = work.take()
                        pe.wait(bf, wv_in, ctxT_done)
                        m = pe.do(lambda e, w=w, b=b: e.matmul(w[0:KV, 0:D], ctxT[:, b, :], wv[:, :],
                                                              start=True, stop=True), sem("attn_v_p"))
                        dve.wait(m, bv_in)
                        v_done = dve.do(lambda e, w=w, b=b: e.tensor_tensor(
                            vaug[:, b, :, 0:DH], w[0:KV, 0:D].rearrange("s (h d) -> s h d", h=H),
                            bvb[:].rearrange("s (h d) -> s h d", h=H), ALU.add), sem("attn_v"))
                        work.release(i, v_done)
                    end_phase()

                xn = sb(st, n + "xn", [P, GT, D])
                xT = sb(st, n + "xT_hi", [P, DC, GN], F32R), sb(st, n + "xT_lo", [P, DC, GN], F32R)
                q_hi, q_lo = sb(st, n + "q_hi", [P, DC, GN], F32R), sb(st, n + "q_lo", [P, DC, GN], F32R)
                qaug = [sb(st, n + f"qaug{i}", [P, DC, 4, GN], F32R) for i in range(2)]
                nmax = sb(st, n + "nmax", [P, GT, H])
                nmaxT = sb(st, n + "nmaxT", [H, GN], F32R)
                prob = sb(st, n + "prob", [KV, H, GN])
                rden = sb(st, n + "rden", [P, 2, H])
                o_sb = sb(st, n + "o", [P, GT, D])
                oT = sb(st, n + "oT_hi", [P, DC, GN], F32R), sb(st, n + "oT_lo", [P, DC, GN], F32R)
                bob = None
                if bo_d is not None:
                    bob = sb(st, n + "bob", [P, D])
                    bo_in = sp.do(lambda e: e.dma_start(bob[:], bo_d.rearrange("(a n) -> a n", a=1)
                                                        .broadcast_to([P, D])), sem("attn_bo"), 16)

                M = {}

                def mark(what, g):
                    return M.get((what, g))

                def front(g):
                    ln = layernorm(g, ln_tmp, xn, xr[g], [mark("xT", g - 1)])
                    yield
                    m = yield from transpose_split(work, xn, ln, xT[0], xT[1], [mark("q_p", g - 1)], "attn_x")
                    M["xT", g] = m
                    b = g * GN // SEQ
                    for m_ in range(DC):
                        i, w, bf = work.take()
                        pe.wait(bf, M["xT", g], w_done)
                        for c in range(DC):
                            ws = slice(m_ * P, (m_ + 1) * P)
                            m = matmul3(w[:, :], wq_hi[:, c, ws], wq_lo[:, c, ws], xT[0][:, c, :], xT[1][:, c, :],
                                        c == 0, c == DC - 1, sem("attn_q_p"))
                        M["q_p", g] = m
                        act.wait(m, bq_in, mark("qaug", g - 1), mark("max_p", g - 1))
                        m = act.do(lambda e, w=w, m_=m_: e.activation(q_hi[:, m_, :], w[:, :], ACT.Identity,
                                                                     bias=qb[:, m_:m_ + 1]), sem("attn_q_hi"))
                        dve.wait(m, bq_in, mark("qaug", g - 1))
                        m = dve.do(lambda e, w=w, m_=m_: e.scalar_tensor_tensor(
                            out=q_lo[:, m_, :], in0=w[:, :], scalar=qb[:, m_:m_ + 1], in1=f(q_hi[:, m_, :]),
                            op0=ALU.add, op1=ALU.subtract), sem("attn_q_lo"))
                        work.release(i, m)
                        M["q", g] = m
                        yield
                    dst = qaug[g % 2]
                    sp.wait(M["q", g], mark("s_p", g - 2))
                    s_q = sem(f"attn_qaug{g % 2}")
                    for r in range(4):
                        for rows, src in ((0, q_hi), (32, q_hi), (64, q_lo)):
                            sp.do(lambda e, dst=dst, r=r, rows=rows, src=src: e.dma_start(
                                f(dst[rows:rows + 32, :, r, :]), f(src[32 * r:32 * r + 32, :, :])), s_q, 16)
                    for j in range(GT):
                        for m_ in range(DC):
                            for half in range(2):
                                i, w, bf = smax.take()
                                pe.wait(bf, M["q", g], kblk_done)
                                hs = slice(half * HC // 2, (half + 1) * HC // 2)
                                m = pe.do(lambda e, w=w, j=j, m_=m_, hs=hs: e.matmul(
                                    w[:, 0:HC // 2 * KV], q_hi[:, m_, j * P:(j + 1) * P],
                                    kblk[:, m_, b, hs, :].rearrange("p h s -> p (h s)"), start=True, stop=True),
                                    sem("attn_max_p"))
                                M["max_p", g] = m
                                h0 = m_ * HC + half * HC // 2
                                dve.wait(m, mark("nmaxT_p", g - 1))
                                m = dve.do(lambda e, w=w, j=j, h0=h0: e.tensor_reduce(
                                    nmax[:, j, h0:h0 + HC // 2],
                                    w[:, 0:HC // 2 * KV].rearrange("p (h s) -> p h s", s=KV), AX_X, ALU.max,
                                    negate=True), sem("attn_nmax"))
                                smax.release(i, m)
                            yield
                    i, w, bf = work.take()
                    pe.wait(bf, m)
                    for j in range(GT):
                        m = pe.do(lambda e, w=w, j=j: e.transpose(w[0:H, j * P:(j + 1) * P], nmax[:, j, :],
                                                                 ident[:, :]), sem("attn_nmaxT_p"))
                    M["nmaxT_p", g] = m
                    dve.wait(m, mark("qaug", g - 1))
                    m = dve.do(lambda e, w=w: e.tensor_copy(nmaxT[:, :], w[0:H, :]), sem("attn_nmaxT"))
                    work.release(i, m)
                    sp.wait(m)
                    M["qaug", g] = sp.do(lambda e, dst=dst: e.dma_start(
                        f(dst[96:96 + H, :, :, :]).rearrange("p m r t -> p (m r) t"),
                        f(nmaxT[:, :]).rearrange("p (o t) -> p o t", o=1).broadcast_to([H, 4 * DC, GN])), s_q, 16)
                    yield

                def scores(g):
                    b = g * GN // SEQ
                    for h in range(H):
                        i, w, bf = sexp.take()
                        pe.wait(bf, M["qaug", g], kaug_done)
                        m = pe.do(lambda e, w=w, h=h: e.matmul(w[0:KV, :], kaug[0:96 + H, h, b, :],
                                                              qaug[g % 2][0:96 + H, h // HC, h % HC // 2, :],
                                                              start=True, stop=True), sem("attn_s_p"))
                        M["s_p", g] = m
                        act.wait(m, mark("pv_p", g - 1))
                        m = act.do(lambda e, w=w, h=h: e.activation(prob[:, h, :], w[0:KV, :], ACT.Exp,
                                                                   scale=float(DH) ** -0.5), sem("attn_prob"))
                        sexp.release(i, m)
                        M["prob", g] = m
                        yield

                def back(g):
                    b = g * GN // SEQ
                    for j in range(GT):
                        i, w, bf = work.take()
                        pe.wait(bf, M["prob", g], v_done, ones)
                        for h in range(H):
                            m = pe.do(lambda e, w=w, j=j, h=h: e.matmul(
                                w[:, h * (DH + 1):(h + 1) * (DH + 1)], prob[:, h, j * P:(j + 1) * P],
                                vaug[:, b, h, :], start=True, stop=True), sem("attn_pv_p") if h == H - 1 else None)
                        M["pv_p", g] = m
                        o = w[:, 0:H * (DH + 1)].rearrange("p (h d) -> p h d", d=DH + 1)
                        dve.wait(m)
                        m = dve.do(lambda e, o=o, j=j: e.reciprocal(
                            rden[:, j % 2, :].rearrange("p (h o) -> p h o", o=1), o[:, :, DH:DH + 1]),
                            sem("attn_rden"))
                        dve.wait(m, mark("oT_p", g - 1))
                        m = dve.do(lambda e, o=o, j=j: e.tensor_tensor(
                            o_sb[:, j, :].rearrange("p (h d) -> p h d", d=DH), o[:, :, 0:DH],
                            rden[:, j % 2, :].rearrange("p (h o) -> p h o", o=1).broadcast_to([P, H, DH]),
                            ALU.mult), sem("attn_o"))
                        work.release(i, m)
                        M["o", g] = m
                        yield
                    m = yield from transpose_split(work, o_sb, M["o", g], oT[0], oT[1], [mark("y_p", g - 1)], "attn_o")
                    M["oT_p", g] = m
                    for j in range(GT):
                        i, w, bf = work.take()
                        pe.wait(bf, M["oT_p", g], w_done)
                        ts = slice(j * P, (j + 1) * P)
                        for c in range(DC):
                            m = matmul3(w[:, 0:D], oT[0][:, c, ts], oT[1][:, c, ts], wo_hi[:, c, :], wo_lo[:, c, :],
                                        c == 0, c == DC - 1, sem("attn_y_p"))
                        M["y_p", g] = m
                        xt = x_sb[:, g * GT + j, :]
                        dve.wait(m)
                        m = dve.do(lambda e, w=w, xt=xt: e.tensor_tensor(xt, w[:, 0:D], xt, ALU.add), sem("attn_x"))
                        work.release(i, m)
                        if bob is not None:
                            pool.wait(m, bo_in)
                            m = pool.do(lambda e, xt=xt: e.tensor_tensor(xt, xt, bob[:], ALU.add), sem("attn_xb"))
                        M["x", g] = m
                        yield

                interleave((front(0), 1))
                for g in range(NG + 1):
                    streams = []
                    if g < NG:
                        streams.append((scores(g), 1))
                    if g > 0:
                        streams.insert(0, (back(g - 1), 1))
                    if g + 1 < NG:
                        streams.append((front(g + 1), 1))
                    if g > 0 and g < NG:
                        bk = back(g - 1)
                        for _ in range(GT):
                            next(bk)
                        streams[0] = (bk, 1)
                    interleave(*streams)
                end_phase()
            return [[M["x", g]] for g in range(NG)]

        def experts_swiglu(xr):
            st = ExitStack()
            with st:
                n = "e0_"
                score = sb(st, n + "score", [P, NT, E0])
                slot = sb(st, n + "slot", [P, NT, E0])
                acc_in = []
                with ExitStack() as s2:
                    work = Banks([bank[i] for i in range(3)])
                    xn = sb(s2, n + "xn", [P, NT, D])
                    ln_tmp = (sb(s2, n + "stats", [P, 2, GT, 6]), sb(s2, n + "mv", [P, 2, GT, 2]),
                              sb(s2, n + "rstd", [P, 2, 2, GT]))
                    xT = [sb(s2, n + f"xT{i}", [P, DC, GN]) for i in range(2)]
                    wg = sb(s2, n + "wg", [P, DC, E0])
                    lg = sb(s2, n + "lg", [P, NT, E0])
                    pr = sb(s2, n + "pr", [P, NT, E0])
                    red = sb(s2, n + "red", [P, 3, NT])
                    s_gate = sem(n + "gate")
                    wg_in = sp.do(lambda e: e.dma_start(wg[:], A["L0_ffn_wg"].rearrange("(c p) n -> p c n", p=P)),
                                  sem(n + "wg"), 16)
                    logits = bank[7]
                    xT_used = [None, None]
                    for g in range(NG):
                        ts = slice(g * GT, (g + 1) * GT)
                        sp.wait(*xr[g])
                        acc_in.append(sp.do(lambda e, ts=ts: e.dma_start(rows(acc_d)[:, ts, :], x_sb[:, ts, :]),
                                            sem(f"x_io{g}"), 16))
                        ln = layernorm(g, ln_tmp, xn[:, ts, :], xr[g], [])
                        sp.wait(ln)
                        xn_out = sp.do(lambda e, ts=ts: e.dma_start(rows(xn_d)[:, ts, :], xn[:, ts, :]),
                                       sem("xn_out"), 16)
                        for c in range(DC):
                            i, w, bf = work.take()
                            pe.wait(bf, ln)
                            for j in range(GT):
                                m = pe.do(lambda e, w=w, g=g, c=c, j=j: e.transpose(
                                    w[:, j * P:(j + 1) * P], xn[:, g * GT + j, c * P:(c + 1) * P], ident[:, :]),
                                    sem(n + "xT_p") if j == GT - 1 else None)
                            act.wait(m, xT_used[g % 2])
                            m = act.do(lambda e, w=w, g=g, c=c: e.activation(xT[g % 2][:, c, :], w[:, :], ACT.Copy),
                                       sem(n + "xT"))
                            work.release(i, m)
                        pe.wait(m, wg_in)
                        for j in range(GT):
                            t = g * GT + j
                            for c in range(DC):
                                m = pe.do(lambda e, g=g, c=c, j=j, t=t: e.matmul(
                                    logits[:, t * E0:(t + 1) * E0], xT[g % 2][:, c, j * P:(j + 1) * P], wg[:, c, :],
                                    start=(c == 0), stop=(c == DC - 1)), sem(n + "logits"))
                        xT_used[g % 2] = m

                    def bc(k):
                        return red[:, k, :].rearrange("p (t o) -> p t o", o=1).broadcast_to([P, NT, E0])

                    lgv = logits[:, 0:NT * E0].rearrange("p (t e) -> p t e", e=E0)
                    dve.wait(m)
                    m = dve.do(lambda e: e.tensor_reduce(red[:, 0, :], lgv, AX_X, ALU.max), s_gate)
                    dve.wait(m)
                    m = dve.do(lambda e: e.tensor_tensor(lg[:], lgv, bc(0), ALU.subtract), s_gate)
                    act.wait(m)
                    m = act.do(lambda e: e.activation(lg[:], lg[:], ACT.Exp), sem(n + "exp"))
                    dve.wait(m)
                    m = dve.do(lambda e: e.tensor_reduce(red[:, 1, :], lg[:], AX_X, ALU.add), s_gate)
                    dve.wait(m)
                    m = dve.do(lambda e: e.reciprocal(red[:, 2, :], red[:, 1, :]), s_gate)
                    dve.wait(m)
                    m = dve.do(lambda e: e.tensor_tensor(pr[:], lg[:], bc(2), ALU.mult), s_gate)
                    select_tokens(s2, n, pr, score, slot, m)
                    end_phase()

                ffn_blocks(st, n, score, slot, xn_out, acc_in)
                end_phase()

        NCH = P // E0
        CHT = NT // NCH
        CHN = CHT * P

        def select_tokens(s2, n, pr, score, slot, ready):
            s = sem(n + "sel")
            cb = Banks([bank[3], bank[4]])
            prc = sb(s2, n + "prc", [P, CHT, E0, NCH])
            prT = sb(s2, n + "prT", [P, CHN])
            junk = sb(s2, n + "junk", [P, CHN])
            cnt = sb(s2, n + "cnt", [P, 2])
            cand = sb(s2, n + "cand", [P, 2], I32)
            flip = sb(s2, n + "flip", [P, 1], I32)
            bits = sb(s2, n + "bits", [P, 31], I32)
            same = sb(s2, n + "same", [P, E0, NCH])
            before = sb(s2, n + "before", [P, E0, NCH])
            eq = sb(s2, n + "eq", [P, CHN])
            gt = sb(s2, n + "gt", [P, CHN])
            rank = sb(s2, n + "rank", [P, CHN])
            zeros = sb(s2, n + "zeros", [P, CHN])
            tot = sb(s2, n + "tot", [P, 4])

            k = sem(n + "selc")
            m = pool.do(lambda e: e.memset(same[:], 1.0), k)
            m = pool.do(lambda e: e.memset(zeros[:], 0.0), k)
            pool.wait(m)
            for sgn, base in ((1, 0), (-1, NCH - 1)):
                m = pool.do(lambda e, sgn=sgn, base=base: e.affine_select(
                    out=same[:], in_=same[:], compare_op=ALU.is_ge, fill=0.0, base=base,
                    pattern=[[-sgn * NCH, E0], [0, NCH]], channel_multiplier=sgn), k)
                pool.wait(m)
            m = pool.do(lambda e: e.affine_select(out=before[:], in_=same[:], compare_op=ALU.is_gt, fill=0.0, base=0,
                                                  pattern=[[NCH, E0], [1, NCH]], channel_multiplier=-1), k)
            for b in range(30):
                m = pool.do(lambda e, b=b: e.memset(bits[:, b:b + 1], 1 << b), k)
            consts = m
            same2, before2 = same[:].rearrange("p e c -> p (e c)"), before[:].rearrange("p e c -> p (e c)")

            dve.wait(ready)
            m = dve.do(lambda e: e.tensor_copy(prc[:].rearrange("p j e c -> p e c j"),
                                               pr[:].rearrange("p (c j) e -> p e c j", j=CHT)), s)
            pe.wait(m)
            i, w, bf = cb.take()
            for j in range(CHT):
                m = pe.do(lambda e, w=w, j=j: e.transpose(w[:, j * P:(j + 1) * P],
                                                          prc[:, j, :, :].rearrange("p e c -> p (e c)"), ident[:, :]),
                          sem(n + "selp"))
            dve.wait(m, consts)
            m = dve.do(lambda e, w=w: e.tensor_copy(prT[:], w[:, 0:CHN]), s)
            cb.release(i, m)
            dve.wait(m)
            m = dve.do(lambda e: e.tensor_copy(cand[:, 0:1], bits[:, 29:30]), s)
            for b in range(29, -1, -1):
                dve.wait(m)
                m = dve.do(lambda e: e.tensor_scalar(junk[:], prT[:], cand[:, 0:1].bitcast(F32), None, ALU.is_ge,
                                                     ALU.add, accum_out=cnt[:, 0:1]), s)
                i, w, bf = cb.take()
                pe.wait(m, bf)
                m = pe.do(lambda e, w=w: e.matmul(w[:, 0:1], same2, cnt[:, 0:1], start=True, stop=True),
                          sem(n + "selp"))
                dve.wait(m)
                m = dve.do(lambda e, w=w, b=b: e.tensor_scalar(flip[:], w[:, 0:1], float(CAP), float(1 << b),
                                                               ALU.is_lt, ALU.mult), s)
                cb.release(i, m)
                dve.wait(m)
                if b:
                    m = dve.do(lambda e, b=b: e.scalar_tensor_tensor(
                        out=cand[:, 0:1], in0=flip[:], scalar=bits[:, b - 1:b], in1=cand[:, 0:1],
                        op0=ALU.bitwise_or, op1=ALU.bitwise_xor), s)
                else:
                    m = dve.do(lambda e: e.tensor_tensor(cand[:, 0:1], flip[:], cand[:, 0:1], ALU.bitwise_xor), s)
            thr = cand[:, 0:1].bitcast(F32)
            dve.wait(m)
            dve.do(lambda e: e.tensor_scalar(gt[:], prT[:], thr, None, ALU.is_gt, ALU.add, accum_out=tot[:, 0:1]), s)
            m = dve.do(lambda e: e.tensor_scalar(eq[:], prT[:], thr, None, ALU.is_equal, ALU.add,
                                                 accum_out=tot[:, 1:2]), s)
            i, w, bf = cb.take()
            pe.wait(m, bf)
            pe.do(lambda e, w=w: e.matmul(w[:, 0:1], same2, tot[:, 0:1], start=True, stop=True))
            m1 = pe.do(lambda e, w=w: e.matmul(w[:, 1:2], before2, tot[:, 1:2], start=True, stop=True),
                       sem(n + "selp"))
            dve.wait(m)
            m = dve.do(lambda e: e.tensor_tensor_scan(rank[:], eq[:], zeros[:], 0.0, ALU.add, ALU.add), s)
            dve.wait(m1)
            m2 = dve.do(lambda e, w=w: e.tensor_copy(tot[:, 2:4], w[:, 0:2]), s)
            cb.release(i, m2)
            dve.wait(m2)
            m = dve.do(lambda e: e.tensor_tensor(tot[:, 0:1], tot[:, 2:3], tot[:, 3:4], ALU.add), s)
            dve.wait(m)
            m = dve.do(lambda e: e.tensor_scalar(rank[:], rank[:], tot[:, 0:1], float(CAP), ALU.add, ALU.is_le), s)
            dve.wait(m)
            m = dve.do(lambda e: e.tensor_tensor(eq[:], eq[:], rank[:], ALU.mult), s)
            dve.wait(m)
            m = dve.do(lambda e: e.tensor_tensor(gt[:], gt[:], eq[:], ALU.add), s)
            dve.wait(m)
            m = dve.do(lambda e: e.tensor_tensor_scan(rank[:], gt[:], zeros[:], 0.0, ALU.add, ALU.add), s)
            pe.wait(m)
            i, w, bf = cb.take()
            pe.wait(bf)
            m1 = pe.do(lambda e, w=w: e.matmul(w[:, 0:1], before2, rank[:, CHN - 1:CHN], start=True, stop=True),
                       sem(n + "selp"))
            m = dve.do(lambda e: e.tensor_tensor(prT[:], prT[:], gt[:], ALU.mult), s)
            dve.wait(m1)
            m2 = dve.do(lambda e, w=w: e.tensor_copy(tot[:, 0:1], w[:, 0:1]), s)
            cb.release(i, m2)
            dve.wait(m2)
            m2 = dve.do(lambda e: e.scalar_tensor_tensor(out=rank[:], in0=rank[:], scalar=tot[:, 0:1], in1=gt[:],
                                                         op0=ALU.add, op1=ALU.mult), s)
            for src, dst, off, done in ((prT, score, 0.0, m), (rank, slot, -1.0, m2)):
                i, w, bf = cb.take()
                pe.wait(bf, done)
                for j in range(CHT):
                    m = pe.do(lambda e, w=w, j=j, src=src: e.transpose(w[:, j * P:(j + 1) * P],
                                                                       src[:, j * P:(j + 1) * P], ident[:, :]),
                              sem(n + "selp"))
                dve.wait(m)
                m = dve.do(lambda e, w=w, dst=dst, off=off: e.tensor_scalar(
                    dst[:].rearrange("p (c j) e -> p j e c", j=CHT),
                    w[:, 0:CHN].rearrange("p (j e c) -> p j e c", j=CHT, e=E0), off, None, ALU.add), s)
                cb.release(i, m)

        def ffn_blocks(st, n, score, slot, xn_out, acc_in):
            tb, ab, yb, lb = Banks(bank[0:2]), Banks(bank[2:5]), Banks(bank[5:7]), Banks(bank[7:8])
            HCH = HID0 // P
            ST = CAP // P
            NBE = ST // GT
            NB = E0 * NBE
            LT = 8
            xg = [sb(st, n + f"xg{i}", [P, GT, D]) for i in range(3)]
            xs = sb(st, n + "xs", [P, GT, D])
            xT = [(sb(st, n + f"xs_hi{i}", [P, DC, GN], F32R), sb(st, n + f"xs_lo{i}", [P, DC, GN], F32R))
                  for i in range(2)]
            hT = [(sb(st, n + f"h_hi{i}", [P, HCH, GN], F32R), sb(st, n + f"h_lo{i}", [P, HCH, GN], F32R))
                  for i in range(2)]
            silu = [sb(st, n + f"silu{i}", [P, GN]) for i in range(2)]
            h32 = [sb(st, n + f"h32_{i}", [P, GN]) for i in range(2)]
            y_sb = [sb(st, n + f"y{i}", [P, GT, D]) for i in range(2)]
            cols = (DC * HID0, DC * HID0, HCH * D)
            stage = sb(st, n + "stage", [P, sum(cols)])
            wts = [(sb(st, n + f"w_hi{i}", [P, sum(cols)], F32R), sb(st, n + f"w_lo{i}", [P, sum(cols)], F32R))
                   for i in range(2)]
            iota_row = sb(st, n + "iota_row", [P, P])
            tok_id = sb(st, n + "tok_id", [P, NT])
            slot_i = sb(st, n + "slot_i", [P, NT, E0], I32)
            slot_col = sb(st, n + "slot_col", [P, NT, E0], I32)
            slot_row = sb(st, n + "slot_row", [P, NT, E0], I32)
            in_col = sb(st, n + "in_col", [P, NT, ST])
            score_hi = sb(st, n + "score_hi", [P, NT], F32R)
            score_lo = sb(st, n + "score_lo", [P, NT])
            payload = sb(st, n + "payload", [P, NT, 3, ST], F32R)
            in_row = [sb(st, n + f"in_row{i}", [P, LT, P], F32R) for i in range(2)]
            ids = sb(st, n + "ids", [P, E0, ST], I32)
            weight = sb(st, n + "weight", [P, E0, ST])
            M = {}

            def mark(*k):
                return M.get(k)

            s_iota = sem(n + "iota")
            pool.do(lambda q: q.iota(iota_row[:], [[1, P]], base=0, channel_multiplier=0,
                                     allow_small_or_imprecise_dtypes=True), s_iota)
            iota_done = pool.do(lambda q: q.iota(tok_id[:], [[P, NT]], base=0, channel_multiplier=1,
                                                 allow_small_or_imprecise_dtypes=True), s_iota)
            s_list = sem(n + "list")
            m = dve.do(lambda q: q.tensor_copy(slot_i[:], slot[:]), s_list)
            dve.wait(m)
            dve.do(lambda q: q.tensor_scalar(slot_row[:], slot_i[:], P - 1, None, ALU.bitwise_and), s_list)
            slots_done = dve.do(lambda q: q.tensor_scalar(slot_col[:], slot_i[:], 7, None, ALU.arith_shift_right),
                                s_list)

            def over_cols(a):
                return a.rearrange("p (t o) -> p t o", o=1).broadcast_to([P, NT, ST])

            def lists(e):
                dve.wait(slots_done, iota_done, mark("list_p", e - 1))
                m = dve.do(lambda q: q.tensor_tensor(
                    in_col[:], over_cols(slot_col[:, :, e]),
                    iota_row[:, 0:ST].rearrange("p (o a) -> p o a", o=1).broadcast_to([P, NT, ST]), ALU.is_equal),
                    s_list)
                m = dve.do(lambda q: q.tensor_copy(score_hi[:], score[:, :, e]), s_list)
                dve.wait(m)
                m = dve.do(lambda q: q.tensor_tensor(score_lo[:], score[:, :, e], f(score_hi[:]), ALU.subtract),
                           s_list)
                dve.wait(m)
                for k, v in enumerate((tok_id[:], f(score_hi[:]), score_lo[:])):
                    m = dve.do(lambda q, k=k, v=v: q.tensor_tensor(payload[:, :, k, :], in_col[:], over_cols(v),
                                                                   ALU.mult), s_list)
                yield
                il, w, bf = lb.take()
                for s0 in range(0, NT, LT):
                    b = s0 // LT % 2
                    dve.wait(mark("in_row_p", b))
                    m = dve.do(lambda q, s0=s0, b=b: q.tensor_tensor(
                        in_row[b][:], slot_row[:, s0:s0 + LT, e].rearrange("p (t o) -> p t o", o=1)
                        .broadcast_to([P, LT, P]),
                        iota_row[:].rearrange("p (o r) -> p o r", o=1).broadcast_to([P, LT, P]), ALU.is_equal),
                        s_list)
                    pe.wait(bf, m)
                    for t in range(s0, s0 + LT):
                        m = pe.do(lambda q, w=w, t=t, s0=s0, b=b: q.matmul(
                            w[:, 0:3 * ST], in_row[b][:, t - s0, :], payload[:, t, :, :].rearrange("p k a -> p (k a)"),
                            start=(t == 0), stop=(t == NT - 1)), sem(n + "list_p"))
                    M["in_row_p", b] = m
                    yield
                M["list_p", e] = m
                dve.wait(m)
                M["ids", e] = dve.do(lambda q, w=w: q.tensor_copy(ids[:, e, :], w[:, 0:ST]), s_list)
                m = dve.do(lambda q, w=w: q.tensor_copy(weight[:, e, :], w[:, ST:2 * ST]), s_list)
                dve.wait(m)
                m = dve.do(lambda q, w=w: q.tensor_tensor(weight[:, e, :], w[:, 2 * ST:3 * ST], weight[:, e, :],
                                                          ALU.add), s_list)
                M["weight", e] = m
                lb.release(il, m)
                yield

            def gather(i):
                e, half = divmod(i, NBE)
                pool.wait(xn_out, M["ids", e], mark("xs", i - 3))
                for j in range(GT):
                    a = half * GT + j
                    m = pool.do(lambda q, j=j, a=a: q.indirect_dma_start(
                        out=xg[i % 3][:, j, :], out_offset=None, in_=xn_d,
                        in_offset=bass.IndirectOffsetOnAxis(ap=ids[:, e, a:a + 1], axis=0)),
                        sem(n + f"gather{i % 3}"), 16)
                M["xg", i] = m

            def weights(e):
                at = 0
                for k, name in enumerate(("w1", "w3", "w2")):
                    src = A["L0_ffn_" + name][e].rearrange("(c p) n -> p c n", p=P)
                    dst = stage[:, at:at + cols[k]].rearrange("p (c n) -> p c n", c=src.shape[1])
                    sp.wait(mark("w", e - 1, k))
                    arrived = sp.do(lambda q, dst=dst, src=src: q.dma_start(dst, src), sem(n + "stage" + name), 16)
                    hi, lo = (t[:, at:at + cols[k]] for t in wts[e % 2])
                    raw = stage[:, at:at + cols[k]]
                    act.wait(arrived, mark("y_p", (e - 1) * NBE - 1))
                    m = act.do(lambda q, hi=hi, raw=raw: q.activation(hi, raw, ACT.Copy), sem(n + "w_hi"))
                    pool.wait(m)
                    M["w", e, k] = pool.do(lambda q, hi=hi, lo=lo, raw=raw: q.tensor_tensor(lo, raw, f(hi),
                                                                                           ALU.subtract), sem(n + "w"))
                    at += cols[k]
                    yield

            def wview(e, k, part):
                at = sum(cols[:k])
                return wts[e % 2][part][:, at:at + cols[k]].rearrange("p (c n) -> p c n", n=HID0 if k < 2 else D)

            def load(i):
                e, half = divmod(i, NBE)
                dve.wait(M["xg", i], M["weight", e], mark("xT", i - 1))
                for j in range(GT):
                    m = dve.do(lambda q, j=j: q.tensor_scalar(xs[:, j, :], xg[i % 3][:, j, :],
                                                              weight[:, e, half * GT + j:half * GT + j + 1], None,
                                                              ALU.mult), sem(n + "xs"))
                M["xs", i] = m
                m = yield from transpose_split(tb, xs, m, xT[i % 2][0], xT[i % 2][1], [mark("h_p", i - 2)], n + "x")
                M["xT", i] = m

            def hidden(i):
                e = i // NBE
                x_hi, x_lo = xT[i % 2]
                h_hi, h_lo = hT[i % 2]
                for m_ in range(HCH):
                    ia, wa, fa = ab.take()
                    ib, wb, fb = ab.take()
                    ws = slice(m_ * P, (m_ + 1) * P)
                    for k, w, bf in ((0, wa, fa), (1, wb, fb)):
                        pe.wait(bf, M["xT", i], M["w", e, k])
                        for c in range(DC):
                            m = matmul3(w[:, :], wview(e, k, 0)[:, c, ws], wview(e, k, 1)[:, c, ws], x_hi[:, c, :],
                                        x_lo[:, c, :], c == 0, c == DC - 1, sem(n + "h_p"))
                        if k == 0:
                            act.wait(m, mark("h32", i, m_ - 2) if m_ > 1 else mark("h32", i - 1, m_ + HCH - 2))
                            ms = act.do(lambda q, w=w, m_=m_: q.activation(silu[m_ % 2][:], w[:, :], ACT.Silu),
                                        sem(n + "silu"))
                            ab.release(ia, ms)
                    M["h_p", i] = m
                    dve.wait(m, ms, mark("h_hi", i, m_ - 2) if m_ > 1 else mark("h_hi", i - 1, m_ + HCH - 2))
                    m = dve.do(lambda q, w=wb, m_=m_: q.tensor_tensor(h32[m_ % 2][:], silu[m_ % 2][:], w[:, :],
                                                                     ALU.mult), sem(n + "h32"))
                    ab.release(ib, m)
                    M["h32", i, m_] = m
                    act.wait(m, mark("y_p", i - 2))
                    m = act.do(lambda q, m_=m_: q.activation(h_hi[:, m_, :], h32[m_ % 2][:], ACT.Copy),
                               sem(n + "h_hi"))
                    M["h_hi", i, m_] = m
                    dve.wait(m)
                    m = dve.do(lambda q, m_=m_: q.tensor_tensor(h_lo[:, m_, :], h32[m_ % 2][:],
                                                               f(h_hi[:, m_, :]), ALU.subtract), sem(n + "h_lo"))
                    M["h", i] = m
                    yield

            def output(i):
                e, half = divmod(i, NBE)
                h_hi, h_lo = hT[i % 2]
                for j in range(GT):
                    iy, w, bf = yb.take()
                    ts = slice(j * P, (j + 1) * P)
                    pe.wait(bf, M["h", i], M["w", e, 2])
                    for c in range(HCH):
                        m = matmul3(w[:, 0:D], h_hi[:, c, ts], h_lo[:, c, ts], wview(e, 2, 0)[:, c, :],
                                    wview(e, 2, 1)[:, c, :], c == 0, c == HCH - 1, sem(n + "y_p"))
                    M["y_p", i] = m
                    act.wait(m, mark("scatter", i - 2))
                    m = act.do(lambda q, w=w, j=j: q.activation(y_sb[i % 2][:, j, :], w[:, 0:D], ACT.Copy),
                               sem(n + "y"))
                    yb.release(iy, m)
                    M["y", i, j] = m
                    yield

            def scatter(i):
                e, half = divmod(i, NBE)
                pool.wait(*acc_in, mark("scatter", e * NBE - 1), mark("scatter", e * NBE - 2))
                for j in range(GT):
                    a = half * GT + j
                    pool.wait(M["y", i, j])
                    m = pool.do(lambda q, j=j, a=a: q.indirect_dma_start(
                        out=acc_d, out_offset=bass.IndirectOffsetOnAxis(ap=ids[:, e, a:a + 1], axis=0),
                        in_=y_sb[i % 2][:, j, :], in_offset=None, compute_op=ALU.add), sem(n + f"scatter{i % 2}"), 16)
                M["scatter", i] = m

            interleave((lists(0), 1), (weights(0), 1))
            gather(0)
            gather(1)
            interleave((load(0), 1), (lists(1), 1))
            for i in range(NB + 1):
                if i + 2 < NB:
                    gather(i + 2)
                if i > 1:
                    scatter(i - 2)
                e, half = divmod(i, NBE)
                streams = []
                if i < NB:
                    streams.append((hidden(i), 1))
                if i > 0:
                    streams.append((output(i - 1), 1))
                if i + 1 < NB:
                    streams.append((load(i + 1), 1))
                if half == 1 and e + 2 < E0:
                    streams.append((lists(e + 2), 2))
                interleave(*streams)
                if half == 0 and e + 1 < E0:
                    interleave((weights(e + 1), 1))
            scatter(NB - 1)
            for g in range(NG):
                ts = slice(g * GT, (g + 1) * GT)
                sp.wait(M["scatter", NB - 1], M["scatter", NB - 2])
                x_back.append([sp.do(lambda q, ts=ts: q.dma_start(x_sb[:, ts, :], rows(acc_d)[:, ts, :]),
                                     sem(f"x_io{g}"), 16)])

        def experts_relu(xr):
            st = ExitStack()
            with st:
                n = "e1_"
                NE = E1 + 1
                cw = sb(st, n + "cw", [P, NT, NE])
                cwT = sb(st, n + "cwT", [NE, NT, P])
                b2 = sb(st, n + "b2", [NE, D])
                b1 = sb(st, n + "b1", [P, NE, HID1 // P])
                b2_in = [sp.do(lambda e: e.dma_start(b2[0:E1, :], A["L1_ffn_eb2"]), sem(n + "b2"), 16),
                         sp.do(lambda e: e.dma_start(b2[E1:NE, :], A["L1_ffn_sb2"].rearrange("(a n) -> a n", a=1)),
                               sem(n + "b2s"), 16)]
                b1_in = [sp.do(lambda e: e.dma_start(b1[:, 0:E1, :], A["L1_ffn_eb1"]), sem(n + "b1"), 16),
                         sp.do(lambda e: e.dma_start(b1[:, E1, :], A["L1_ffn_sb1"]),
                               sem(n + "b1s"), 16)]
                xT = [(sb(st, n + f"xT_hi{g}", [P, DC, GN], F32R), sb(st, n + f"xT_lo{g}", [P, DC, GN], F32R))
                      for g in range(NG)]
                xT_done = []
                with ExitStack() as s2:
                    work = Banks([bank[i] for i in range(3)])
                    ln_tmp = (sb(s2, n + "stats", [P, 2, GT, 6]), sb(s2, n + "mv", [P, 2, GT, 2]),
                              sb(s2, n + "rstd", [P, 2, 2, GT]))
                    xn = sb(s2, n + "xn", [P, GT, D])
                    x32 = [sb(s2, n + f"x32_{i}", [P, DC, GN]) for i in range(2)]
                    rw = sb(s2, n + "rw", [P, DC, E1])
                    rb = sb(s2, n + "rb", [P, E1])
                    lg = sb(s2, n + "lg", [P, NT, E1])
                    pr = sb(s2, n + "pr", [P, NT, E1])
                    red = sb(s2, n + "red", [P, 3, NT])
                    top8 = sb(s2, n + "top8", [P, NT, 8])
                    eq = sb(s2, n + "eq", [P, NT, E1])
                    gt = sb(s2, n + "gt", [P, NT, E1])
                    rank = sb(s2, n + "rank", [P, NT * E1])
                    ngt = sb(s2, n + "ngt", [P, NT])
                    seg = sb(s2, n + "seg", [P, NT, E1])
                    rw_in = sp.do(lambda e: e.dma_start(rw[:], A["L1_ffn_router_W"].rearrange("(c p) n -> p c n", p=P)),
                                  sem(n + "rw"), 16)
                    rb_in = sp.do(lambda e: e.dma_start(rb[:], A["L1_ffn_router_b"].rearrange("(a n) -> a n", a=1)
                                                        .broadcast_to([P, E1])), sem(n + "rb"), 16)
                    logits = bank[7]
                    x32_used = [None, None]
                    xT_p = None
                    for g in range(NG):
                        ln = layernorm(g, ln_tmp, xn, xr[g], [xT_p])
                        for c in range(DC):
                            i, w, bf = work.take()
                            pe.wait(bf, ln)
                            for j in range(GT):
                                m = pe.do(lambda e, w=w, c=c, j=j: e.transpose(
                                    w[:, j * P:(j + 1) * P], xn[:, j, c * P:(c + 1) * P], ident[:, :]),
                                    sem(n + "xT_p") if j == GT - 1 else None)
                            xT_p = m
                            act.wait(m, x32_used[g % 2])
                            m = act.do(lambda e, w=w, g=g, c=c: e.activation(x32[g % 2][:, c, :], w[:, :], ACT.Copy),
                                       sem(n + "x32"))
                            work.release(i, m)
                            pool.wait(m)
                            mh = pool.do(lambda e, g=g, c=c: e.tensor_copy(xT[g][0][:, c, :], x32[g % 2][:, c, :]),
                                         sem(n + "xT_hi"))
                            dve.wait(mh)
                            ml = dve.do(lambda e, g=g, c=c: e.tensor_tensor(xT[g][1][:, c, :], x32[g % 2][:, c, :],
                                                                           f(xT[g][0][:, c, :]), ALU.subtract),
                                        sem(n + "xT_lo"))
                        xT_done.append(ml)
                        pe.wait(m, rw_in)
                        for j in range(GT):
                            t = g * GT + j
                            for c in range(DC):
                                m = pe.do(lambda e, g=g, c=c, j=j, t=t: e.matmul(
                                    logits[:, t * NE:t * NE + E1], x32[g % 2][:, c, j * P:(j + 1) * P], rw[:, c, :],
                                    start=(c == 0), stop=(c == DC - 1)), sem(n + "logits"))
                        pe.wait(ml)
                        x32_used[g % 2] = pe.do(lambda e: e.nop(), sem(n + "x32_used"))

                    s = sem(n + "route")

                    def bc(a, e=E1):
                        return a.rearrange("p (t o) -> p t o", o=1).broadcast_to([P, NT, e])

                    def step(fn, *marks):
                        dve.wait(*(marks or (last[0],)))
                        last[0] = dve.do(fn, s)

                    last = [m]
                    lgv = logits[:, :].rearrange("p (t e) -> p t e", e=NE)[:, :, 0:E1]
                    step(lambda e: e.tensor_tensor(lg[:], lgv, rb[:].rearrange("p (o e) -> p o e", o=1)
                                                   .broadcast_to([P, NT, E1]), ALU.add), m, rb_in)
                    step(lambda e: e.tensor_reduce(red[:, 0, :], lg[:], AX_X, ALU.max))
                    step(lambda e: e.tensor_tensor(lg[:], lg[:], bc(red[:, 0, :]), ALU.subtract))
                    act.wait(last[0])
                    m = act.do(lambda e: e.activation(pr[:], lg[:], ACT.Exp), sem(n + "exp"))
                    step(lambda e: e.tensor_reduce(red[:, 1, :], pr[:], AX_X, ALU.add), m)
                    step(lambda e: e.reciprocal(red[:, 2, :], red[:, 1, :]))
                    step(lambda e: e.tensor_tensor(pr[:], pr[:], bc(red[:, 2, :]), ALU.mult))
                    dve.wait(last[0])
                    for t in range(NT):
                        last[0] = dve.do(lambda e, t=t: e.max(top8[:, t, :], pr[:, t, :]), s)
                    thr = top8[:, :, TOP - 1]
                    step(lambda e: e.tensor_tensor(gt[:], pr[:], bc(thr), ALU.is_gt))
                    step(lambda e: e.tensor_tensor(eq[:], pr[:], bc(thr), ALU.is_equal))
                    step(lambda e: e.tensor_reduce(ngt[:], gt[:], AX_X, ALU.add))
                    step(lambda e: e.memset(seg[:], 1.0))
                    step(lambda e: e.memset(seg[:, :, 0:1], 0.0))
                    step(lambda e: e.tensor_tensor_scan(rank[:], seg[:].rearrange("p t e -> p (t e)"),
                                                        eq[:].rearrange("p t e -> p (t e)"), 0.0, ALU.mult, ALU.add))
                    rk = rank[:].rearrange("p (t e) -> p t e", e=E1)
                    step(lambda e: e.tensor_tensor(rk, rk, bc(ngt[:]), ALU.add))
                    step(lambda e: e.tensor_scalar(rk, rk, float(TOP), None, ALU.is_le))
                    step(lambda e: e.tensor_tensor(eq[:], eq[:], rk, ALU.mult))
                    step(lambda e: e.tensor_tensor(gt[:], gt[:], eq[:], ALU.add))
                    step(lambda e: e.tensor_tensor(cw[:, :, 0:E1], gt[:], pr[:], ALU.mult))
                    step(lambda e: e.memset(cw[:, :, E1:NE], 1.0))
                    for g in range(NG):
                        i, w, bf = work.take()
                        pe.wait(bf, last[0])
                        for j in range(GT):
                            m = pe.do(lambda e, w=w, g=g, j=j: e.transpose(w[0:NE, j * P:(j + 1) * P],
                                                                          cw[:, g * GT + j, :], ident[:, :]),
                                      sem(n + "cwT_p"))
                        act.wait(m)
                        cwT_done = act.do(lambda e, w=w, g=g: e.activation(
                            cwT[:, g * GT:(g + 1) * GT, :].rearrange("p t n -> p (t n)"), w[0:NE, :], ACT.Copy),
                            sem(n + "cwT"))
                        work.release(i, cwT_done)
                    pe.wait(cwT_done, *b2_in)
                    for t in range(NT):
                        i, w, bf = work.take()
                        pe.wait(bf)
                        m = pe.do(lambda e, w=w, t=t: e.matmul(w[:, 0:D], cwT[:, t, :], b2[:, :], start=True, stop=True),
                                  sem(n + "b2_p"))
                        dve.wait(m)
                        m = dve.do(lambda e, w=w, t=t: e.tensor_tensor(x_sb[:, t, :], w[:, 0:D], x_sb[:, t, :], ALU.add),
                                   sem(n + "xb"))
                        work.release(i, m)
                    end_phase()

                ab, yb = Banks(bank[0:4]), Banks(bank[4:8])
                HCH = HID1 // P
                h32 = [sb(st, n + f"h32_{i}", [P, GN]) for i in range(2)]
                hT = [(sb(st, n + f"h_hi{i}", [P, HCH, GN], F32R), sb(st, n + f"h_lo{i}", [P, HCH, GN], F32R))
                      for i in range(2)]
                cols = (DC * HID1, HCH * D)
                stage = sb(st, n + "stage", [P, sum(cols)])
                wts = [(sb(st, n + f"w_hi{i}", [P, sum(cols)], F32R), sb(st, n + f"w_lo{i}", [P, sum(cols)], F32R))
                       for i in range(2)]
                M = {}

                def mark(*k):
                    return M.get(k)

                def weights(e):
                    at = 0
                    for k, (name, sname) in enumerate((("eW1", "sW1"), ("eW2", "sW2"))):
                        src = (A["L1_ffn_" + name][e] if e < E1 else A["L1_ffn_" + sname]).rearrange(
                            "(c p) n -> p c n", p=P)
                        raw = stage[:, at:at + cols[k]]
                        sp.wait(mark("w", e - 1, k))
                        arrived = sp.do(lambda q, raw=raw, src=src: q.dma_start(
                            raw.rearrange("p (c n) -> p c n", c=src.shape[1]), src), sem(n + "stage" + name), 16)
                        hi, lo = (t[:, at:at + cols[k]] for t in wts[e % 2])
                        pool.wait(arrived, mark("y_p", (e - 1) * NG - 1))
                        m = pool.do(lambda q, hi=hi, raw=raw: q.tensor_copy(hi, raw), sem(n + "w"))
                        pool.wait(m)
                        M["w", e, k] = pool.do(lambda q, hi=hi, lo=lo, raw=raw: q.tensor_tensor(
                            lo, raw, f(hi), ALU.subtract), sem(n + "w"))
                        at += cols[k]

                def wview(e, k, part):
                    at = sum(cols[:k])
                    return wts[e % 2][part][:, at:at + cols[k]].rearrange("p (c n) -> p c n", c=2)

                def hidden(i):
                    e, g = divmod(i, NG)
                    x_hi, x_lo = xT[g]
                    for m_ in range(HCH):
                        ia, w, bf = ab.take()
                        ws = slice(m_ * P, (m_ + 1) * P)
                        pe.wait(bf, xT_done[g], M["w", e, 0])
                        for c in range(DC):
                            m = matmul3(w[:, :], wview(e, 0, 0)[:, c, ws], wview(e, 0, 1)[:, c, ws], x_hi[:, c, :],
                                        x_lo[:, c, :], c == 0, c == DC - 1, sem(n + "h_p"))
                        act.wait(m, mark("h_lo", i - 1, m_), *b1_in)
                        m = act.do(lambda q, w=w, m_=m_, e=e: q.activation(h32[m_][:], w[:, :], ACT.Relu,
                                                                         bias=b1[:, e, m_:m_ + 1]), sem(n + "h32"))
                        ab.release(ia, m)
                        act.wait(m, mark("y_p", i - 2))
                        m = act.do(lambda q, m_=m_: q.activation(hT[i % 2][0][:, m_, :], h32[m_][:], ACT.Copy),
                                   sem(n + "h_hi"))
                        dve.wait(m)
                        m = dve.do(lambda q, m_=m_: q.tensor_tensor(hT[i % 2][1][:, m_, :], h32[m_][:],
                                                                   f(hT[i % 2][0][:, m_, :]), ALU.subtract),
                                   sem(n + "h_lo"))
                        M["h_lo", i, m_] = m
                        M["h", i] = m
                        yield

                def output(i):
                    e, g = divmod(i, NG)
                    h_hi, h_lo = hT[i % 2]
                    for j in range(GT):
                        iy, w, bf = yb.take()
                        ts = slice(j * P, (j + 1) * P)
                        pe.wait(bf, M["h", i], M["w", e, 1])
                        for c in range(HCH):
                            m = matmul3(w[:, 0:D], h_hi[:, c, ts], h_lo[:, c, ts], wview(e, 1, 0)[:, c, :],
                                        wview(e, 1, 1)[:, c, :], c == 0, c == HCH - 1, sem(n + "y_p"))
                        M["y_p", i] = m
                        t = g * GT + j
                        dve.wait(m, mark("x", i - 1))
                        m = dve.do(lambda q, w=w, t=t: q.scalar_tensor_tensor(
                            out=x_sb[:, t, :], in0=w[:, 0:D], scalar=cw[:, t, e:e + 1], in1=x_sb[:, t, :],
                            op0=ALU.mult, op1=ALU.add), sem(n + "x"))
                        yb.release(iy, m)
                        M["x", i] = m
                        if j % 2:
                            yield
                    if e == NE - 1:
                        store_group(g, m)

                NB = NE * NG
                weights(0)
                for i in range(NB + 1):
                    if i % NG == 2 and i // NG + 1 < NE:
                        weights(i // NG + 1)
                    interleave(*([(hidden(i), 1)] if i < NB else []), *([(output(i - 1), 1)] if i else []))

        stored = []
        out_v = out.rearrange("b (t p) d -> p (b t) d", p=P)

        def store_group(g, ready):
            sp.wait(ready)
            stored.append(sp.do(lambda e: e.dma_start(out_v[:, g * GT:(g + 1) * GT, :],
                                                      x_sb[:, g * GT:(g + 1) * GT, :]), sem(f"x_io{g}"), 16))

        xr = attention(0, A["L0_xattn_Wq"], A["L0_xattn_Wk"], A["L0_xattn_Wv"], A["L0_xattn_Wo"], A["L0_xattn_bq"],
                       A["L0_xattn_bk"], A["L0_xattn_bv"], A["L0_xattn_bo"], x_ready)
        x_back = []
        experts_swiglu(xr)
        xr = attention(1, A["L1_WqT"], A["L1_WkT"], A["L1_WvT"], A["L1_WoT"], None, None, None, None,
                       x_back)
        experts_relu(xr)
        sp.wait(*stored)

        block = ctx.enter_context(nc.Block())

        @block.sync
        def _(eng):
            sp.play(eng)

        @block.gpsimd
        def _(eng):
            pool.play(eng)

        @block.scalar
        def _(eng):
            act.play(eng)

        @block.vector
        def _(eng):
            dve.play(eng)

        @block.tensor
        def _(eng):
            pe.play(eng)


_DIRECT = ["x", "ctx_512", "L0_xattn_Wq", "L0_xattn_bq", "L0_xattn_Wk", "L0_xattn_bk", "L0_xattn_Wv", "L0_xattn_bv",
           "L0_xattn_Wo", "L0_xattn_bo", "L0_ffn_wg", "L0_ffn_w1", "L0_ffn_w3", "L0_ffn_w2", "L1_ffn_router_W",
           "L1_ffn_router_b", "L1_ffn_sW1", "L1_ffn_sb1", "L1_ffn_sW2", "L1_ffn_sb2", "L1_ffn_eW1", "L1_ffn_eW2",
           "L1_ffn_eb2"]


def kernel(**inputs):
    import numpy as np
    import concourse.bacc as bacc
    from concourse.bass_utils import run_bass_kernel_spmd

    laid = {name: np.asarray(inputs[name]) for name in _DIRECT}
    laid["L1_WqT"] = np.asarray(inputs["L1_xattn_Wq"]).T
    laid["L1_WkT"] = np.asarray(inputs["L1_xattn_Wkv"])[:D].T
    laid["L1_WvT"] = np.asarray(inputs["L1_xattn_Wkv"])[D:].T
    laid["L1_WoT"] = np.asarray(inputs["L1_xattn_Wo"]).T
    laid["L1_ffn_eb1"] = np.asarray(inputs["L1_ffn_eb1"]).reshape(E1, HID1 // P, P).transpose(2, 0, 1)

    for name in ("L0_xattn_bq", "L0_xattn_bk", "L1_ffn_sb1"):
        laid[name] = np.asarray(inputs[name]).reshape(-1, P).T

    nc = bacc.Bacc("TRN2", target_bir_lowering=False, num_devices=1)
    arrays, aps = {}, {}
    for name, a in laid.items():
        arrays[f"in_{name}"] = np.ascontiguousarray(a)
        aps[name] = nc.dram_tensor(f"in_{name}", a.shape, mybir.dt.from_np(a.dtype), kind="ExternalInput").ap()
    out = nc.dram_tensor("out_x", (BATCH, SEQ, D), F32, kind="ExternalOutput").ap()
    build(nc, aps, out)
    r = run_bass_kernel_spmd(nc, [arrays], core_ids=[0])
    return r.results[0]["out_x"]
```

```python
from contextlib import ExitStack

import concourse.bass as bass
from concourse import mybir

ALU = mybir.AluOpType
ACT = mybir.ActivationFunctionType
F32 = mybir.dt.float32
F32R = mybir.dt.float32r
I32 = mybir.dt.int32
AX_X = mybir.AxisListType.X

P = 128
BATCH, SEQ, D = 4, 1024, 256
TOK = BATCH * SEQ
NT = TOK // P
GT = 4
GN = GT * P
NG = TOK // GN
DC = D // P
KV, CTX = 77, 128
H, DH = 16, 16
HC = H // DC
VC = [(0, 6), (6, 11), (11, 16)]
SUMS = 96
EPS = 1e-5
E0, CAP, HID0 = 8, 1024, 512
E1, TOP, HID1 = 15, 3, 256
BLK = 256
NBLK = (TOP * TOK + E1 * (BLK - 1)) // BLK
BANK = 512


class Sem:

    def __init__(self, handle):
        self.handle, self.value = handle, 0

    def now(self):
        return self, self.value

    def mark(self, by):
        self.value += by
        return (self, self.value)


class Lane:

    def __init__(self):
        self.steps, self.seen = [], {}

    def wait(self, *marks):
        for m in marks:
            if m is not None and self.seen.get(m[0], 0) < m[1]:
                self.seen[m[0]] = m[1]
                self.steps.append(lambda eng, m=m: eng.wait_ge(m[0].handle, m[1]))

    def do(self, call, sem=None, by=1):
        if sem is None:
            self.steps.append(call)
            return None
        self.steps.append(lambda eng: call(eng).then_inc(sem.handle, by))
        return sem.mark(by)

    def play(self, eng):
        for s in self.steps:
            s(eng)


class Banks:

    def __init__(self, tensors):
        self.tensors, self.free, self.n = tensors, [None] * len(tensors), 0

    def take(self):
        i = self.n % len(self.tensors)
        self.n += 1
        return i, self.tensors[i], self.free[i]

    def release(self, i, mark):
        self.free[i] = mark


def run(steps):
    for _ in steps:
        pass


def interleave(*streams):
    live = [[g, n] for g, n in streams]
    while live:
        for item in list(live):
            for _ in range(item[1]):
                try:
                    next(item[0])
                except StopIteration:
                    live.remove(item)
                    break


def f(ap):
    return ap.bitcast(F32)


def build(nc, A, out):
    pe, act, dve, pool, sp = (Lane() for _ in range(5))
    ctx = ExitStack()
    names = {}

    def sem(name):
        if name not in names:
            names[name] = Sem(ctx.enter_context(nc.semaphore("s_" + name)))
        return names[name]

    def sb(stack, name, shape, dt=F32):
        return stack.enter_context(nc.sbuf_tensor(name, shape, dt))

    with ctx:
        bank = [ctx.enter_context(nc.psum_tensor(f"bank{i}", [P, BANK], F32)) for i in range(8)]
        x_sb = sb(ctx, "x_sb", [P, NT, D])
        ident = sb(ctx, "ident", [P, P])
        neg_half = sb(ctx, "neg_half", [P, GT])
        phase_end = sem("phase_end")
        plane_d = nc.dram_tensor("plane_scratch", (TOP * TOK, D), F32, kind="Internal").ap()
        xn_d = nc.dram_tensor("xn_scratch", (TOK, D), F32, kind="Internal").ap()
        acc_d = nc.dram_tensor("acc_scratch", (TOK, D), F32, kind="Internal").ap()

        s_const = sem("const")
        zero = pool.do(lambda e: e.memset(ident[:, :], 0.0), s_const)
        pool.wait(zero)
        pool.do(lambda e: e.affine_select(out=ident[:, :], in_=ident[:, :], compare_op=ALU.not_equal, fill=1.0,
                                          base=0, pattern=[[-1, P]], channel_multiplier=1), s_const)
        const_done = pool.do(lambda e: e.memset(neg_half[:, :], -0.5), s_const)

        x_in = A["x"].rearrange("b (t p) d -> p (b t) d", p=P)

        def load_x(g):
            return [sp.do(lambda e: e.dma_start(x_sb[:, g * GT:(g + 1) * GT, :], x_in[:, g * GT:(g + 1) * GT, :]),
                          sem(f"x_io{g}"), 16)]

        def rows(d):
            return d.rearrange("(t p) d -> p t d", p=P)

        def end_phase():
            for lane in (pe, act, dve, pool, sp):
                lane.do(lambda e: e.drain(), phase_end)
            for lane in (pe, act, dve, pool, sp):
                lane.wait((phase_end, phase_end.value))

        def matmul3(o, w_hi, w_lo, x_hi, x_lo, first, last, done=None):
            pe.do(lambda e: e.matmul(o, w_hi, x_hi, start=first, stop=False))
            pe.do(lambda e: e.matmul(o, w_lo, x_hi, start=False, stop=False))
            return pe.do(lambda e: e.matmul(o, w_hi, x_lo, start=False, stop=last), done)

        def layernorm_steps(g, tmp, xn, ready, free):
            b = g % 2
            stats, mv, rstd = tmp
            dve.wait(*ready)
            for j in range(GT):
                m = dve.do(lambda e, j=j: e.bn_stats(stats[:, b, j, :], x_sb[:, g * GT + j, :]), sem("ln_stats"))
                if j % 2:
                    yield
            dve.wait(m)
            for j in range(GT):
                m = dve.do(lambda e, j=j: e.bn_aggr(mv[:, b, j, :], stats[:, b, j, :]), sem("ln_stats"))
            dve.wait(m)
            m = dve.do(lambda e: e.tensor_scalar(rstd[:, b, 0, :], mv[:, b, :, 1], EPS, None, ALU.add), sem("ln_var"))
            pool.wait(m, const_done)
            rstd_done = pool.do(lambda e: e.tensor_tensor(rstd[:, b, 1, :], rstd[:, b, 0, :], neg_half[:, :], ALU.pow),
                                sem("ln_rstd"))
            yield
            dve.wait(rstd_done, *free)
            for j in range(GT):
                m = dve.do(lambda e, j=j: e.tensor_scalar(xn[:, j, :], x_sb[:, g * GT + j, :], mv[:, b, j, 0:1],
                                                          rstd[:, b, 1, j:j + 1], ALU.subtract, ALU.mult),
                           sem("ln_out"))
                if j % 2:
                    yield
            return m

        def layernorm(*args):
            steps = layernorm_steps(*args)
            while True:
                try:
                    next(steps)
                except StopIteration as end:
                    return end.value

        def transpose_split(banks, src, src_ready, hi, lo, free, what):
            marks = []
            for c in range(DC):
                i, w, bank_free = banks.take()
                pe.wait(bank_free, src_ready, const_done)
                for j in range(GT):
                    m = pe.do(lambda e, w=w, c=c, j=j: e.transpose(w[:, j * P:(j + 1) * P],
                                                                   src[:, j, c * P:(c + 1) * P], ident[:, :]),
                              sem(what + "_T") if j == GT - 1 else None)
                act.wait(m, *free)
                m = act.do(lambda e, w=w, c=c: e.activation(hi[:, c, :], w[:, :], ACT.Copy), sem(what + "_hi"))
                dve.wait(m, *free)
                m = dve.do(lambda e, w=w, c=c: e.tensor_tensor(lo[:, c, :], w[:, :], f(hi[:, c, :]), ALU.subtract),
                           sem(what + "_lo"))
                banks.release(i, m)
                marks.append(m)
                yield
            return marks[-1]

        def attention(L, wq_d, wk_d, wv_d, wo_d, bq_d, bk_d, bv_d, bo_d, load_x):
            xr = [load_x(0)]
            st = ExitStack()
            with st:
                work, sexp, pv = Banks(bank[0:4]), Banks(bank[4:6]), Banks(bank[6:8])
                n = f"a{L}_"
                ln_tmp = (sb(st, n + "stats", [P, 2, GT, 6]), sb(st, n + "mv", [P, 2, GT, 2]),
                          sb(st, n + "rstd", [P, 2, 2, GT]))
                kaug = sb(st, n + "kaug", [P, H, BATCH, KV], F32R)
                kblk = sb(st, n + "kblk", [P, DC, BATCH, HC, KV], F32R)
                v_sb = sb(st, n + "v", [KV, BATCH, D])
                vpad = [sb(st, n + f"vpad{i}", [KV, H, P]) for i in range(2)]
                qb = sb(st, n + "qb", [P, 4 * DC])
                wq_hi, wq_lo = sb(st, n + "wq_hi", [P, DC, D], F32R), sb(st, n + "wq_lo", [P, DC, D], F32R)
                NV = len(VC)
                wo_hi, wo_lo = sb(st, n + "wo_hi", [P, NV, D], F32R), sb(st, n + "wo_lo", [P, NV, D], F32R)
                ones16 = sb(st, n + "ones16", [H, NV, SUMS])
                spread = sb(st, n + "spread", [H, NV, SUMS], F32R)

                o_sb = sb(st, n + "o", [P, NV, GN])
                stage = o_sb[:].rearrange("p c n -> p (c n)")[:, 0:(DC + NV) * D].rearrange("p (k n) -> p k n", n=D)
                wk = sb(st, n + "wk", [P, D])
                wv = sb(st, n + "wv", [P, D])
                ctx_sb = sb(st, n + "ctx", [KV, BATCH, CTX])
                ctxT = sb(st, n + "ctxT", [P, BATCH, KV])
                k_hi = sb(st, n + "k_hi", [P, DC, BATCH * KV], F32R)
                k_lo = sb(st, n + "k_lo", [P, DC, BATCH * KV], F32R)
                pair = sb(st, n + "pair", [P, 2])
                head = sb(st, n + "head", [P, HC])
                bvb = sb(st, n + "bvb", [KV, D])

                bob = sb(st, n + "bob", [P, D])
                xn = sb(st, n + "xn", [P, GT, D])

                def load(dst, src, name):
                    return sp.do(lambda e: e.dma_start(dst, src), sem("attn_in_" + name), 16)

                ctx_in = load(ctx_sb[:], A["ctx_512"].rearrange("b s c -> s b c"), "ctx")
                wk_in = load(wk[:], wk_d, "wk")
                wv_in = load(wv[:], wv_d, "wv")
                wq_in = load(stage[:, 0:DC, :], wq_d.rearrange("(c p) n -> p c n", p=P), "wq")
                m = pool.do(lambda e: e.memset(stage[:, DC:, :], 0.0), sem("attn_mask"))
                sp.wait(m)
                for c, (h0, h1) in enumerate(VC):
                    wo_in = load(stage[0:(h1 - h0) * DH, DC + c, :], wo_d[h0 * DH:h1 * DH, :], "wo")
                if bq_d is not None:
                    bq_in = load(qb[:, 0:DC], bq_d, "bq")
                    bk_in = load(qb[:, DC:2 * DC], bk_d, "bk")
                    bo_in = load(bob[:], bo_d.rearrange("(a n) -> a n", a=1).broadcast_to([P, D]), "bo")
                    bv_in = load(bvb[:], bv_d.rearrange("(a n) -> a n", a=1).broadcast_to([KV, D]), "bv")
                else:
                    bq_in = bk_in = dve.do(lambda e: e.memset(qb[:], 0.0), sem("attn_bias"))
                    bv_in = dve.do(lambda e: e.memset(bvb[:], 0.0), sem("attn_bias"))

                xr += [load_x(g) for g in range(1, NG)]
                ln0 = layernorm(0, ln_tmp, xn, xr[0], [])

                pool.do(lambda e: e.memset(pair[:], 1.0), sem("attn_mask"))
                m = pool.do(lambda e: e.memset(head[:], 1.0), sem("attn_mask"))
                pool.wait(m)
                m = pool.do(lambda e: e.affine_select(out=head[:], in_=head[:], compare_op=ALU.is_ge, fill=0.0,
                                                      base=0, pattern=[[-DH, HC]], channel_multiplier=1),
                            sem("attn_mask"))
                pool.wait(m)
                m = pool.do(lambda e: e.affine_select(out=head[:], in_=head[:], compare_op=ALU.is_ge, fill=0.0,
                                                      base=DH - 1, pattern=[[DH, HC]], channel_multiplier=-1),
                            sem("attn_mask"))
                head_done = m
                pool.do(lambda e: e.memset(ones16[:], 1.0), sem("attn_mask"))
                for c, (h0, h1) in enumerate(VC):
                    for base, sign in ((h0 * DH, 1), (DH - 1 - h0 * DH, -1)):
                        pool.wait(sem("attn_mask").now())
                        m = pool.do(lambda e, c=c, base=base, sign=sign: e.affine_select(
                            out=ones16[:, c, :], in_=ones16[:, c, :], compare_op=ALU.is_ge, fill=0.0, base=base,
                            pattern=[[sign, SUMS]], channel_multiplier=-sign * DH), sem("attn_mask"))
                ones16_done = m
                dve.wait(head_done)
                m = dve.do(lambda e: e.tensor_reduce(pair[:], head[:].rearrange("p (a i) -> p i a", i=2),
                                                     AX_X, ALU.add), sem("attn_mask2"))
                pair_done = m

                pool.wait(wo_in)
                m = pool.do(lambda e: e.tensor_copy(wo_hi[:], stage[:, DC:, :]), sem("attn_w"))
                pool.wait(m)
                wo_done = pool.do(lambda e: e.tensor_tensor(wo_lo[:], stage[:, DC:, :], f(wo_hi[:]), ALU.subtract),
                                  sem("attn_w"))

                for i in range(2):
                    zeros = pool.do(lambda e, i=i: e.memset(vpad[i][:], 0.0), sem("attn_pad"))
                pool.wait(zeros)
                for i in range(2):
                    for c, (h0, h1) in enumerate(VC):
                        for h in range(h0, h1):
                            pool.do(lambda e, i=i, h=h, col=SUMS + h - h0: e.memset(vpad[i][:, h, col:col + 1], 1.0),
                                    sem("attn_pad"))
                i, w, bf = work.take()
                pe.wait(bf, ctx_in, const_done)
                for b in range(BATCH):
                    m = pe.do(lambda e, b=b, w=w: e.transpose(w[:, b * KV:(b + 1) * KV], ctx_sb[:, b, :],
                                                              ident[0:KV, 0:KV]), sem("attn_ctxT_p"))
                act.wait(m)
                ctxT_done = act.do(lambda e, w=w: e.activation(ctxT[:].rearrange("p b s -> p (b s)"),
                                                               w[:, 0:BATCH * KV], ACT.Copy), sem("attn_ctxT"))
                work.release(i, ctxT_done)

                act.wait(wq_in)
                m = act.do(lambda e: e.activation(wq_hi[:], stage[:, 0:DC, :], ACT.Copy), sem("attn_wq_hi"))
                dve.wait(m)
                wq_done = dve.do(lambda e: e.tensor_tensor(wq_lo[:], stage[:, 0:DC, :], f(wq_hi[:]), ALU.subtract),
                                 sem("attn_wq_lo"))

                k_done = []
                for m_ in range(DC):
                    i, w, bf = work.take()
                    pe.wait(bf, wk_in, ctxT_done)
                    m = pe.do(lambda e, w=w, m_=m_: e.matmul(w[:, 0:BATCH * KV], wk[:, m_ * P:(m_ + 1) * P],
                                                            ctxT[:].rearrange("p b s -> p (b s)"),
                                                            start=True, stop=True), sem("attn_k_p"))
                    act.wait(m, bk_in)
                    m = act.do(lambda e, w=w, m_=m_: e.activation(k_hi[:, m_, :], w[:, 0:BATCH * KV], ACT.Identity,
                                                                 bias=qb[:, DC + m_:DC + m_ + 1]), sem("attn_k_hi"))
                    dve.wait(m, bk_in)
                    m = dve.do(lambda e, w=w, m_=m_: e.scalar_tensor_tensor(
                        out=k_lo[:, m_, :], in0=w[:, 0:BATCH * KV], scalar=qb[:, DC + m_:DC + m_ + 1],
                        in1=f(k_hi[:, m_, :]), op0=ALU.add, op1=ALU.subtract), sem("attn_k_lo"))
                    work.release(i, m)
                    k_done.append(m)

                xT = sb(st, n + "xT_hi", [P, DC, GN], F32R), sb(st, n + "xT_lo", [P, DC, GN], F32R)
                q_hi, q_lo = sb(st, n + "q_hi", [P, DC, GN], F32R), sb(st, n + "q_lo", [P, DC, GN], F32R)
                qaug = [sb(st, n + f"qaug{i}", [P, DC, 4, GN], F32R) for i in range(2)]
                nmax = sb(st, n + "nmax", [P, GT, H])
                nmaxT = sb(st, n + "nmaxT", [H, GN], F32R)
                NR = 6
                prob = sb(st, n + "prob", [KV, NR, GN])
                TS = P // H
                sums, recip = sb(st, n + "sums", [P, GN // TS]), sb(st, n + "recip", [P, GN // TS])
                recip_hi, recip_lo = (sb(st, n + "recip_" + k, [P, GN // TS], F32R) for k in ("hi", "lo"))
                rh_hi, rh_lo = (sb(st, n + "rh_" + k, [H, GN], F32R) for k in ("hi", "lo"))
                oT = sb(st, n + "oT_hi", [P, NV, GN], F32R), sb(st, n + "oT_lo", [P, NV, GN], F32R)

                M = {("xn", 0): ln0}

                def mark(what, g):
                    return M.get((what, g))

                def norm(g):
                    M["xn", g] = yield from layernorm_steps(g, ln_tmp, xn, xr[g], [mark("xT", g - 1)])

                def query(g):
                    M["xT", g] = yield from transpose_split(work, xn, M["xn", g], xT[0], xT[1],
                                                            [mark("q_p", g - 1)], "attn_x")
                    for m_ in range(DC):
                        i, w, bf = work.take()
                        pe.wait(bf, M["xT", g], wq_done)
                        for c in range(DC):
                            ws = slice(m_ * P, (m_ + 1) * P)
                            m = matmul3(w[:, :], wq_hi[:, c, ws], wq_lo[:, c, ws], xT[0][:, c, :], xT[1][:, c, :],
                                        c == 0, c == DC - 1, sem("attn_q_p"))
                        M["q_p", g] = m
                        act.wait(m, bq_in, mark("qaug", g - 1), mark("max_p", g - 1))
                        m = act.do(lambda e, w=w, m_=m_: e.activation(q_hi[:, m_, :], w[:, :], ACT.Identity,
                                                                     bias=qb[:, m_:m_ + 1]), sem("attn_q_hi"))
                        dve.wait(m, bq_in)
                        m = dve.do(lambda e, w=w, m_=m_: e.scalar_tensor_tensor(
                            out=q_lo[:, m_, :], in0=w[:, :], scalar=qb[:, m_:m_ + 1], in1=f(q_hi[:, m_, :]),
                            op0=ALU.add, op1=ALU.subtract), sem("attn_q_lo"))
                        work.release(i, m)
                        M["q", g, m_] = m
                        yield
                    dst = qaug[g % 2]
                    sp.wait(m, mark("s_p", g - 2))
                    s_q = sem(f"attn_qaug{g % 2}")
                    for r in range(4):
                        for rows, src in ((0, q_hi), (32, q_hi), (64, q_lo)):
                            sp.do(lambda e, dst=dst, r=r, rows=rows, src=src: e.dma_start(
                                f(dst[rows:rows + 32, :, r, :]), f(src[32 * r:32 * r + 32, :, :])), s_q, 16)
                    yield

                def maxima(g):
                    b = g * GN // SEQ
                    dst = qaug[g % 2]
                    for m_ in range(DC):
                        for j in range(GT):
                            for half in range(2):
                                i, w, bf = work.take()
                                pe.wait(bf, M["q", g, m_], *kblk_done)
                                hs = slice(half * HC // 2, (half + 1) * HC // 2)
                                m = pe.do(lambda e, w=w, j=j, m_=m_, hs=hs: e.matmul(
                                    w[:, 0:HC // 2 * KV], q_hi[:, m_, j * P:(j + 1) * P],
                                    kblk[:, m_, b, hs, :].rearrange("p h s -> p (h s)"), start=True, stop=True),
                                    sem("attn_max_p"))
                                M["max_p", g] = m
                                h0 = m_ * HC + half * HC // 2
                                dve.wait(m, mark("nmaxT_p", g - 1))
                                m = dve.do(lambda e, w=w, j=j, h0=h0: e.tensor_reduce(
                                    nmax[:, j, h0:h0 + HC // 2],
                                    w[:, 0:HC // 2 * KV].rearrange("p (h s) -> p h s", s=KV), AX_X, ALU.max,
                                    negate=True), sem("attn_nmax"))
                                work.release(i, m)
                            yield
                    i, w, bf = work.take()
                    pe.wait(bf, m)
                    for j in range(GT):
                        m = pe.do(lambda e, w=w, j=j: e.transpose(w[0:H, j * P:(j + 1) * P], nmax[:, j, :],
                                                                 ident[:, :]), sem("attn_nmaxT_p"))
                    M["nmaxT_p", g] = m
                    dve.wait(m, mark("qaug", g - 1))
                    m = dve.do(lambda e, w=w: e.tensor_copy(nmaxT[:, :], w[0:H, :]), sem("attn_nmaxT"))
                    work.release(i, m)
                    sp.wait(m)
                    M["qaug", g] = sp.do(lambda e: e.dma_start(
                        f(dst[96:96 + H, :, :, :]).rearrange("p m r t -> p (m r) t"),
                        f(nmaxT[:, :]).rearrange("p (o t) -> p o t", o=1).broadcast_to([H, 4 * DC, GN])),
                        sem(f"attn_qaug{g % 2}"), 16)
                    yield

                def score(g, h):
                    b = g * GN // SEQ
                    k = g * H + h
                    i, w, bf = sexp.take()
                    pe.wait(bf, M["qaug", g], *kaug_done)
                    m = pe.do(lambda e, w=w: e.matmul(w[0:KV, :], kaug[0:96 + H, h, b, :],
                                                      qaug[g % 2][0:96 + H, h // HC, h % HC // 2, :],
                                                      start=True, stop=True), sem("attn_s_p"))
                    M["s_p", g] = m
                    act.wait(m, mark("pv_p", k - NR))
                    m = act.do(lambda e, w=w: e.activation(prob[:, k % NR, :], w[0:KV, :], ACT.Exp,
                                                           scale=float(DH) ** -0.5), sem("attn_prob"))
                    sexp.release(i, m)
                    M["prob", k] = m

                pv_bank = {}

                def pad(b):
                    pool.wait(v_done, mark("pv_p", ((b - 1) * SEQ // GN) * H - 1))
                    for h0, h1 in VC:
                        for h in range(h0, h1):
                            M["vpad", b] = pool.do(lambda e, h=h, col=(h - h0) * DH: e.tensor_copy(
                                vpad[b % 2][:, h, col:col + DH], v_sb[:, b, h * DH:(h + 1) * DH]), sem("attn_pad"))

                def values(g, h):
                    b = g * GN // SEQ
                    k = g * H + h
                    c = [h0 <= h < h1 for h0, h1 in VC].index(True)
                    h0, h1 = VC[c]
                    if h == h0:
                        pv_bank[g, c] = pv.take()
                    i, w, bf = pv_bank[g, c]
                    pe.wait(bf, M["prob", k], M["vpad", b])
                    M["pv_p", k] = pe.do(lambda e: e.matmul(w[:, :], vpad[b % 2][:, h, :], prob[:, k % NR, :],
                                                            start=(h == h0), stop=(h == h1 - 1)), sem("attn_pv_p"))

                def unload(g, c):
                    i, w, _ = pv_bank[g, c]
                    h0, h1 = VC[c]
                    rows = SUMS + h1 - h0
                    act.wait(M["pv_p", g * H + h1 - 1], mark("oT", (g - 1) * NV + c), wo_done)
                    m = act.do(lambda e: e.activation(o_sb[0:rows, c, :], w[0:rows, :], ACT.Copy), sem("attn_o"))
                    pv.release(i, m)
                    M["o", g, c] = m
                    sp.wait(m, mark("recip", g - 1))
                    M["sums", g] = sp.do(lambda e: e.dma_start(
                        sums[h0 * TS:h1 * TS, :], o_sb[SUMS:rows, c, :].rearrange("h (a t) -> h a t", a=TS)),
                        sem("attn_sums"), 16)

                def reciprocals(g):
                    dve.wait(M["sums", g])
                    m = M["recip", g] = dve.do(lambda e: e.reciprocal(recip[:], sums[:]), sem("attn_recip"))
                    dve.wait(m, mark("rh", g - 1))
                    m = dve.do(lambda e: e.tensor_copy(recip_hi[:], recip[:]), sem("attn_recip"))
                    dve.wait(m)
                    m = dve.do(lambda e: e.tensor_tensor(recip_lo[:], recip[:], f(recip_hi[:]), ALU.subtract),
                               sem("attn_recip"))
                    sp.wait(m, mark("rb_p", g - 1))
                    for dst, src in ((rh_hi, recip_hi), (rh_lo, recip_lo)):
                        M["rh", g] = sp.do(lambda e, dst=dst, src=src: e.dma_start(
                            f(dst[:]).rearrange("h (a t) -> h a t", a=TS), f(src[:])), sem("attn_rh"), 16)

                def normalise(g):
                    reciprocals(g)
                    yield
                    for c, (h0, h1) in enumerate(VC):
                        nf = (h1 - h0) * DH
                        i, w, bf = work.take()
                        pe.wait(bf, M["rh", g], spread_done)
                        pe.do(lambda e, w=w, nf=nf, c=c: e.matmul(w[0:nf, :], spread[:, c, 0:nf], rh_hi[:],
                                                                  start=True, stop=False))
                        m = pe.do(lambda e, w=w, nf=nf, c=c: e.matmul(w[0:nf, :], spread[:, c, 0:nf], rh_lo[:],
                                                                      start=False, stop=True), sem("attn_rb_p"))
                        M["rb_p", g] = m
                        o = o_sb[0:nf, c, :]
                        dve.wait(m, M["o", g, c], M["sums", g])
                        m = dve.do(lambda e, w=w, o=o, nf=nf: e.tensor_tensor(o, w[0:nf, :], o, ALU.mult),
                                   sem("attn_on"))
                        work.release(i, m)
                        act.wait(m, mark("y_p", g - 1))
                        m = act.do(lambda e, c=c, nf=nf, o=o: e.activation(oT[0][0:nf, c, :], o, ACT.Copy),
                                   sem("attn_o_hi"))
                        yield
                        dve.wait(m)
                        M["oT", g * NV + c] = dve.do(lambda e, c=c, nf=nf, o=o: e.tensor_tensor(
                            oT[1][0:nf, c, :], o, f(oT[0][0:nf, c, :]), ALU.subtract), sem("attn_o_lo"))
                        yield

                def back(g):
                    for j in range(0, GT, 2):
                        i, w, bf = work.take()
                        pe.wait(bf, M["oT", g * NV + NV - 1], wo_done)
                        for o in range(2):
                            ts = slice((j + o) * P, (j + o + 1) * P)
                            for c, (h0, h1) in enumerate(VC):
                                r = slice(0, (h1 - h0) * DH)
                                m = matmul3(w[:, o * D:(o + 1) * D], oT[0][r, c, ts], oT[1][r, c, ts],
                                            wo_hi[r, c, :], wo_lo[r, c, :], c == 0, c == NV - 1, sem("attn_y_p"))
                        M["y_p", g] = m
                        xt = x_sb[:, g * GT + j:g * GT + j + 2, :]
                        dve.wait(m)
                        m = dve.do(lambda e, w=w, xt=xt: e.tensor_tensor(
                            xt, w[:, :].rearrange("p (j d) -> p j d", j=2), xt, ALU.add), sem("attn_x"))
                        work.release(i, m)
                        if bo_d is not None:
                            pool.wait(m, bo_in)
                            m = pool.do(lambda e, xt=xt: e.tensor_tensor(
                                xt, xt, bob[:].rearrange("p (o d) -> p o d", o=1).broadcast_to([P, 2, D]), ALU.add),
                                sem("attn_xb"))
                        M["x", g] = m
                        yield

                LAG = 2
                first = query(0)
                for c in range(DC):
                    next(first)
                act.wait(head_done, k_done[-1])
                for h in range(HC):
                    m = act.do(lambda e, h=h: e.activation(
                        kblk[:, 0, :, h, :], f(k_hi[:, 0, :]).rearrange("p (b s) -> p b s", b=BATCH), ACT.Copy,
                        scale=head[:, h:h + 1]), sem("attn_kblk"))
                dve.wait(head_done, k_done[-1])
                for b in range(BATCH):
                    m2 = dve.do(lambda e, b=b: e.tensor_tensor(
                        kblk[:, 1, b, :, :],
                        f(k_hi[:, 1, b * KV:(b + 1) * KV]).rearrange("p (o s) -> p o s", o=1).broadcast_to([P, HC, KV]),
                        head[:].rearrange("p (h o) -> p h o", o=1).broadcast_to([P, HC, KV]),
                        ALU.mult), sem("attn_kblk2"))
                kblk_done = [m, m2]

                for b in range(BATCH):
                    i, w, bf = work.take()
                    pe.wait(bf, wv_in, ctxT_done)
                    m = pe.do(lambda e, w=w, b=b: e.matmul(w[0:KV, 0:D], ctxT[:, b, :], wv[:, :],
                                                          start=True, stop=True), sem("attn_v_p"))
                    dve.wait(m, bv_in)
                    v_done = dve.do(lambda e, w=w, b=b: e.tensor_tensor(v_sb[:, b, :], w[0:KV, 0:D], bvb[:], ALU.add),
                                    sem("attn_v"))
                    work.release(i, v_done)

                dve.wait(k_done[-1], pair_done)
                act.wait(pair_done)
                for m_ in range(DC):
                    for r in range(4):
                        q = slice(32 * r, 32 * r + 32)
                        h0 = m_ * HC + 2 * r
                        kaug_hi = dve.do(lambda e, q=q, h0=h0, m_=m_: e.tensor_tensor(
                            kaug[0:32, h0:h0 + 2, :, :].rearrange("p h b s -> p h (b s)"),
                            f(k_hi[q, m_, :]).rearrange("p (o s) -> p o s", o=1).broadcast_to([32, 2, BATCH * KV]),
                            pair[q, :].rearrange("p (h o) -> p h o", o=1).broadcast_to([32, 2, BATCH * KV]),
                            ALU.mult), sem("attn_kaug_hi"))
                        for i in range(2):
                            kaug_lo = act.do(lambda e, q=q, h=h0 + i, m_=m_, i=i: e.activation(
                                kaug[32:64, h, :, :].rearrange("p b s -> p (b s)"), f(k_lo[q, m_, :]), ACT.Copy,
                                scale=pair[q, i:i + 1]), sem("attn_kaug_lo"))
                sp.wait(kaug_hi)
                kaug_hi2 = sp.do(lambda e: e.dma_start(f(kaug[64:96, :, :, :]), f(kaug[0:32, :, :, :])),
                                 sem("attn_kaug_hi2"), 16)
                run(first)
                act.wait(ones16_done)
                spread_done = act.do(lambda e: e.activation(spread[:], ones16[:], ACT.Copy), sem("attn_spread"))
                kaug_ones = act.do(lambda e: e.activation(
                    kaug[96:96 + H, :, :, :].rearrange("p h b s -> p h (b s)"),
                    ident[96:96 + H, 96:96 + H].rearrange("p (h o) -> p h o", o=1).broadcast_to([H, H, BATCH * KV]),
                    ACT.Copy), sem("attn_kaug_ones"))
                kaug_done = [kaug_ones, kaug_lo, kaug_hi2]
                interleave((maxima(0), 2), (norm(1), 1))
                for b in range(2):
                    pad(b)

                none = iter(())
                OVER, OVER_END = 6, 8
                full = []
                for g in range(NG + 1):
                    over_at = OVER_END if g == NG - 1 else OVER
                    queries, tops = (query(g + 1), maxima(g + 1)) if g + 1 < NG else (none, none)
                    second = norm(g + 2) if g + 2 < NG else none
                    over, rest = (normalise(g - 1), back(g - 1)) if g > 0 else (none, none)
                    for h in range(H):
                        if g < NG:
                            score(g, h)
                        if h == 3:
                            next(over, None)
                        if h <= 4:
                            next(queries, None)
                        if h >= 4 and h != 12:
                            next(tops, None)
                        if over_at <= h < over_at + 2 * NV:
                            next(over, None)
                        if h in (0, 1, 2, 12, 14):
                            next(second, None)
                        k = g * H + h - LAG
                        if 0 <= k < NG * H:
                            values(k // H, k % H)
                            for c, (h0, h1) in enumerate(VC):
                                if k % H == h1 - 1:
                                    full.append((k // H, c))
                        while full and not (g == NG - 1 and (full[0][0], full[0][1]) == (g, 0) and h < OVER_END + 2):
                            unload(*full.pop(0))
                        if h in (13, 15):
                            next(rest, None)
                        if h == LAG and 0 < g < NG and g * GN % SEQ == 0 and g * GN // SEQ + 1 < BATCH:
                            pad(g * GN // SEQ + 1)
                    run(second)
                end_phase()
            return [[M["x", g]] for g in range(NG)]

        def experts_swiglu(xr):
            st = ExitStack()
            with st:
                n = "e0_"
                score = sb(st, n + "score", [P, NT, E0])
                slot = sb(st, n + "slot", [P, NT, E0])
                acc_in = []
                with ExitStack() as s2:
                    work = Banks([bank[i] for i in range(3)])
                    xn = sb(s2, n + "xn", [P, NT, D])
                    ln_tmp = (sb(s2, n + "stats", [P, 2, GT, 6]), sb(s2, n + "mv", [P, 2, GT, 2]),
                              sb(s2, n + "rstd", [P, 2, 2, GT]))
                    xT = [sb(s2, n + f"xT{i}", [P, DC, GN]) for i in range(2)]
                    wg = sb(s2, n + "wg", [P, DC, E0])
                    lg = sb(s2, n + "lg", [P, NT, E0])
                    pr = sb(s2, n + "pr", [P, NT, E0])
                    red = sb(s2, n + "red", [P, 3, NT])
                    s_gate = sem(n + "gate")
                    wg_in = sp.do(lambda e: e.dma_start(wg[:], A["L0_ffn_wg"].rearrange("(c p) n -> p c n", p=P)),
                                  sem(n + "wg"), 16)
                    logits = bank[7]
                    xT_used = [None, None]
                    normed, xn_outs = {}, []

                    def norm(g):
                        ts = slice(g * GT, (g + 1) * GT)
                        sp.wait(*xr[g])
                        acc_in.append(sp.do(lambda e: e.dma_start(rows(acc_d)[:, ts, :], x_sb[:, ts, :]),
                                            sem(f"x_io{g}"), 16))
                        normed[g] = yield from layernorm_steps(g, ln_tmp, xn[:, ts, :], xr[g], [])
                        sp.wait(normed[g])
                        xn_outs.append(sp.do(lambda e: e.dma_start(rows(xn_d)[:, ts, :], xn[:, ts, :]),
                                             sem("xn_out"), 16))

                    def turned(g):
                        for c in range(DC):
                            i, w, bf = work.take()
                            pe.wait(bf, normed[g])
                            for j in range(GT):
                                m = pe.do(lambda e, w=w, c=c, j=j: e.transpose(
                                    w[:, j * P:(j + 1) * P], xn[:, g * GT + j, c * P:(c + 1) * P], ident[:, :]),
                                    sem(n + "xT_p") if j == GT - 1 else None)
                            act.wait(m, xT_used[g % 2])
                            m = act.do(lambda e, w=w, c=c: e.activation(xT[g % 2][:, c, :], w[:, :], ACT.Copy),
                                       sem(n + "xT"))
                            work.release(i, m)
                            xT_done[g] = m

                    def products(g):
                        pe.wait(xT_done[g], wg_in)
                        for j in range(GT):
                            t = g * GT + j
                            for c in range(DC):
                                m = pe.do(lambda e, c=c, j=j, t=t: e.matmul(
                                    logits[:, t * E0:(t + 1) * E0], xT[g % 2][:, c, j * P:(j + 1) * P], wg[:, c, :],
                                    start=(c == 0), stop=(c == DC - 1)), sem(n + "logits"))
                        xT_used[g % 2] = m
                        return m

                    xT_done = {}
                    ahead = norm(0)
                    for _ in range(3):
                        next(ahead)
                    for g in range(NG):
                        now, ahead = ahead, norm(g + 1) if g + 1 < NG else iter(())
                        for _ in range(3):
                            next(ahead, None)
                        run(now)
                        turned(g)
                        if g > 0:
                            products(g - 1)
                    m = products(NG - 1)
                    xn_out = xn_outs[-1]

                    def bc(k):
                        return red[:, k, :].rearrange("p (t o) -> p t o", o=1).broadcast_to([P, NT, E0])

                    lgv = logits[:, 0:NT * E0].rearrange("p (t e) -> p t e", e=E0)
                    dve.wait(m)
                    m = dve.do(lambda e: e.tensor_reduce(red[:, 0, :], lgv, AX_X, ALU.max), s_gate)
                    dve.wait(m)
                    m = dve.do(lambda e: e.tensor_tensor(lg[:], lgv, bc(0), ALU.subtract), s_gate)
                    act.wait(m)
                    m = act.do(lambda e: e.activation(lg[:], lg[:], ACT.Exp), sem(n + "exp"))
                    dve.wait(m)
                    m = dve.do(lambda e: e.tensor_reduce(red[:, 1, :], lg[:], AX_X, ALU.add), s_gate)
                    dve.wait(m)
                    m = dve.do(lambda e: e.reciprocal(red[:, 2, :], red[:, 1, :]), s_gate)
                    dve.wait(m)
                    m = dve.do(lambda e: e.tensor_tensor(pr[:], lg[:], bc(2), ALU.mult), s_gate)
                    select_tokens(s2, n, pr, score, slot, m)
                    end_phase()

                ffn_blocks(st, n, score, slot, xn_out, acc_in)
                end_phase()

        NCH = P // E0
        CHT = NT // NCH
        CHN = CHT * P

        def select_tokens(s2, n, pr, score, slot, ready):
            s = sem(n + "sel")
            cb = Banks([bank[3], bank[4]])
            prc = sb(s2, n + "prc", [P, CHT, E0, NCH])
            prT = sb(s2, n + "prT", [P, CHN])
            junk = sb(s2, n + "junk", [P, 3, CHN])
            cnt = sb(s2, n + "cnt", [P, 3])
            reach = sb(s2, n + "reach", [P, 3])
            found = sb(s2, n + "found", [P, 1], I32)
            cand = sb(s2, n + "cand", [P, 3], I32)
            digit = sb(s2, n + "digit", [P, 1])
            digit_i = sb(s2, n + "digit_i", [P, 1], I32)
            steps = sb(s2, n + "steps", [P, 15, 3], I32)
            same = sb(s2, n + "same", [P, E0, NCH])
            before = sb(s2, n + "before", [P, E0, NCH])
            eq = sb(s2, n + "eq", [P, CHN])
            gt = sb(s2, n + "gt", [P, CHN])
            rank = sb(s2, n + "rank", [P, CHN])
            zeros = sb(s2, n + "zeros", [P, CHN])
            tot = sb(s2, n + "tot", [P, 4])

            k = sem(n + "selc")
            m = pool.do(lambda e: e.memset(same[:], 1.0), k)
            m = pool.do(lambda e: e.memset(zeros[:], 0.0), k)
            pool.wait(m)
            for sgn, base in ((1, 0), (-1, NCH - 1)):
                m = pool.do(lambda e, sgn=sgn, base=base: e.affine_select(
                    out=same[:], in_=same[:], compare_op=ALU.is_ge, fill=0.0, base=base,
                    pattern=[[-sgn * NCH, E0], [0, NCH]], channel_multiplier=sgn), k)
                pool.wait(m)
            m = pool.do(lambda e: e.affine_select(out=before[:], in_=same[:], compare_op=ALU.is_gt, fill=0.0, base=0,
                                                  pattern=[[NCH, E0], [1, NCH]], channel_multiplier=-1), k)
            for b in range(15):
                for v in range(3):
                    m = pool.do(lambda e, b=b, v=v: e.memset(steps[:, b, v:v + 1], (v + 1) << 2 * b), k)
            consts = m
            same2, before2 = same[:].rearrange("p e c -> p (e c)"), before[:].rearrange("p e c -> p (e c)")

            dve.wait(ready)
            m = dve.do(lambda e: e.tensor_copy(prc[:].rearrange("p j e c -> p e c j"),
                                               pr[:].rearrange("p (c j) e -> p e c j", j=CHT)), s)
            pe.wait(m)
            i, w, bf = cb.take()
            for j in range(CHT):
                m = pe.do(lambda e, w=w, j=j: e.transpose(w[:, j * P:(j + 1) * P],
                                                          prc[:, j, :, :].rearrange("p e c -> p (e c)"), ident[:, :]),
                          sem(n + "selp"))
            dve.wait(m, consts)
            m = dve.do(lambda e, w=w: e.tensor_copy(prT[:], w[:, 0:CHN]), s)
            cb.release(i, m)
            dve.wait(m)
            dve.do(lambda e: e.tensor_copy(cand[:], steps[:, 14, :]), s)
            m = dve.do(lambda e: e.memset(found[:], 0), s)
            for b in range(14, -1, -1):
                dve.wait(m)
                for v in range(3):
                    m = dve.do(lambda e, v=v: e.tensor_scalar(junk[:, v, :], prT[:], cand[:, v:v + 1].bitcast(F32), None,
                                                              ALU.is_ge, ALU.add, accum_out=cnt[:, v:v + 1]), s)
                i, w, bf = cb.take()
                pe.wait(m, bf)
                m = pe.do(lambda e, w=w: e.matmul(w[:, 0:3], same2, cnt[:], start=True, stop=True), sem(n + "selp"))
                dve.wait(m)
                m = dve.do(lambda e, w=w: e.tensor_scalar(reach[:], w[:, 0:3], float(CAP), None, ALU.is_ge, ALU.add,
                                                          accum_out=digit[:]), s)
                cb.release(i, m)
                dve.wait(m)
                m = dve.do(lambda e, b=b: e.tensor_scalar(digit_i[:], digit[:], float(1 << 2 * b), None, ALU.mult), s)
                dve.wait(m)
                if b:
                    m = dve.do(lambda e, b=b: e.scalar_tensor_tensor(
                        out=cand[:], in0=steps[:, b - 1, :], scalar=digit_i[:], in1=found[:].broadcast_to([P, 3]),
                        op0=ALU.bitwise_or, op1=ALU.bitwise_or), s)
                    dve.wait(m)
                m = dve.do(lambda e: e.tensor_tensor(found[:], digit_i[:], found[:], ALU.bitwise_or), s)
            thr = found[:].bitcast(F32)
            dve.wait(m)
            dve.do(lambda e: e.tensor_scalar(gt[:], prT[:], thr, None, ALU.is_gt, ALU.add, accum_out=tot[:, 0:1]), s)
            m = dve.do(lambda e: e.tensor_scalar(eq[:], prT[:], thr, None, ALU.is_equal, ALU.add,
                                                 accum_out=tot[:, 1:2]), s)
            i, w, bf = cb.take()
            pe.wait(m, bf)
            pe.do(lambda e, w=w: e.matmul(w[:, 0:1], same2, tot[:, 0:1], start=True, stop=True))
            m1 = pe.do(lambda e, w=w: e.matmul(w[:, 1:2], before2, tot[:, 1:2], start=True, stop=True),
                       sem(n + "selp"))
            dve.wait(m)
            m = dve.do(lambda e: e.tensor_tensor_scan(rank[:], eq[:], zeros[:], 0.0, ALU.add, ALU.add), s)
            dve.wait(m1)
            m2 = dve.do(lambda e, w=w: e.tensor_copy(tot[:, 2:4], w[:, 0:2]), s)
            cb.release(i, m2)
            dve.wait(m2)
            m = dve.do(lambda e: e.tensor_tensor(tot[:, 0:1], tot[:, 2:3], tot[:, 3:4], ALU.add), s)
            dve.wait(m)
            m = dve.do(lambda e: e.tensor_scalar(rank[:], rank[:], tot[:, 0:1], float(CAP), ALU.add, ALU.is_le), s)
            dve.wait(m)
            m = dve.do(lambda e: e.tensor_tensor(eq[:], eq[:], rank[:], ALU.mult), s)
            dve.wait(m)
            m = dve.do(lambda e: e.tensor_tensor(gt[:], gt[:], eq[:], ALU.add), s)
            dve.wait(m)
            m = dve.do(lambda e: e.tensor_tensor_scan(rank[:], gt[:], zeros[:], 0.0, ALU.add, ALU.add), s)
            pe.wait(m)
            i, w, bf = cb.take()
            pe.wait(bf)
            m1 = pe.do(lambda e, w=w: e.matmul(w[:, 0:1], before2, rank[:, CHN - 1:CHN], start=True, stop=True),
                       sem(n + "selp"))
            m = dve.do(lambda e: e.tensor_tensor(prT[:], prT[:], gt[:], ALU.mult), s)
            dve.wait(m1)
            m2 = dve.do(lambda e, w=w: e.tensor_copy(tot[:, 0:1], w[:, 0:1]), s)
            cb.release(i, m2)
            dve.wait(m2)
            m2 = dve.do(lambda e: e.scalar_tensor_tensor(out=rank[:], in0=rank[:], scalar=tot[:, 0:1], in1=gt[:],
                                                         op0=ALU.add, op1=ALU.mult), s)
            for src, dst, off, done in ((prT, score, 0.0, m), (rank, slot, -1.0, m2)):
                i, w, bf = cb.take()
                pe.wait(bf, done)
                for j in range(CHT):
                    m = pe.do(lambda e, w=w, j=j, src=src: e.transpose(w[:, j * P:(j + 1) * P],
                                                                       src[:, j * P:(j + 1) * P], ident[:, :]),
                              sem(n + "selp"))
                dve.wait(m)
                m = dve.do(lambda e, w=w, dst=dst, off=off: e.tensor_scalar(
                    dst[:].rearrange("p (c j) e -> p j e c", j=CHT),
                    w[:, 0:CHN].rearrange("p (j e c) -> p j e c", j=CHT, e=E0), off, None, ALU.add), s)
                cb.release(i, m)

        def ffn_blocks(st, n, score, slot, xn_out, acc_in):
            tb, ab, yb, lb = Banks(bank[0:2]), Banks(bank[2:5]), Banks(bank[5:7]), Banks(bank[7:8])
            HCH = HID0 // P
            ST = CAP // P
            NBE = ST // GT
            NB = E0 * NBE
            LT = 8
            xg = [sb(st, n + f"xg{i}", [P, GT, D]) for i in range(3)]
            xs = sb(st, n + "xs", [P, GT, D])
            xT = [(sb(st, n + f"xs_hi{i}", [P, DC, GN], F32R), sb(st, n + f"xs_lo{i}", [P, DC, GN], F32R))
                  for i in range(2)]
            hT = [(sb(st, n + f"h_hi{i}", [P, HCH, GN], F32R), sb(st, n + f"h_lo{i}", [P, HCH, GN], F32R))
                  for i in range(2)]
            silu = [sb(st, n + f"silu{i}", [P, GN]) for i in range(2)]
            h32 = [sb(st, n + f"h32_{i}", [P, GN]) for i in range(2)]
            y_sb = [sb(st, n + f"y{i}", [P, GT, D]) for i in range(2)]
            cols = (DC * HID0, DC * HID0, HCH * D)
            stage = sb(st, n + "stage", [P, sum(cols)])
            wts = [(sb(st, n + f"w_hi{i}", [P, sum(cols)], F32R), sb(st, n + f"w_lo{i}", [P, sum(cols)], F32R))
                   for i in range(2)]
            iota_row = sb(st, n + "iota_row", [P, P])
            tok_id = sb(st, n + "tok_id", [P, NT])
            slot_i = sb(st, n + "slot_i", [P, NT, E0], I32)
            slot_col = sb(st, n + "slot_col", [P, NT, E0], I32)
            slot_row = sb(st, n + "slot_row", [P, NT, E0], I32)
            in_col = sb(st, n + "in_col", [P, NT, ST])
            score_hi = sb(st, n + "score_hi", [P, NT], F32R)
            score_lo = sb(st, n + "score_lo", [P, NT])
            payload = sb(st, n + "payload", [P, NT, 3, ST], F32R)
            in_row = [sb(st, n + f"in_row{i}", [P, LT, P], F32R) for i in range(2)]
            ids = sb(st, n + "ids", [P, E0, ST], I32)
            weight = sb(st, n + "weight", [P, E0, ST])
            M = {}

            def mark(*k):
                return M.get(k)

            s_iota = sem(n + "iota")
            pool.do(lambda q: q.iota(iota_row[:], [[1, P]], base=0, channel_multiplier=0,
                                     allow_small_or_imprecise_dtypes=True), s_iota)
            iota_done = pool.do(lambda q: q.iota(tok_id[:], [[P, NT]], base=0, channel_multiplier=1,
                                                 allow_small_or_imprecise_dtypes=True), s_iota)
            s_list = sem(n + "list")
            m = dve.do(lambda q: q.tensor_copy(slot_i[:], slot[:]), s_list)
            dve.wait(m)
            dve.do(lambda q: q.tensor_scalar(slot_row[:], slot_i[:], P - 1, None, ALU.bitwise_and), s_list)
            slots_done = dve.do(lambda q: q.tensor_scalar(slot_col[:], slot_i[:], 7, None, ALU.arith_shift_right),
                                s_list)

            def over_cols(a):
                return a.rearrange("p (t o) -> p t o", o=1).broadcast_to([P, NT, ST])

            def lists(e):
                dve.wait(slots_done, iota_done, mark("list_p", e - 1))
                m = dve.do(lambda q: q.tensor_tensor(
                    in_col[:], over_cols(slot_col[:, :, e]),
                    iota_row[:, 0:ST].rearrange("p (o a) -> p o a", o=1).broadcast_to([P, NT, ST]), ALU.is_equal),
                    s_list)
                m = dve.do(lambda q: q.tensor_copy(score_hi[:], score[:, :, e]), s_list)
                dve.wait(m)
                m = dve.do(lambda q: q.tensor_tensor(score_lo[:], score[:, :, e], f(score_hi[:]), ALU.subtract),
                           s_list)
                dve.wait(m)
                for k, v in enumerate((tok_id[:], f(score_hi[:]), score_lo[:])):
                    m = dve.do(lambda q, k=k, v=v: q.tensor_tensor(payload[:, :, k, :], in_col[:], over_cols(v),
                                                                   ALU.mult), s_list)
                yield
                il, w, bf = lb.take()

                def rows_of(s0):
                    b = s0 // LT % 2
                    dve.wait(mark("in_row_p", b))
                    return dve.do(lambda q: q.tensor_tensor(
                        in_row[b][:], slot_row[:, s0:s0 + LT, e].rearrange("p (t o) -> p t o", o=1)
                        .broadcast_to([P, LT, P]),
                        iota_row[:].rearrange("p (o r) -> p o r", o=1).broadcast_to([P, LT, P]), ALU.is_equal),
                        s_list)

                ahead = rows_of(0)
                yield
                for s0 in range(0, NT, LT):
                    b = s0 // LT % 2
                    now, ahead = ahead, rows_of(s0 + LT) if s0 + LT < NT else None
                    pe.wait(bf, now)
                    for t in range(s0, s0 + LT):
                        m = pe.do(lambda q, w=w, t=t, s0=s0, b=b: q.matmul(
                            w[:, 0:3 * ST], in_row[b][:, t - s0, :], payload[:, t, :, :].rearrange("p k a -> p (k a)"),
                            start=(t == 0), stop=(t == NT - 1)), sem(n + "list_p"))
                    M["in_row_p", b] = m
                    yield
                M["list_p", e] = m
                dve.wait(m)
                M["ids", e] = dve.do(lambda q, w=w: q.tensor_copy(ids[:, e, :], w[:, 0:ST]), s_list)
                m = dve.do(lambda q, w=w: q.tensor_copy(weight[:, e, :], w[:, ST:2 * ST]), s_list)
                dve.wait(m)
                m = dve.do(lambda q, w=w: q.tensor_tensor(weight[:, e, :], w[:, 2 * ST:3 * ST], weight[:, e, :],
                                                          ALU.add), s_list)
                M["weight", e] = m
                lb.release(il, m)
                yield

            def gather(i):
                e, half = divmod(i, NBE)
                pool.wait(xn_out, M["ids", e], mark("xs", i - 3))
                for j in range(GT):
                    a = half * GT + j
                    m = pool.do(lambda q, j=j, a=a: q.indirect_dma_start(
                        out=xg[i % 3][:, j, :], out_offset=None, in_=xn_d,
                        in_offset=bass.IndirectOffsetOnAxis(ap=ids[:, e, a:a + 1], axis=0)),
                        sem(n + f"gather{i % 3}"), 16)
                M["xg", i] = m

            def weights(e):
                at = 0
                for k, name in enumerate(("w1", "w3", "w2")):
                    src = A["L0_ffn_" + name][e].rearrange("(c p) n -> p c n", p=P)
                    dst = stage[:, at:at + cols[k]].rearrange("p (c n) -> p c n", c=src.shape[1])
                    sp.wait(mark("w", e - 1, k))
                    arrived = sp.do(lambda q, dst=dst, src=src: q.dma_start(dst, src), sem(n + "stage" + name), 16)
                    hi, lo = (t[:, at:at + cols[k]] for t in wts[e % 2])
                    raw = stage[:, at:at + cols[k]]
                    act.wait(arrived, mark("y_p", (e - 1) * NBE - 1))
                    m = act.do(lambda q, hi=hi, raw=raw: q.activation(hi, raw, ACT.Copy), sem(n + "w_hi"))
                    pool.wait(m)
                    M["w", e, k] = pool.do(lambda q, hi=hi, lo=lo, raw=raw: q.tensor_tensor(lo, raw, f(hi),
                                                                                           ALU.subtract), sem(n + "w"))
                    at += cols[k]
                    yield

            def wview(e, k, part):
                at = sum(cols[:k])
                return wts[e % 2][part][:, at:at + cols[k]].rearrange("p (c n) -> p c n", n=HID0 if k < 2 else D)

            def load(i):
                e, half = divmod(i, NBE)
                dve.wait(M["xg", i], M["weight", e], mark("xT", i - 1))
                for j in range(GT):
                    m = dve.do(lambda q, j=j: q.tensor_scalar(xs[:, j, :], xg[i % 3][:, j, :],
                                                              weight[:, e, half * GT + j:half * GT + j + 1], None,
                                                              ALU.mult), sem(n + "xs"))
                M["xs", i] = m
                yield
                m = yield from transpose_split(tb, xs, m, xT[i % 2][0], xT[i % 2][1], [mark("h_p", i - 2)], n + "x")
                M["xT", i] = m

            def hidden(i):
                e = i // NBE
                x_hi, x_lo = xT[i % 2]
                h_hi, h_lo = hT[i % 2]
                for m_ in range(HCH):
                    ia, wa, fa = ab.take()
                    ib, wb, fb = ab.take()
                    ws = slice(m_ * P, (m_ + 1) * P)
                    for k, w, bf in ((0, wa, fa), (1, wb, fb)):
                        pe.wait(bf, M["xT", i], M["w", e, k])
                        for c in range(DC):
                            m = matmul3(w[:, :], wview(e, k, 0)[:, c, ws], wview(e, k, 1)[:, c, ws], x_hi[:, c, :],
                                        x_lo[:, c, :], c == 0, c == DC - 1, sem(n + "h_p"))
                        if k == 0:
                            act.wait(m, mark("h32", i, m_ - 2) if m_ > 1 else mark("h32", i - 1, m_ + HCH - 2))
                            ms = act.do(lambda q, w=w, m_=m_: q.activation(silu[m_ % 2][:], w[:, :], ACT.Silu),
                                        sem(n + "silu"))
                            ab.release(ia, ms)
                    M["h_p", i] = m
                    dve.wait(m, ms, mark("h_hi", i, m_ - 2) if m_ > 1 else mark("h_hi", i - 1, m_ + HCH - 2))
                    m = dve.do(lambda q, w=wb, m_=m_: q.tensor_tensor(h32[m_ % 2][:], silu[m_ % 2][:], w[:, :],
                                                                     ALU.mult), sem(n + "h32"))
                    ab.release(ib, m)
                    M["h32", i, m_] = m
                    act.wait(m, mark("y_p", i - 2))
                    m = act.do(lambda q, m_=m_: q.activation(h_hi[:, m_, :], h32[m_ % 2][:], ACT.Copy),
                               sem(n + "h_hi"))
                    M["h_hi", i, m_] = m
                    dve.wait(m)
                    m = dve.do(lambda q, m_=m_: q.tensor_tensor(h_lo[:, m_, :], h32[m_ % 2][:],
                                                               f(h_hi[:, m_, :]), ALU.subtract), sem(n + "h_lo"))
                    M["h", i] = m
                    yield

            def output(i):
                e, half = divmod(i, NBE)
                h_hi, h_lo = hT[i % 2]
                for j in range(GT):
                    iy, w, bf = yb.take()
                    ts = slice(j * P, (j + 1) * P)
                    pe.wait(bf, M["h", i], M["w", e, 2])
                    for c in range(HCH):
                        m = matmul3(w[:, 0:D], h_hi[:, c, ts], h_lo[:, c, ts], wview(e, 2, 0)[:, c, :],
                                    wview(e, 2, 1)[:, c, :], c == 0, c == HCH - 1, sem(n + "y_p"))
                    M["y_p", i] = m
                    act.wait(m, mark("scatter", i - 2))
                    m = act.do(lambda q, w=w, j=j: q.activation(y_sb[i % 2][:, j, :], w[:, 0:D], ACT.Copy),
                               sem(n + "y"))
                    yb.release(iy, m)
                    M["y", i, j] = m
                    yield

            def scatter(i):
                e, half = divmod(i, NBE)
                pool.wait(*acc_in, mark("scatter", e * NBE - 1), mark("scatter", e * NBE - 2))
                for j in range(GT):
                    a = half * GT + j
                    pool.wait(M["y", i, j])
                    m = pool.do(lambda q, j=j, a=a: q.indirect_dma_start(
                        out=acc_d, out_offset=bass.IndirectOffsetOnAxis(ap=ids[:, e, a:a + 1], axis=0),
                        in_=y_sb[i % 2][:, j, :], in_offset=None, compute_op=ALU.add), sem(n + f"scatter{i % 2}"), 16)
                M["scatter", i] = m

            interleave((lists(0), 1), (weights(0), 1))
            gather(0)
            gather(1)
            run(lists(1))
            run(load(0))
            none = iter(())
            listing = none
            for i in range(NB + 1):
                if i + 2 < NB:
                    gather(i + 2)
                if i > 1:
                    scatter(i - 2)
                e, half = divmod(i, NBE)
                if half == 0:
                    run(listing)
                    listing = lists(e + 2) if e + 2 < E0 else none
                ahead = load(i + 1) if i + 1 < NB else none
                now = hidden(i) if i < NB else none
                before = output(i - 1) if i > 0 else none
                next(ahead, None)
                for _ in range(HCH):
                    next(now, None)
                    next(before, None)
                    next(ahead, None)
                    next(listing, None)
                run(ahead)
                if half == 0 and e + 1 < E0:
                    run(weights(e + 1))
            scatter(NB - 1)
            added.extend((M["scatter", NB - 1], M["scatter", NB - 2]))

        def experts_relu(xr):
            n = "e1_"
            NE = E1 + 1
            CB = BLK // P
            NSC = NBLK * CB
            n1, n2 = DC, HID1 // P
            st = ExitStack()
            with st:
                gates = sb(ctx, n + "gates", [P, NT, TOP])
                gather_id = sb(st, n + "gather_id", [P, NSC], I32)
                scatter_id = sb(st, n + "scatter_id", [P, NSC], I32)
                block_expert = sb(st, n + "block_expert", [1, NBLK], I32)
                bias = sb(st, n + "bias", [P, 2, D], F32R)
                pick = sb(st, n + "pick", [P, NBLK + 1], F32R)
                row_expert = sb(st, n + "row_expert", [P, 1])
                row_i = sb(st, n + "row_i", [P, 1], I32)
                w_hi = sb(st, n + "w_hi", [P, E1, n1 + n2, D], F32R)
                w_lo = sb(st, n + "w_lo", [P, E1, n1 + n2, D], F32R)
                logit = sb(st, n + "logit", [P, NT, E1])
                M = {}

                def mark(*k):
                    return M.get(k)

                with ExitStack() as s2:
                    tb, hb, yb = Banks(bank[0:2]), Banks(bank[2:4]), Banks(bank[4:6] + bank[7:8])
                    rbk = Banks(bank[6:7])
                    ln_tmp = (sb(s2, n + "stats", [P, 2, GT, 6]), sb(s2, n + "mv", [P, 2, GT, 2]),
                              sb(s2, n + "rstd", [P, 2, 2, GT]))
                    xn = [sb(s2, n + f"xn{i}", [P, GT, D]) for i in range(2)]
                    x32 = sb(s2, n + "x32", [P, DC, GN])
                    x_hi, x_lo = sb(s2, n + "x_hi", [P, DC, GN], F32R), sb(s2, n + "x_lo", [P, DC, GN], F32R)
                    h32 = sb(s2, n + "h32s", [P, GN])
                    h_hi, h_lo = sb(s2, n + "hs_hi", [P, n2, GN], F32R), sb(s2, n + "hs_lo", [P, n2, GN], F32R)
                    sw_hi, sw_lo = (sb(s2, n + "sw_" + k, [P, n1 + n2, D], F32R) for k in ("hi", "lo"))
                    sb1 = sb(s2, n + "sb1", [P, n2])
                    stage = [sb(s2, n + f"stage{i}", [P, n1 + n2, D]) for i in range(2)]
                    braw = xn[1][0:2 * NE, 0:2, :]
                    blo = h_lo[0:2 * NE, 0, :].rearrange("p (k n) -> p k n", k=2)
                    rw = sb(s2, n + "rw", [P, DC, E1])
                    rb = sb(s2, n + "rb", [P, E1])
                    def fetch(k):
                        b = k % 2
                        src1, src2 = ((A["L1_ffn_sW1"], A["L1_ffn_sW2"]) if k == 0 else
                                      (A["L1_ffn_eW1"][k - 1], A["L1_ffn_eW2"][k - 1]))
                        sp.wait(mark("w", k - 2))
                        sp.do(lambda e: e.dma_start(stage[b][:, 0:n1, :], src1.rearrange("(c p) n -> p c n", p=P)),
                              sem(n + f"stage{b}"), 16)
                        M["stage", k] = sp.do(lambda e: e.dma_start(stage[b][:, n1:, :],
                                                                    src2.rearrange("(c p) n -> p c n", p=P)),
                                              sem(n + f"stage{b}"), 16)

                    def split(k):
                        b = k % 2
                        hi, lo = (sw_hi[:], sw_lo[:]) if k == 0 else (w_hi[:, k - 1, :, :], w_lo[:, k - 1, :, :])
                        act.wait(M["stage", k])
                        m = act.do(lambda e: e.activation(hi, stage[b][:], ACT.Copy), sem(n + "w_hi"))
                        pool.wait(m)
                        M["w", k] = pool.do(lambda e: e.tensor_tensor(lo, stage[b][:], f(hi), ALU.subtract),
                                            sem(n + "w_lo"))

                    def norm(g):
                        m = yield from layernorm_steps(g, ln_tmp, xn[g % 2], xr[g],
                                                       [mark("xT_p", g - 2), mark("xn_out", g - 2), mark("braw")])
                        M["ln", g] = m

                    def turned(g):
                        b = g % 2
                        ln = M["ln", g]
                        sp.wait(ln)
                        M["xn_out", g] = sp.do(lambda e: e.dma_start(rows(xn_d)[:, g * GT:(g + 1) * GT, :], xn[b][:]),
                                               sem(f"xn_io{b}"), 16)
                        for c in range(DC):
                            i, w, bf = tb.take()
                            pe.wait(bf, ln)
                            for j in range(GT):
                                m = pe.do(lambda e, w=w, c=c, j=j: e.transpose(
                                    w[:, j * P:(j + 1) * P], xn[b][:, j, c * P:(c + 1) * P], ident[:, :]),
                                    sem(n + "xT_p") if j == GT - 1 else None)
                            M["xT_p", g] = m
                            act.wait(m, mark("logit_p", g - 1), mark("x_lo", g - 1))
                            m = act.do(lambda e, w=w, c=c: e.activation(x32[:, c, :], w[:, :], ACT.Copy),
                                       sem(n + "x32"))
                            tb.release(i, m)
                            act.wait(m, mark("hs_p", g - 1))
                            M["x_hi", g] = act.do(lambda e, c=c: e.activation(x_hi[:, c, :], x32[:, c, :], ACT.Copy),
                                                  sem(n + "x_hi"))
                            M["x_hi", g, c] = M["x_hi", g]
                            yield
                        for c in range(DC):
                            dve.wait(M["x_hi", g, c])
                            M["x_lo", g] = dve.do(lambda e, c=c: e.tensor_tensor(
                                x_lo[:, c, :], x32[:, c, :], f(x_hi[:, c, :]), ALU.subtract), sem(n + "x_lo"))
                            yield
                        i, w, bf = rbk.take()
                        pe.wait(M["x_hi", g], rw_in, bf)
                        for j in range(GT):
                            for c in range(DC):
                                m = pe.do(lambda e, w=w, c=c, j=j: e.matmul(
                                    w[:, j * E1:(j + 1) * E1], x32[:, c, j * P:(j + 1) * P], rw[:, c, :],
                                    start=(c == 0), stop=(c == DC - 1)), sem(n + "logit_p"))
                        M["logit_p", g] = m
                        dve.wait(m, rb_in)
                        m = dve.do(lambda e, w=w: e.tensor_tensor(
                            logit[:, g * GT:(g + 1) * GT, :], w[:, 0:GT * E1].rearrange("p (t e) -> p t e", e=E1),
                            rb[:].rearrange("p (o e) -> p o e", o=1).broadcast_to([P, GT, E1]), ALU.add),
                            sem(n + "logit"))
                        M["logit", g] = m
                        rbk.release(i, m)
                        yield

                    def shared(g):
                        for m_ in range(n2):
                            i, w, bf = hb.take()
                            ws = slice(m_ * P, (m_ + 1) * P)
                            pe.wait(bf, M["x_lo", g], M["w", 0])
                            for c in range(n1):
                                m = matmul3(w[:, :], sw_hi[:, c, ws], sw_lo[:, c, ws], x_hi[:, c, :], x_lo[:, c, :],
                                            c == 0, c == n1 - 1, sem(n + "hs_p"))
                            M["hs_p", g] = m
                            act.wait(m, sb1_in, mark("hs_lo", g, m_ - 1) or mark("hs_lo", g - 1, n2 - 1))
                            m = act.do(lambda e, w=w, m_=m_: e.activation(h32[:], w[:, :], ACT.Relu,
                                                                         bias=sb1[:, m_:m_ + 1]), sem(n + "hs"))
                            hb.release(i, m)
                            act.wait(m, mark("ys_p", g - 1))
                            m = act.do(lambda e, m_=m_: e.activation(h_hi[:, m_, :], h32[:], ACT.Copy), sem(n + "hs_hi"))
                            dve.wait(m, bias_done)
                            m = dve.do(lambda e, m_=m_: e.tensor_tensor(h_lo[:, m_, :], h32[:], f(h_hi[:, m_, :]),
                                                                       ALU.subtract), sem(n + "hs_lo"))
                            M["hs_lo", g, m_] = m
                            yield
                        for j in range(GT):
                            i, w, bf = yb.take()
                            ts = slice(j * P, (j + 1) * P)
                            pe.wait(bf, M["hs_lo", g, n2 - 1], bias_done, pick_done)
                            pe.do(lambda e, w=w: e.matmul(w[:, 0:D], pick[:, NBLK:].broadcast_to([P, P]), bias[:, 1, :],
                                                          start=True, stop=False))
                            for c in range(n2):
                                m = matmul3(w[:, 0:D], h_hi[:, c, ts], h_lo[:, c, ts], sw_hi[:, n1 + c, :],
                                            sw_lo[:, n1 + c, :], False, c == n2 - 1, sem(n + "ys_p"))
                            M["ys_p", g] = m
                            t = g * GT + j
                            dve.wait(m, M["xn_out", g])
                            m = dve.do(lambda e, w=w, t=t: e.tensor_tensor(x_sb[:, t, :], w[:, 0:D], x_sb[:, t, :],
                                                                          ALU.add), sem(n + "xs"))
                            M["x", g] = m
                            yb.release(i, m)
                            yield

                    fetch(0)
                    fetch(1)
                    rw_in = sp.do(lambda e: e.dma_start(rw[:], A["L1_ffn_router_W"].rearrange("(c p) n -> p c n", p=P)),
                                  sem(n + "rw"), 16)
                    rb_in = sp.do(lambda e: e.dma_start(rb[:], A["L1_ffn_router_b"].rearrange("(a n) -> a n", a=1)
                                                        .broadcast_to([P, E1])), sem(n + "rb"), 16)
                    sb1_in = sp.do(lambda e: e.dma_start(sb1[:], A["L1_ffn_sb1"]), sem(n + "sb1"), 16)
                    s_b = sem(n + "b_in")
                    for r in (0, NE):
                        sp.do(lambda e, r=r: e.dma_start(braw[r:r + E1, 0, :], A["L1_ffn_eb1"]), s_b, 16)
                        sp.do(lambda e, r=r: e.dma_start(braw[r:r + E1, 1, :], A["L1_ffn_eb2"]), s_b, 16)
                        for k in range(2):
                            b_in = sp.do(lambda e, r=r, k=k: e.dma_start(
                                braw[r + E1:r + NE, k, :], A["L1_ffn_sb2"].rearrange("(a n) -> a n", a=1)), s_b, 16)
                    run(norm(0))
                    m = dve.do(lambda e: e.memset(f(bias[:]), 0.0), sem(n + "b"))
                    dve.wait(b_in, m)
                    m = dve.do(lambda e: e.tensor_copy(bias[0:2 * NE, :, :], braw), sem(n + "b"))
                    dve.wait(m)
                    m = M["braw",] = dve.do(lambda e: e.tensor_tensor(blo, braw, f(bias[0:2 * NE, :, :]), ALU.subtract),
                                           sem(n + "b"))
                    sp.wait(m)
                    bias_done = sp.do(lambda e: e.dma_start(f(bias[NE:2 * NE, :, :]), f(blo[NE:2 * NE, :, :])),
                                      sem(n + "bias"), 16)
                    m = pool.do(lambda e: e.iota(row_i[:], [[0, 1]], base=0, channel_multiplier=1), sem(n + "row"))
                    dve.wait(m)
                    m = dve.do(lambda e: e.tensor_scalar(row_i[:], row_i[:], NE - 1, None, ALU.bitwise_and),
                               sem(n + "b"))
                    dve.wait(m)
                    m = dve.do(lambda e: e.memset(row_expert[:], -1.0), sem(n + "b"))
                    dve.wait(m)
                    m = dve.do(lambda e: e.tensor_copy(row_expert[0:2 * NE, :], row_i[0:2 * NE, :]), sem(n + "b"))
                    dve.wait(m)
                    pick_done = dve.do(lambda e: e.tensor_scalar(pick[:, NBLK:NBLK + 1], row_expert[:], float(E1), None,
                                                                 ALU.is_equal), sem(n + "b"))
                    ahead = turned(0)
                    for c in range(2 * DC):
                        next(ahead)
                    split(0)
                    run(norm(1))
                    split(1)
                    for g in range(NG):
                        now, router = shared(g), ahead
                        ahead = turned(g + 1) if g + 1 < NG else iter(())
                        second = norm(g + 2) if g + 2 < NG else iter(())
                        for m_ in range(n2):
                            next(now)
                        run(router)
                        for c in range(DC):
                            next(ahead, None)
                        for j, _ in enumerate(now):
                            if j < DC:
                                next(ahead, None)
                            next(second, None)
                        run(second)
                        for k in (2 + 2 * g, 3 + 2 * g):
                            if k <= E1:
                                fetch(k)
                                split(k)
                    end_phase()

                with ExitStack() as s2:
                    route(s2, n, logit, [M["logit", g] for g in range(NG)], gates, gather_id, scatter_id, block_expert,
                          pick, row_expert, NSC)
                    end_phase()

                with ExitStack() as s2:
                    tb, hb, ub, yb = (Banks(bank[2 * k:2 * k + 2]) for k in range(4))
                    xg = [sb(s2, n + f"xg{i}", [P, CB, D]) for i in range(4)]
                    xT = [[sb(s2, n + f"xT{i}_{k}", [P, n1, BLK], F32R) for k in range(2)] for i in range(2)]
                    hidden32 = [sb(s2, n + f"h32_{i}", [P, CB, HID1]) for i in range(2)]
                    hT = [[sb(s2, n + f"hT{i}_{k}", [P, n2, BLK], F32R) for k in range(2)] for i in range(2)]
                    y_sb = [sb(s2, n + f"y{i}", [P, CB, D]) for i in range(3)]
                    expert = {}

                    def gather(i):
                        pool.wait(M["xn_out", NG - 1], M["xn_out", NG - 2], mark("xT_p", "b", i - 4))
                        for j in range(CB):
                            a = i * CB + j
                            m = pool.do(lambda e, j=j, a=a: e.indirect_dma_start(
                                out=xg[i % 4][:, j, :], out_offset=None, in_=xn_d,
                                in_offset=bass.IndirectOffsetOnAxis(ap=gather_id[:, a:a + 1], axis=0)),
                                sem(n + f"gather{i % 4}"), 16)
                        M["xg", i] = m

                    def turn(banks, src, src_ready, dst, free, what, i):
                        k, w, bf = banks.take()
                        pe.wait(bf, src_ready)
                        for c in range(2):
                            for j in range(CB):
                                m = pe.do(lambda e, w=w, c=c, j=j: e.transpose(
                                    w[:, (c * CB + j) * P:(c * CB + j + 1) * P], src[:, j, c * P:(c + 1) * P],
                                    ident[:, :]), sem(n + what + "_p") if c + j == CB else None)
                        M[what + "_p", "b", i] = m
                        act.wait(m, free)
                        flat = "p c n -> p (c n)"
                        m = act.do(lambda e, w=w: e.activation(dst[0][:].rearrange(flat), w[:, :], ACT.Copy),
                                   sem(n + what + "_hi"))
                        dve.wait(m)
                        m = dve.do(lambda e, w=w: e.tensor_tensor(dst[1][:].rearrange(flat), w[:, :],
                                                                  f(dst[0][:].rearrange(flat)), ALU.subtract),
                                   sem(n + what + "_lo"))
                        banks.release(k, m)
                        M[what, i] = m

                    def product(banks, x2, ready, k0, kb, what, i):
                        k, w, bf = banks.take()
                        pe.wait(bf, ready)
                        for j in range(CB):
                            ts = slice(j * P, (j + 1) * P)
                            o = w[:, j * D:(j + 1) * D]

                            def at(t, c):
                                return lambda: t[:, bass.ds(expert[i], 1), k0 + c, :].rearrange("p o n -> p (o n)")

                            pe.do(lambda e, o=o: e.matmul(o, pick[:, i:i + 1].broadcast_to([P, P]), bias[:, kb, :],
                                                          start=True, stop=False))
                            for c in range(2):
                                for part, t in ((0, w_hi), (1, w_hi), (0, w_lo)):
                                    last = c == 1 and t is w_lo
                                    m = pe.do(lambda e, o=o, part=part, ts=ts, c=c, rhs=at(t, c), last=last: e.matmul(
                                        o, x2[part][:, c, ts], rhs(), start=False, stop=last),
                                        sem(n + what) if last and j == CB - 1 else None)
                        M[what, i] = m
                        return k, w, m

                    def hidden(i):
                        k, w, m = product(hb, xT[i % 2], M["xT", i], 0, 0, "h_p", i)
                        act.wait(m, mark("hT_p", "b", i - 2))
                        m = act.do(lambda e, w=w: e.activation(hidden32[i % 2][:].rearrange("p j n -> p (j n)"), w[:, :],
                                                               ACT.Relu), sem(n + "h32"))
                        hb.release(k, m)
                        M["h32", i] = m

                    def output(i):
                        k, w, m = product(yb, hT[i % 2], M["hT", i], n1, 1, "y_p", i)
                        dve.wait(m, mark("scatter", i - 3))
                        m = dve.do(lambda e, w=w: e.tensor_copy(y_sb[i % 3][:].rearrange("p j n -> p (j n)"), w[:, :]),
                                   sem(n + "y"))
                        yb.release(k, m)
                        M["y", i] = m

                    def scatter(i):
                        pool.wait(M["y", i])
                        for j in range(CB):
                            a = i * CB + j
                            m = pool.do(lambda e, j=j, a=a: e.indirect_dma_start(
                                out=plane_d, out_offset=bass.IndirectOffsetOnAxis(ap=scatter_id[:, a:a + 1], axis=0),
                                in_=y_sb[i % 3][:, j, :], in_offset=None, bounds_check=TOP * TOK - 1,
                                oob_is_err=False), sem(n + f"scatter{i % 3}"), 16)
                        M["scatter", i] = m

                    for i in range(3):
                        gather(i)
                    for s in range(-3, NBLK):
                        if s + 6 < NBLK and s + 6 >= 3:
                            gather(s + 6)
                        if 0 <= s + 3 < NBLK:
                            i = s + 3
                            turn(tb, xg[i % 4], M["xg", i], xT[i % 2], mark("h_p", i - 2), "xT", i)
                        if 0 <= s + 2 < NBLK:
                            i = s + 2
                            pe.steps.append(lambda e, i=i: expert.__setitem__(
                                i, e.value_load(block_expert[0:1, i:i + 1], min_val=0, max_val=E1 - 1)))
                            hidden(i)
                        if 0 <= s + 1 < NBLK:
                            i = s + 1
                            turn(ub, hidden32[i % 2], M["h32", i], hT[i % 2], mark("y_p", i - 2), "hT", i)
                        if s >= 0:
                            output(s)
                            scatter(s)
                    end_phase()

            with ExitStack() as s2:
                yc = [sb(s2, n + f"yc{i}", [P, TOP, GT, D]) for i in range(3)]
                sp.wait(*(M["scatter", NBLK - 1 - k] for k in range(3)))
                used, arrived = {}, {}

                def load_choices(g):
                    sp.wait(used.get(g - 3))
                    for k in range(TOP):
                        arrived[g] = sp.do(lambda e, k=k: e.dma_start(
                            yc[g % 3][:, k, :, :], rows(plane_d[k * TOK:(k + 1) * TOK, :])[:, g * GT:(g + 1) * GT, :]),
                            sem(n + f"yc{g % 3}"), 16)

                load_choices(0)
                load_choices(1)
                for g in range(NG):
                    if g + 2 < NG:
                        load_choices(g + 2)
                    dve.wait(arrived[g])
                    for k in range(TOP):
                        for j in range(GT):
                            t = g * GT + j
                            last = dve.do(lambda e, g=g, k=k, j=j, t=t: e.scalar_tensor_tensor(
                                out=x_sb[:, t, :], in0=yc[g % 3][:, k, j, :], scalar=gates[:, t, k:k + 1],
                                in1=x_sb[:, t, :], op0=ALU.mult, op1=ALU.add), sem(n + "sum"))
                        dve.wait(last)
                    used[g] = last
                    act.wait(last)
                    stored.append(act.do(lambda e, g=g: e.dma_start(out_v[:, g * GT:(g + 1) * GT, :],
                                                                    x_sb[:, g * GT:(g + 1) * GT, :]),
                                         sem(f"x_io{g}"), 16))

        def route(s2, n, logit, ready, gates, gather_id, scatter_id, block_expert, pick,
                  row_expert, NSC):
            s = sem(n + "route")
            s_c = sem(n + "route_c")
            last = [None]

            def step(fn, *marks):
                dve.wait(last[0], *marks)
                last[0] = dve.do(fn, s)

            pr, sel, eq, tmp, rank = (sb(s2, n + k, [P, NT, E1]) for k in ("pr", "sel", "eq", "tmp", "rank"))
            sel_e, slot_e, seg_e = (sb(s2, n + k, [P, E1, NT]) for k in ("sel_e", "slot_e", "seg_e"))
            red = sb(s2, n + "red", [P, 4, NT])
            top8 = sb(s2, n + "top8", [P, NT, 8])
            seg = sb(s2, n + "seg", [P, NT, E1])
            lower, all1 = sb(s2, n + "lower", [P, P]), sb(s2, n + "all1", [P, P])
            cnt = sb(s2, n + "cnt", [P, 6, E1])
            cnt_i = sb(s2, n + "cnt_i", [P, E1], I32)
            slot = sb(s2, n + "slot", [P, TOP, NT])
            slot_i, row, col = (sb(s2, n + k, [P, TOP, NT], I32) for k in ("slot_i", "row", "col"))
            rowf, colf, value = (sb(s2, n + k, [P, TOP, NT]) for k in ("rowf", "colf", "value"))
            iota = sb(s2, n + "iota", [P, P])
            blk = sb(s2, n + "blk", [P, NBLK, E1])
            blkf = sb(s2, n + "blkf", [P, 2, NBLK])
            LT = 8
            in_row = [sb(s2, n + f"in_row{i}", [P, LT, P]) for i in range(2)]
            in_col = [sb(s2, n + f"in_col{i}", [P, LT, NSC]) for i in range(2)]
            idf = sb(s2, n + "idf", [P, NSC])

            pool.do(lambda e: e.memset(all1[:], 1.0), s_c)
            pool.do(lambda e: e.memset(seg[:], 1.0), s_c)
            pool.do(lambda e: e.memset(seg_e[:], 1.0), s_c)
            pool.do(lambda e: e.iota(iota[:], [[1, P]], base=0, channel_multiplier=0,
                                     allow_small_or_imprecise_dtypes=True), s_c)
            m = pool.do(lambda e: e.iota(value[:], [[TOK, TOP], [P, NT]], base=-TOP * TOK, channel_multiplier=1,
                                         allow_small_or_imprecise_dtypes=True), s_c)
            pool.wait(m)
            pool.do(lambda e: e.memset(seg[:, :, 0:1], 0.0), s_c)
            pool.do(lambda e: e.memset(seg_e[:, :, 0:1], 0.0), s_c)
            consts = pool.do(lambda e: e.affine_select(out=lower[:], in_=all1[:], compare_op=ALU.is_gt, fill=0.0,
                                                       base=0, pattern=[[1, P]], channel_multiplier=-1), s_c)

            def bc(a):
                return a.rearrange("p (t o) -> p t o", o=1).broadcast_to([P, NT, E1])

            step(lambda e: e.tensor_reduce(red[:, 0, :], logit[:], AX_X, ALU.max), *ready)
            step(lambda e: e.tensor_tensor(tmp[:], logit[:], bc(red[:, 0, :]), ALU.subtract))
            act.wait(last[0])
            m = act.do(lambda e: e.activation(pr[:], tmp[:], ACT.Exp), sem(n + "exp"))
            step(lambda e: e.tensor_reduce(red[:, 1, :], pr[:], AX_X, ALU.add), m)
            step(lambda e: e.reciprocal(red[:, 2, :], red[:, 1, :]))
            step(lambda e: e.tensor_tensor(pr[:], pr[:], bc(red[:, 2, :]), ALU.mult))
            dve.wait(last[0])
            for t in range(NT):
                last[0] = dve.do(lambda e, t=t: e.max(top8[:, t, :], pr[:, t, :]), s)
            thr = top8[:, :, TOP - 1]
            step(lambda e: e.tensor_tensor(sel[:], pr[:], bc(thr), ALU.is_gt), consts)
            step(lambda e: e.tensor_tensor(eq[:], pr[:], bc(thr), ALU.is_equal))
            step(lambda e: e.tensor_reduce(red[:, 3, :], sel[:], AX_X, ALU.add))
            flat = "p t e -> p (t e)"
            step(lambda e: e.tensor_tensor_scan(rank[:].rearrange(flat), seg[:].rearrange(flat),
                                                eq[:].rearrange(flat), 0.0, ALU.mult, ALU.add))
            step(lambda e: e.tensor_tensor(rank[:], rank[:], bc(red[:, 3, :]), ALU.add))
            step(lambda e: e.scalar_tensor_tensor(out=eq[:], in0=rank[:], scalar=float(TOP), in1=eq[:],
                                                  op0=ALU.is_le, op1=ALU.mult))
            step(lambda e: e.tensor_tensor(sel[:], sel[:], eq[:], ALU.add))
            step(lambda e: e.tensor_copy(sel_e[:].rearrange("p e t -> p t e"), sel[:]))
            step(lambda e: e.tensor_tensor_scan(slot_e[:].rearrange("p e t -> p (e t)"),
                                                seg_e[:].rearrange("p e t -> p (e t)"),
                                                sel_e[:].rearrange("p e t -> p (e t)"), 0.0, ALU.mult, ALU.add))
            step(lambda e: e.tensor_copy(cnt[:, 0, :], slot_e[:, :, NT - 1]))
            w = bank[0]
            pe.wait(last[0], consts)
            pe.do(lambda e: e.matmul(w[:, 0:E1], lower[:], cnt[:, 0, :], start=True, stop=True))
            m = pe.do(lambda e: e.matmul(w[:, 16:16 + E1], all1[:], cnt[:, 0, :], start=True, stop=True),
                      sem(n + "route_p"))
            step(lambda e: e.tensor_tensor_scan(rank[:].rearrange(flat), seg[:].rearrange(flat),
                                                sel[:].rearrange(flat), 0.0, ALU.mult, ALU.add))
            step(lambda e: e.tensor_tensor(rank[:], rank[:], sel[:], ALU.mult))
            step(lambda e: e.tensor_scalar(cnt_i[:], w[:, 16:16 + E1], float(BLK - 1), None, ALU.add), m)
            step(lambda e: e.tensor_scalar(cnt_i[:], cnt_i[:], BLK.bit_length() - 1, None, ALU.arith_shift_right))
            step(lambda e: e.tensor_copy(cnt[:, 1, :], cnt_i[:]))
            step(lambda e: e.tensor_tensor_scan(cnt[:, 2, :], all1[:, 0:E1], cnt[:, 1, :], 0.0, ALU.mult, ALU.add))
            step(lambda e: e.tensor_tensor(cnt[:, 3, :], cnt[:, 2, :], cnt[:, 1, :], ALU.subtract))
            step(lambda e: e.tensor_scalar(cnt[:, 4, :], cnt[:, 3, :], float(BLK), -1.0, ALU.mult, ALU.add))
            step(lambda e: e.tensor_tensor(cnt[:, 5, :], w[:, 0:E1], cnt[:, 4, :], ALU.add))
            step(lambda e: e.tensor_tensor(slot_e[:], slot_e[:], cnt[:, 5, :].rearrange("p (e o) -> p e o", o=1)
                                           .broadcast_to([P, E1, NT]), ALU.add))
            step(lambda e: e.tensor_tensor(
                blk[:], iota[:, 0:NBLK].rearrange("p (b o) -> p b o", o=1).broadcast_to([P, NBLK, E1]),
                cnt[:, 2, :].rearrange("p (o e) -> p o e", o=1).broadcast_to([P, NBLK, E1]), ALU.is_ge))
            step(lambda e: e.tensor_reduce(blkf[:, 0, :], blk[:], AX_X, ALU.add))
            step(lambda e: e.tensor_scalar(blkf[:, 1, :], blkf[:, 0, :], float(E1 - 1), None, ALU.min))
            step(lambda e: e.tensor_copy(block_expert[:], blkf[0:1, 1, :]))
            step(lambda e: e.tensor_scalar(pick[:, 0:NBLK], blkf[:, 1, :], row_expert[:], None, ALU.is_equal))
            slot_te = slot_e[:].rearrange("p e t -> p t e")
            for k in range(TOP):
                step(lambda e, k=k: e.scalar_tensor_tensor(out=tmp[:], in0=rank[:], scalar=float(k + 1), in1=pr[:],
                                                           op0=ALU.is_equal, op1=ALU.mult))
                step(lambda e, k=k: e.tensor_reduce(gates[:, :, k], tmp[:], AX_X, ALU.add))
                step(lambda e, k=k: e.scalar_tensor_tensor(out=tmp[:], in0=rank[:], scalar=float(k + 1), in1=slot_te,
                                                           op0=ALU.is_equal, op1=ALU.mult))
                step(lambda e, k=k: e.tensor_reduce(slot[:, k, :], tmp[:], AX_X, ALU.add))
            step(lambda e: e.tensor_copy(slot_i[:], slot[:]))
            step(lambda e: e.tensor_scalar(row[:], slot_i[:], P - 1, None, ALU.bitwise_and))
            step(lambda e: e.tensor_scalar(col[:], slot_i[:], 7, None, ALU.arith_shift_right))
            step(lambda e: e.tensor_copy(rowf[:], row[:]))
            step(lambda e: e.tensor_copy(colf[:], col[:]))
            out_b = bank[1]
            used = [None, None]
            dve.wait(last[0])
            pairs = [(k, t) for k in range(TOP) for t in range(NT)]
            for s0 in range(0, len(pairs), LT):
                b = s0 // LT % 2
                k, t0 = pairs[s0]
                dve.wait(used[b])
                mr = dve.do(lambda e, k=k, t0=t0, b=b: e.tensor_tensor(
                    in_row[b][:], rowf[:, k, t0:t0 + LT].rearrange("p (t o) -> p t o", o=1).broadcast_to([P, LT, P]),
                    iota[:].rearrange("p (o r) -> p o r", o=1).broadcast_to([P, LT, P]), ALU.is_equal),
                    sem(n + "in_row"))
                for j in range(LT):
                    mc = dve.do(lambda e, k=k, t=t0 + j, j=j, b=b: e.tensor_scalar(
                        in_col[b][:, j, :], iota[:, 0:NSC], colf[:, k, t:t + 1], value[:, k, t:t + 1],
                        ALU.is_equal, ALU.mult), sem(n + "in_col"))
                pe.wait(mr, mc)
                for j in range(LT):
                    m = pe.do(lambda e, j=j, b=b, s0=s0: e.matmul(
                        out_b[:, 0:NSC], in_row[b][:, j, :], in_col[b][:, j, :], start=(s0 + j == 0),
                        stop=(s0 + j == TOP * NT - 1)), sem(n + "list_p"))
                used[b] = m
            step(lambda e: e.tensor_scalar(scatter_id[:], out_b[:, 0:NSC], float(TOP * TOK), None, ALU.add), m)
            step(lambda e: e.tensor_scalar(gather_id[:], scatter_id[:], TOK - 1, None, ALU.bitwise_and))

        stored = []
        out_v = out.rearrange("b (t p) d -> p (b t) d", p=P)

        xr = attention(0, A["L0_xattn_Wq"], A["L0_xattn_Wk"], A["L0_xattn_Wv"], A["L0_xattn_Wo"], A["L0_xattn_bq"],
                       A["L0_xattn_bk"], A["L0_xattn_bv"], A["L0_xattn_bo"], load_x)
        added = []

        def load_x_back(g):
            ts = slice(g * GT, (g + 1) * GT)
            sp.wait(*added)
            return [sp.do(lambda e: e.dma_start(x_sb[:, ts, :], rows(acc_d)[:, ts, :]), sem(f"x_io{g}"), 16)]

        experts_swiglu(xr)
        xr = attention(1, A["L1_WqT"], A["L1_WkT"], A["L1_WvT"], A["L1_WoT"], None, None, None, None,
                       load_x_back)
        experts_relu(xr)
        sp.wait(*stored)

        block = ctx.enter_context(nc.Block())

        @block.sync
        def _(eng):
            sp.play(eng)

        @block.gpsimd
        def _(eng):
            pool.play(eng)

        @block.scalar
        def _(eng):
            act.play(eng)

        @block.vector
        def _(eng):
            dve.play(eng)

        @block.tensor
        def _(eng):
            pe.play(eng)


_DIRECT = ["x", "ctx_512", "L0_xattn_Wq", "L0_xattn_bq", "L0_xattn_Wk", "L0_xattn_bk", "L0_xattn_Wv", "L0_xattn_bv",
           "L0_xattn_Wo", "L0_xattn_bo", "L0_ffn_wg", "L0_ffn_w1", "L0_ffn_w3", "L0_ffn_w2", "L1_ffn_router_W",
           "L1_ffn_router_b", "L1_ffn_sW1", "L1_ffn_sb1", "L1_ffn_sW2", "L1_ffn_sb2", "L1_ffn_eW1", "L1_ffn_eW2",
           "L1_ffn_eb1", "L1_ffn_eb2"]


def kernel(**inputs):
    import numpy as np
    import concourse.bacc as bacc
    from concourse.bass_utils import run_bass_kernel_spmd

    laid = {name: np.asarray(inputs[name]) for name in _DIRECT}
    laid["L1_WqT"] = np.asarray(inputs["L1_xattn_Wq"]).T
    laid["L1_WkT"] = np.asarray(inputs["L1_xattn_Wkv"])[:D].T
    laid["L1_WvT"] = np.asarray(inputs["L1_xattn_Wkv"])[D:].T
    laid["L1_WoT"] = np.asarray(inputs["L1_xattn_Wo"]).T

    for name in ("L0_xattn_bq", "L0_xattn_bk", "L1_ffn_sb1"):
        laid[name] = np.asarray(inputs[name]).reshape(-1, P).T

    nc = bacc.Bacc("TRN2", target_bir_lowering=False, num_devices=1)
    arrays, aps = {}, {}
    for name, a in laid.items():
        arrays[f"in_{name}"] = np.ascontiguousarray(a)
        aps[name] = nc.dram_tensor(f"in_{name}", a.shape, mybir.dt.from_np(a.dtype), kind="ExternalInput").ap()
    out = nc.dram_tensor("out_x", (BATCH, SEQ, D), F32, kind="ExternalOutput").ap()
    build(nc, aps, out)
    r = run_bass_kernel_spmd(nc, [arrays], core_ids=[0])
    return r.results[0]["out_x"]
```
